# Optimizing a Trainium2 kernel written in Bass

```python
import numpy as np
import jax
import jax.numpy as jnp

def _softmax(x, axis=-1):
    return jax.nn.softmax(x, axis=axis)

def _gelu(x):
    return jax.nn.gelu(x, approximate=True)

def _silu(x):
    return jax.nn.silu(x)

def _sigmoid(x):
    return jax.nn.sigmoid(x)

def _layernorm(x, axis=-1, eps=1e-05):
    m = jnp.mean(x, axis=axis, keepdims=True)
    v = jnp.var(x, axis=axis, keepdims=True)
    return (x - m) / jnp.sqrt(v + eps)

def _scatter_add(tgt, idx, src, axis=0):
    return tgt.at[idx].add(src)

def _segment_sum(src, seg, n):
    return jax.ops.segment_sum(src, seg, n)
kernel_name = 'mk_gnn_ffn_d4_gnn_r8_9f68f3'

def setup_inputs(seed: int=0):
    np.random.seed(seed)
    _w = jnp.asarray

    def _rec_inputs():
        import jax
        import jax.numpy as jnp
        _gk = jax.random.key(seed)
        x = -8.776e-05 + 1 * jax.random.normal(jax.random.fold_in(_gk, 1), (2500, 256), jnp.float32)
        src = jax.random.randint(jax.random.fold_in(_gk, 2), (80000,), 0, 2500, jnp.int32)
        dst = jnp.minimum((2500 * jax.random.uniform(jax.random.fold_in(_gk, 3), (80000,)) ** 2.0).astype(jnp.int32), 19999)
        _o = jnp.argsort(dst, stable=True)
        src = src[_o]
        dst = dst[_o]
        return (x, src, dst)
    x, src, dst = _rec_inputs()

    def _L0_gnn_setup():
        import jax, jax.numpy as jnp
        import numpy as np
        N_NODES = 2500
        key = jax.random.key(seed)
        k1, k2, k3, k4 = jax.random.split(key, 4)
        d = 256
        E = 40000
        x = jax.random.normal(k1, (N_NODES, d), dtype=jnp.float32)
        edge_index = jax.random.randint(k2, (2, E), 0, N_NODES, dtype=jnp.int64)
        limit = float(np.sqrt(6.0 / (d + d)))
        W_l = jax.random.uniform(k3, (d, d), dtype=jnp.float32, minval=-limit, maxval=limit)
        W_r = jax.random.uniform(k4, (d, d), dtype=jnp.float32, minval=-limit, maxval=limit)
        b_r = jnp.zeros((d,), dtype=jnp.float32)
        return {'x': x, 'edge_index': edge_index, 'W_l': W_l, 'W_r': W_r, 'b_r': b_r}
    _L0_gnn_all = _L0_gnn_setup()
    _L0_gnn_in = {k: v for k, v in _L0_gnn_all.items() if k in ('W_l', 'W_r', 'b_r')}
    del _L0_gnn_all

    def _L0_ffn_setup():
        import math
        import jax, jax.numpy as jnp
        import numpy as np
        CAPACITY_FACTOR = 1.25
        TOP_K = 2
        LN_EPS = 1e-05

        def _layer_norm(x, gamma, beta):
            mu = jnp.mean(x, axis=-1, keepdims=True)
            var = jnp.var(x, axis=-1, keepdims=True)
            return (x - mu) * jax.lax.rsqrt(var + LN_EPS) * gamma + beta
        key = jax.random.key(seed)
        ks = jax.random.split(key, 4)
        B, S, D, F, E = (8, 512, 256, 512, 8)
        x = jax.random.normal(ks[0], (B, S, D), dtype=jnp.float32)
        Wr = jax.random.normal(ks[1], (D, E), dtype=jnp.float32) / np.sqrt(D)
        br = jnp.zeros((E,), jnp.float32)
        W1 = jax.random.normal(ks[2], (E, D, F), dtype=jnp.float32) / np.sqrt(D)
        b1 = jnp.zeros((E, F), jnp.float32)
        W2 = jax.random.normal(ks[3], (E, F, D), dtype=jnp.float32) / np.sqrt(F)
        b2 = jnp.zeros((E, D), jnp.float32)
        gamma = jnp.ones((D,), jnp.float32)
        beta = jnp.zeros((D,), jnp.float32)
        return {'x': x, 'Wr': Wr, 'br': br, 'W1': W1, 'b1': b1, 'W2': W2, 'b2': b2, 'gamma': gamma, 'beta': beta}
    _L0_ffn_all = _L0_ffn_setup()
    _L0_ffn_in = {k: v for k, v in _L0_ffn_all.items() if k in ('Wr', 'br', 'W1', 'b1', 'W2', 'b2', 'gamma', 'beta')}
    del _L0_ffn_all

    def _L1_gnn_setup():
        import jax, jax.numpy as jnp
        import numpy as np
        N_NODES = 6250
        N_EDGES = 312500
        WIDTH = 256
        LN_EPS = 1e-05

        def gcn_conv(x, edge_index, W, b):
            n = x.shape[0]
            loops = jnp.arange(n, dtype=edge_index.dtype)
            src = jnp.concatenate([edge_index[0], loops])
            dst = jnp.concatenate([edge_index[1], loops])
            deg = jax.ops.segment_sum(jnp.ones_like(dst, dtype=x.dtype), dst, num_segments=n)
            dinv = jnp.where(deg > 0, jax.lax.rsqrt(deg), 0.0)
            norm = dinv[src] * dinv[dst]
            h = x @ W.T
            msgs = norm[:, None] * h[src]
            out = jax.ops.segment_sum(msgs, dst, num_segments=n)
            return out + b

        def layer_norm(x, gamma, beta):
            mu = jnp.mean(x, axis=-1, keepdims=True)
            var = jnp.mean(jnp.square(x - mu), axis=-1, keepdims=True)
            return (x - mu) * jax.lax.rsqrt(var + LN_EPS) * gamma + beta
        key = jax.random.key(seed)
        k1, k2, k3, k4 = jax.random.split(key, 4)
        x = jax.random.normal(k1, (N_NODES, WIDTH), dtype=jnp.float32)
        edge_index = jax.random.randint(k2, (2, N_EDGES), 0, N_NODES, dtype=jnp.int64)
        W = jax.random.normal(k3, (WIDTH, WIDTH), dtype=jnp.float32) / np.sqrt(WIDTH)
        b = jax.random.normal(k4, (WIDTH,), dtype=jnp.float32) * 0.01
        gamma = jnp.ones((WIDTH,), dtype=jnp.float32)
        beta = jnp.zeros((WIDTH,), dtype=jnp.float32)
        return {'x': x, 'edge_index': edge_index, 'W': W, 'b': b, 'gamma': gamma, 'beta': beta}
    _L1_gnn_all = _L1_gnn_setup()
    _L1_gnn_in = {k: v for k, v in _L1_gnn_all.items() if k in ('W', 'b', 'gamma', 'beta')}
    del _L1_gnn_all

    def _L1_ffn_setup():
        import jax, jax.numpy as jnp
        import numpy as np
        E, D, H, TOP_K = (6, 256, 256, 2)
        ROUTER_H = D // 2
        key = jax.random.key(seed)
        ks = jax.random.split(key, 12)
        s = 1.0 / np.sqrt(D)
        sh = 1.0 / np.sqrt(H)
        sr = 1.0 / np.sqrt(ROUTER_H)
        return {'features': jax.random.normal(ks[0], (8, 512, D), dtype=jnp.float32), 'router_w1': jax.random.uniform(ks[1], (D, ROUTER_H), jnp.float32, -s, s), 'router_b1': jnp.zeros((ROUTER_H,), jnp.float32), 'router_w2': jax.random.uniform(ks[2], (ROUTER_H, E), jnp.float32, -sr, sr), 'router_b2': jnp.zeros((E,), jnp.float32), 'expert_w1': jax.random.uniform(ks[3], (E, D, H), jnp.float32, -s, s), 'expert_b1': jnp.zeros((E, H), jnp.float32), 'expert_w2': jax.random.uniform(ks[4], (E, H, H), jnp.float32, -sh, sh), 'expert_b2': jnp.zeros((E, H), jnp.float32), 'expert_w3': jax.random.uniform(ks[5], (E, H, D), jnp.float32, -sh, sh), 'expert_b3': jnp.zeros((E, D), jnp.float32)}
    _L1_ffn_all = _L1_ffn_setup()
    _L1_ffn_in = {k: v for k, v in _L1_ffn_all.items() if k in ('router_w1', 'router_b1', 'router_w2', 'router_b2', 'expert_w1', 'expert_b1', 'expert_w2', 'expert_b2', 'expert_w3', 'expert_b3')}
    del _L1_ffn_all

    def _L2_gnn_setup():
        import jax, jax.numpy as jnp
        import numpy as np
        N_NODES = 6250
        N_EDGES = 200000
        IN_DIM, HID_DIM, OUT_DIM = (256, 1024, 256)
        key = jax.random.key(seed)
        k1, k2, k3, k4, k5, k6 = jax.random.split(key, 6)
        x = jax.random.normal(k1, (N_NODES, IN_DIM), dtype=jnp.float32)
        edge_index = jax.random.randint(k2, (2, N_EDGES), 0, N_NODES, dtype=jnp.int64)
        W1 = jax.random.normal(k3, (IN_DIM, HID_DIM), dtype=jnp.float32) / np.sqrt(IN_DIM)
        b1 = jax.random.normal(k4, (HID_DIM,), dtype=jnp.float32) * 0.01
        W2 = jax.random.normal(k5, (HID_DIM, OUT_DIM), dtype=jnp.float32) / np.sqrt(HID_DIM)
        b2 = jax.random.normal(k6, (OUT_DIM,), dtype=jnp.float32) * 0.01
        return {'x': x, 'edge_index': edge_index, 'W1': W1, 'b1': b1, 'W2': W2, 'b2': b2}
    _L2_gnn_all = _L2_gnn_setup()
    _L2_gnn_in = {k: v for k, v in _L2_gnn_all.items() if k in ('W1', 'b1', 'W2', 'b2')}
    del _L2_gnn_all

    def _L2_ffn_setup():
        import jax, jax.numpy as jnp
        import numpy as np
        E = 8
        K = 2
        D = 256
        H = 512
        DOUT = 256
        EPS = 1e-05
        key = jax.random.key(seed)
        ks = jax.random.split(key, 9)
        s = 0.02
        return {'x': jax.random.normal(ks[0], (4, 1024, D), jnp.float32), 'gamma': 1.0 + 0.05 * jax.random.normal(ks[1], (D,), jnp.float32), 'beta': 0.05 * jax.random.normal(ks[2], (D,), jnp.float32), 'Wr': 0.01 * jax.random.normal(ks[3], (D, E), jnp.float32), 'br': jnp.zeros((E,), jnp.float32), 'W1': s * jax.random.normal(ks[4], (E, D, H), jnp.float32), 'b1': s * jax.random.normal(ks[5], (E, H), jnp.float32), 'W2': s * jax.random.normal(ks[6], (E, H, DOUT), jnp.float32), 'b2': s * jax.random.normal(ks[7], (E, DOUT), jnp.float32)}
    _L2_ffn_all = _L2_ffn_setup()
    _L2_ffn_in = {k: v for k, v in _L2_ffn_all.items() if k in ('gamma', 'beta', 'Wr', 'br', 'W1', 'b1', 'W2', 'b2')}
    del _L2_ffn_all

    def _L3_gnn_setup():
        import jax, jax.numpy as jnp
        import numpy as np
        N_NODES = 6250
        N_EDGES = 200000
        IN_DIM, OUT_DIM, N_HEADS = (256, 64, 4)
        EPS = 1e-12
        key = jax.random.key(seed)
        k1, k2, k3, k4, k5 = jax.random.split(key, 5)
        h = jax.random.normal(k1, (N_NODES, IN_DIM), dtype=jnp.float32)
        edge_index = jax.random.randint(k2, (2, N_EDGES), 0, N_NODES, dtype=jnp.int32)
        W = jax.random.normal(k3, (IN_DIM, OUT_DIM), dtype=jnp.float32) * 0.05
        Wl = jax.random.normal(k4, (N_HEADS, OUT_DIM), dtype=jnp.float32) * 0.05
        Wr = jax.random.normal(k5, (N_HEADS, OUT_DIM), dtype=jnp.float32) * 0.05
        b = jnp.zeros((OUT_DIM,), dtype=jnp.float32)
        return {'h': h, 'W': W, 'Wl': Wl, 'Wr': Wr, 'b': b, 'edge_index': edge_index}
    _L3_gnn_all = _L3_gnn_setup()
    _L3_gnn_in = {k: v for k, v in _L3_gnn_all.items() if k in ('W', 'Wl', 'Wr', 'b')}
    del _L3_gnn_all

    def _L3_ffn_setup():
        import jax, jax.numpy as jnp
        import numpy as np
        BN_EPS = 0.001

        def _bn(h, g, b, m, v):
            return g * (h - m) * jax.lax.rsqrt(v + BN_EPS) + b
        key = jax.random.key(seed)
        ks = jax.random.split(key, 8)
        B, F, Df = (256, 64, 256)
        E, H, D = (8, 256, 256)
        s1 = 1.0 / np.sqrt(Df)
        s2 = 1.0 / np.sqrt(H)
        return {'x': jax.random.normal(ks[0], (B, F, Df), jnp.float32), 'Wr': jax.random.normal(ks[1], (Df, E), jnp.float32) * s1, 'br': jnp.zeros((E,), jnp.float32), 'W1': jax.random.normal(ks[2], (E, Df, H), jnp.float32) * s1, 'b1': jnp.zeros((E, H), jnp.float32), 'g1': jnp.ones((E, H), jnp.float32), 'be1': jnp.zeros((E, H), jnp.float32), 'm1': jnp.zeros((E, H), jnp.float32), 'v1': jnp.ones((E, H), jnp.float32), 'W2': jax.random.normal(ks[3], (E, H, H), jnp.float32) * s2, 'b2': jnp.zeros((E, H), jnp.float32), 'g2': jnp.ones((E, H), jnp.float32), 'be2': jnp.zeros((E, H), jnp.float32), 'm2': jnp.zeros((E, H), jnp.float32), 'v2': jnp.ones((E, H), jnp.float32), 'Wo': jax.random.normal(ks[4], (E, H, D), jnp.float32) * s2, 'bo': jnp.zeros((E, D), jnp.float32)}
    _L3_ffn_all = _L3_ffn_setup()
    _L3_ffn_in = {k: v for k, v in _L3_ffn_all.items() if k in ('Wr', 'br', 'W1', 'b1', 'g1', 'be1', 'm1', 'v1', 'W2', 'b2', 'g2', 'be2', 'm2', 'v2', 'Wo', 'bo')}
    del _L3_ffn_all
    return {'x': x, 'src': src, 'dst': dst, 'L0_gnn_W_l': _L0_gnn_in['W_l'], 'L0_gnn_W_r': _L0_gnn_in['W_r'], 'L0_gnn_b_r': _L0_gnn_in['b_r'], 'L0_ffn_Wr': _L0_ffn_in['Wr'], 'L0_ffn_br': _L0_ffn_in['br'], 'L0_ffn_W1': _L0_ffn_in['W1'], 'L0_ffn_b1': _L0_ffn_in['b1'], 'L0_ffn_W2': _L0_ffn_in['W2'], 'L0_ffn_b2': _L0_ffn_in['b2'], 'L0_ffn_gamma': _L0_ffn_in['gamma'], 'L0_ffn_beta': _L0_ffn_in['beta'], 'L1_gnn_W': _L1_gnn_in['W'], 'L1_gnn_b': _L1_gnn_in['b'], 'L1_gnn_gamma': _L1_gnn_in['gamma'], 'L1_gnn_beta': _L1_gnn_in['beta'], 'L1_ffn_router_w1': _L1_ffn_in['router_w1'], 'L1_ffn_router_b1': _L1_ffn_in['router_b1'], 'L1_ffn_router_w2': _L1_ffn_in['router_w2'], 'L1_ffn_router_b2': _L1_ffn_in['router_b2'], 'L1_ffn_expert_w1': _L1_ffn_in['expert_w1'], 'L1_ffn_expert_b1': _L1_ffn_in['expert_b1'], 'L1_ffn_expert_w2': _L1_ffn_in['expert_w2'], 'L1_ffn_expert_b2': _L1_ffn_in['expert_b2'], 'L1_ffn_expert_w3': _L1_ffn_in['expert_w3'], 'L1_ffn_expert_b3': _L1_ffn_in['expert_b3'], 'L2_gnn_W1': _L2_gnn_in['W1'], 'L2_gnn_b1': _L2_gnn_in['b1'], 'L2_gnn_W2': _L2_gnn_in['W2'], 'L2_gnn_b2': _L2_gnn_in['b2'], 'L2_ffn_gamma': _L2_ffn_in['gamma'], 'L2_ffn_beta': _L2_ffn_in['beta'], 'L2_ffn_Wr': _L2_ffn_in['Wr'], 'L2_ffn_br': _L2_ffn_in['br'], 'L2_ffn_W1': _L2_ffn_in['W1'], 'L2_ffn_b1': _L2_ffn_in['b1'], 'L2_ffn_W2': _L2_ffn_in['W2'], 'L2_ffn_b2': _L2_ffn_in['b2'], 'L3_gnn_W': _L3_gnn_in['W'], 'L3_gnn_Wl': _L3_gnn_in['Wl'], 'L3_gnn_Wr': _L3_gnn_in['Wr'], 'L3_gnn_b': _L3_gnn_in['b'], 'L3_ffn_Wr': _L3_ffn_in['Wr'], 'L3_ffn_br': _L3_ffn_in['br'], 'L3_ffn_W1': _L3_ffn_in['W1'], 'L3_ffn_b1': _L3_ffn_in['b1'], 'L3_ffn_g1': _L3_ffn_in['g1'], 'L3_ffn_be1': _L3_ffn_in['be1'], 'L3_ffn_m1': _L3_ffn_in['m1'], 'L3_ffn_v1': _L3_ffn_in['v1'], 'L3_ffn_W2': _L3_ffn_in['W2'], 'L3_ffn_b2': _L3_ffn_in['b2'], 'L3_ffn_g2': _L3_ffn_in['g2'], 'L3_ffn_be2': _L3_ffn_in['be2'], 'L3_ffn_m2': _L3_ffn_in['m2'], 'L3_ffn_v2': _L3_ffn_in['v2'], 'L3_ffn_Wo': _L3_ffn_in['Wo'], 'L3_ffn_bo': _L3_ffn_in['bo']}

def reference(x, src, dst, L0_gnn_W_l, L0_gnn_W_r, L0_gnn_b_r, L0_ffn_Wr, L0_ffn_br, L0_ffn_W1, L0_ffn_b1, L0_ffn_W2, L0_ffn_b2, L0_ffn_gamma, L0_ffn_beta, L1_gnn_W, L1_gnn_b, L1_gnn_gamma, L1_gnn_beta, L1_ffn_router_w1, L1_ffn_router_b1, L1_ffn_router_w2, L1_ffn_router_b2, L1_ffn_expert_w1, L1_ffn_expert_b1, L1_ffn_expert_w2, L1_ffn_expert_b2, L1_ffn_expert_w3, L1_ffn_expert_b3, L2_gnn_W1, L2_gnn_b1, L2_gnn_W2, L2_gnn_b2, L2_ffn_gamma, L2_ffn_beta, L2_ffn_Wr, L2_ffn_br, L2_ffn_W1, L2_ffn_b1, L2_ffn_W2, L2_ffn_b2, L3_gnn_W, L3_gnn_Wl, L3_gnn_Wr, L3_gnn_b, L3_ffn_Wr, L3_ffn_br, L3_ffn_W1, L3_ffn_b1, L3_ffn_g1, L3_ffn_be1, L3_ffn_m1, L3_ffn_v1, L3_ffn_W2, L3_ffn_b2, L3_ffn_g2, L3_ffn_be2, L3_ffn_m2, L3_ffn_v2, L3_ffn_Wo, L3_ffn_bo):
    import jax
    import jax.numpy as jnp

    def _L0_gnn_ref(x, edge_index, W_l, W_r, b_r):
        import jax, jax.numpy as jnp
        import numpy as np
        N_NODES = 2500
        src, dst = (edge_index[0], edge_index[1])
        messages = x[src]
        sums = jax.ops.segment_sum(messages, dst, num_segments=N_NODES)
        counts = jax.ops.segment_sum(jnp.ones_like(dst, dtype=x.dtype), dst, num_segments=N_NODES)
        aggr = sums / jnp.maximum(counts, 1.0)[:, None]
        out = aggr @ W_l.T + x @ W_r.T + b_r
        return out

    def _L0_ffn_ref(x, Wr, br, W1, b1, W2, b2, gamma, beta):
        import math
        import jax, jax.numpy as jnp
        import numpy as np
        CAPACITY_FACTOR = 1.25
        TOP_K = 2
        LN_EPS = 1e-05

        def _layer_norm(x, gamma, beta):
            mu = jnp.mean(x, axis=-1, keepdims=True)
            var = jnp.var(x, axis=-1, keepdims=True)
            return (x - mu) * jax.lax.rsqrt(var + LN_EPS) * gamma + beta
        B, S, D = x.shape
        E = Wr.shape[1]
        N = B * S
        K = TOP_K
        logits = jnp.mean(x, axis=1) @ Wr + br
        routing_weights = jax.nn.softmax(logits, axis=-1)
        capacity = float(math.ceil(N * CAPACITY_FACTOR / E))
        expected_loads = routing_weights.sum(axis=0) * (N / B)
        scale = jnp.where(expected_loads > capacity, capacity / expected_loads, 1.0)
        routing_weights = jax.nn.softmax(routing_weights * scale, axis=-1)
        rw_tok = jnp.broadcast_to(routing_weights[:, None, :], (B, S, E)).reshape(N, E)
        top_w, top_i = jax.lax.top_k(rw_tok, K)
        top_w = jax.nn.softmax(top_w, axis=-1)
        xf = x.reshape(N, D)
        h = jax.nn.gelu(jnp.einsum('nd,edf->enf', xf, W1) + b1[:, None, :], approximate=False)
        y = jnp.einsum('enf,efd->end', h, W2) + b2[:, None, :]
        w_dense = jnp.zeros((N, E), x.dtype).at[jnp.arange(N)[:, None], top_i].add(top_w)
        out = jnp.einsum('ne,end->nd', w_dense, y).reshape(B, S, D)
        out = _layer_norm(out + x, gamma, beta)
        return out

    def _L1_gnn_ref(x, edge_index, W, b, gamma, beta):
        import jax, jax.numpy as jnp
        import numpy as np
        N_NODES = 6250
        N_EDGES = 312500
        WIDTH = 256
        LN_EPS = 1e-05

        def gcn_conv(x, edge_index, W, b):
            n = x.shape[0]
            loops = jnp.arange(n, dtype=edge_index.dtype)
            src = jnp.concatenate([edge_index[0], loops])
            dst = jnp.concatenate([edge_index[1], loops])
            deg = jax.ops.segment_sum(jnp.ones_like(dst, dtype=x.dtype), dst, num_segments=n)
            dinv = jnp.where(deg > 0, jax.lax.rsqrt(deg), 0.0)
            norm = dinv[src] * dinv[dst]
            h = x @ W.T
            msgs = norm[:, None] * h[src]
            out = jax.ops.segment_sum(msgs, dst, num_segments=n)
            return out + b

        def layer_norm(x, gamma, beta):
            mu = jnp.mean(x, axis=-1, keepdims=True)
            var = jnp.mean(jnp.square(x - mu), axis=-1, keepdims=True)
            return (x - mu) * jax.lax.rsqrt(var + LN_EPS) * gamma + beta
        h = gcn_conv(x, edge_index, W, b)
        h = layer_norm(h, gamma, beta)
        h = jax.nn.relu(h)
        return h

    def _L1_ffn_ref(features, router_w1, router_b1, router_w2, router_b2, expert_w1, expert_b1, expert_w2, expert_b2, expert_w3, expert_b3):
        import jax, jax.numpy as jnp
        import numpy as np
        E, D, H, TOP_K = (6, 256, 256, 2)
        ROUTER_H = D // 2
        rh = jax.nn.relu(features @ router_w1 + router_b1)
        expert_logits = jax.nn.softmax(rh @ router_w2 + router_b2, axis=-1)
        top_w, top_i = jax.lax.top_k(expert_logits, TOP_K)
        routing_weights = jax.nn.softmax(top_w, axis=-1)
        h1 = jax.nn.relu(jnp.einsum('bsd,edh->bseh', features, expert_w1) + expert_b1)
        h2 = jax.nn.relu(jnp.einsum('bseh,ehf->bsef', h1, expert_w2) + expert_b2)
        expert_out = jnp.einsum('bsef,efo->bseo', h2, expert_w3) + expert_b3
        sel = jnp.take_along_axis(expert_out, top_i[:, :, :, None], axis=2)
        combined = jnp.sum(sel * routing_weights[..., None], axis=2)
        return combined

    def _L2_gnn_ref(x, edge_index, W1, b1, W2, b2):
        import jax, jax.numpy as jnp
        import numpy as np
        N_NODES = 6250
        N_EDGES = 200000
        IN_DIM, HID_DIM, OUT_DIM = (256, 1024, 256)
        num_nodes = x.shape[0]
        src, dst = (edge_index[0], edge_index[1])
        deg = jax.ops.segment_sum(jnp.ones_like(dst, dtype=x.dtype), dst, num_segments=num_nodes)
        dinv = jnp.where(deg > 0, jax.lax.rsqrt(jnp.maximum(deg, 1e-12)), 0.0)
        edge_weight = dinv[src] * dinv[dst]
        msg = edge_weight[:, None] * x[src]
        agg = jax.ops.segment_sum(msg, dst, num_segments=num_nodes)
        h = jax.nn.gelu(agg @ W1 + b1, approximate=False)
        out = h @ W2 + b2
        return out

    def _L2_ffn_ref(x, gamma, beta, Wr, br, W1, b1, W2, b2):
        import jax, jax.numpy as jnp
        import numpy as np
        E = 8
        K = 2
        D = 256
        H = 512
        DOUT = 256
        EPS = 1e-05
        mu = jnp.mean(x, axis=-1, keepdims=True)
        var = jnp.mean(jnp.square(x - mu), axis=-1, keepdims=True)
        xn = (x - mu) * jax.lax.rsqrt(var + EPS) * gamma + beta
        logits = jnp.einsum('bsd,de->bse', xn, Wr) + br
        top_vals, top_idx = jax.lax.top_k(logits, K)
        w = jax.nn.softmax(top_vals, axis=-1)
        w_full = jnp.einsum('bsk,bske->bse', w, jax.nn.one_hot(top_idx, E, dtype=w.dtype))
        y = jnp.zeros(x.shape[:-1] + (DOUT,), x.dtype)
        for e in range(E):
            h = jax.nn.gelu(jnp.einsum('bsd,dh->bsh', xn, W1[e]) + b1[e], approximate=False)
            y_e = jnp.einsum('bsh,hd->bsd', h, W2[e]) + b2[e]
            y = y + y_e * w_full[..., e, None]
        return y

    def _L3_gnn_ref(h, W, Wl, Wr, b, edge_index):
        import jax, jax.numpy as jnp
        import numpy as np
        N_NODES = 6250
        N_EDGES = 200000
        IN_DIM, OUT_DIM, N_HEADS = (256, 64, 4)
        EPS = 1e-12
        N = h.shape[0]
        H = Wl.shape[0]
        x = h @ W
        el = x @ Wl.T
        er = x @ Wr.T
        src, dst = (edge_index[0], edge_index[1])
        e = el[src] + er[dst]
        e = jnp.exp(jax.nn.leaky_relu(e, negative_slope=0.2))
        rowsum = jax.ops.segment_sum(e, src, num_segments=N)
        w = e / jnp.maximum(rowsum, EPS)[src]
        heads = [jax.ops.segment_sum(w[:, hd:hd + 1] * x[dst], src, num_segments=N) for hd in range(H)]
        out = jnp.stack(heads, axis=1)
        out = jax.nn.elu(out + b)
        return out.reshape(N, H * x.shape[1])

    def _L3_ffn_ref(x, Wr, br, W1, b1, g1, be1, m1, v1, W2, b2, g2, be2, m2, v2, Wo, bo):
        import jax, jax.numpy as jnp
        import numpy as np
        BN_EPS = 0.001

        def _bn(h, g, b, m, v):
            return g * (h - m) * jax.lax.rsqrt(v + BN_EPS) + b
        feat = jnp.mean(x, axis=0)
        w = jax.nn.softmax(feat @ Wr + br, axis=-1)
        h = jnp.einsum('bfd,edh->bfeh', x, W1) + b1
        h = jax.nn.relu(_bn(h, g1, be1, m1, v1))
        h = jnp.einsum('bfeh,ehk->bfek', h, W2) + b2
        h = jax.nn.relu(_bn(h, g2, be2, m2, v2))
        y = jnp.einsum('bfeh,ehd->bfed', h, Wo) + bo
        return jnp.einsum('bfed,fe->bfd', y, w)
    edge_index = jnp.stack([src, dst])
    x = x + _L0_gnn_ref(_layernorm(x, axis=-1), edge_index, L0_gnn_W_l, L0_gnn_W_r, L0_gnn_b_r)
    x = x + _L0_ffn_ref(_layernorm(x, axis=-1)[None], L0_ffn_Wr, L0_ffn_br, L0_ffn_W1, L0_ffn_b1, L0_ffn_W2, L0_ffn_b2, L0_ffn_gamma, L0_ffn_beta)[0]
    x = x + _L1_gnn_ref(_layernorm(x, axis=-1), edge_index, L1_gnn_W, L1_gnn_b, L1_gnn_gamma, L1_gnn_beta)
    x = x + _L1_ffn_ref(_layernorm(x, axis=-1)[None], L1_ffn_router_w1, L1_ffn_router_b1, L1_ffn_router_w2, L1_ffn_router_b2, L1_ffn_expert_w1, L1_ffn_expert_b1, L1_ffn_expert_w2, L1_ffn_expert_b2, L1_ffn_expert_w3, L1_ffn_expert_b3)[0]
    x = x + _L2_gnn_ref(_layernorm(x, axis=-1), edge_index, L2_gnn_W1, L2_gnn_b1, L2_gnn_W2, L2_gnn_b2)
    x = x + _L2_ffn_ref(_layernorm(x, axis=-1)[None], L2_ffn_gamma, L2_ffn_beta, L2_ffn_Wr, L2_ffn_br, L2_ffn_W1, L2_ffn_b1, L2_ffn_W2, L2_ffn_b2)[0]
    x = x + _L3_gnn_ref(_layernorm(x, axis=-1), L3_gnn_W, L3_gnn_Wl, L3_gnn_Wr, L3_gnn_b, edge_index)
    x = x + _L3_ffn_ref(_layernorm(x, axis=-1)[None], L3_ffn_Wr, L3_ffn_br, L3_ffn_W1, L3_ffn_b1, L3_ffn_g1, L3_ffn_be1, L3_ffn_m1, L3_ffn_v1, L3_ffn_W2, L3_ffn_b2, L3_ffn_g2, L3_ffn_be2, L3_ffn_m2, L3_ffn_v2, L3_ffn_Wo, L3_ffn_bo)[0]
    return x

_drawn_inputs = setup_inputs


def setup_inputs(seed=0):
    import zlib

    import numpy as np

    out = dict(_drawn_inputs(seed))
    spreads = {'L0_gnn_b_r': (0.0, 0.1),
     'L0_ffn_br': (0.0, 0.1),
     'L0_ffn_b1': (0.0, 0.305),
     'L0_ffn_b2': (0.0, 0.1),
     'L0_ffn_gamma': (1.0, 0.2),
     'L0_ffn_beta': (0.0, 0.1),
     'L1_gnn_gamma': (1.0, 0.2),
     'L1_gnn_beta': (0.0, 0.1),
     'L1_ffn_router_b1': (0.0, 0.407),
     'L1_ffn_router_b2': (0.0, 0.473),
     'L1_ffn_expert_b1': (0.0, 0.8),
     'L1_ffn_expert_b2': (0.0, 0.718),
     'L1_ffn_expert_b3': (0.0, 0.279),
     'L2_ffn_br': (0.0, 0.459),
     'L3_gnn_b': (0.0, 0.294),
     'L3_ffn_br': (0.0, 0.8),
     'L3_ffn_b1': (0.0, 0.782),
     'L3_ffn_g1': (1.0, 0.6),
     'L3_ffn_be1': (0.0, 0.8),
     'L3_ffn_m1': (0.0, 0.768),
     'L3_ffn_v1': (1.0, 0.6),
     'L3_ffn_b2': (0.0, 0.574),
     'L3_ffn_g2': (1.0, 0.6),
     'L3_ffn_be2': (0.0, 0.588),
     'L3_ffn_m2': (0.0, 0.553),
     'L3_ffn_v2': (1.0, 0.6),
     'L3_ffn_bo': (0.0, 0.416)}
    factors = {'L1_gnn_b': 4.591,
     'L1_ffn_expert_w1': 2.735,
     'L2_gnn_b1': 8.0,
     'L2_gnn_b2': 8.0,
     'L2_ffn_gamma': 8.0,
     'L2_ffn_beta': 8.0,
     'L2_ffn_Wr': 3.067,
     'L2_ffn_W1': 2.677,
     'L2_ffn_b1': 32.27,
     'L2_ffn_b2': 8.0,
     'L3_gnn_Wl': 22.181,
     'L3_gnn_Wr': 3.736}
    for name, (base, spread) in spreads.items():
        noise = np.random.default_rng([zlib.crc32(name.encode()), seed]).standard_normal(out[name].shape)
        drawn = base * np.exp(spread * noise) if base else spread * noise
        out[name] = jnp.asarray(drawn.astype(out[name].dtype))
    for name, factor in factors.items():
        out[name] = (out[name] * factor).astype(out[name].dtype)
    return out
```

```python
from contextlib import ExitStack

import concourse.bass as bass
from concourse import mybir

F32 = mybir.dt.float32
F16 = mybir.dt.float16
I32 = mybir.dt.int32
ALU = mybir.AluOpType
ACT = mybir.ActivationFunctionType
AX = mybir.AxisListType

P = 128
N = 2500
D = 256
DK = D // P
NT = -(-N // P)
NP = NT * P
BLK = 512
NB = NP // BLK
TB = BLK // P
E = 80000
GC = 5
NG = E // (GC * P)
HALF = NP // 2
FH = 512
EPS = 1e-5
EXP_TOP = 88.7
BIG = 3.0e38
ds = bass.ds


class Steps:

    def __init__(self, eng, sem, base=0):
        self.eng, self.sem, self.n = eng, sem, base

    def step(self, ins):
        ins.then_inc(self.sem, 1)
        self.n = self.n + 1

    def join(self, ins):
        self.step(ins)
        self.eng.wait_ge(self.sem, self.n)


class Mem:
    pass


def rows(ap):
    return ap.rearrange("(k p) n -> p k n", p=P)


def per_partition(ap):
    return ap.rearrange("(k p) -> p k", p=P)



def phase_setup(nc, m, x, src, dst):
    sem = nc.alloc_semaphore
    main_in, tail_in, edges_in = sem("main_in"), sem("tail_in"), sem("edges_in")
    tail_zeroed, made, dve_own = sem("tail_zeroed"), sem("consts_made"), sem("setup_dve")
    turned, turned_rng, turned_row = sem("edges_turned"), sem("range_turned"), sem("range_row")
    full = N // P
    with (
        nc.sbuf_tensor("edge_i", [P, 2, GC * P], I32) as edge_i,
        nc.sbuf_tensor("edge_f", [P, 2, GC * P], F32) as edge_f,
        nc.sbuf_tensor("bounds", [P, 2, NT], F32) as bounds,
        nc.sbuf_tensor("tile_low", [P, 2], F32) as tile_low,
        nc.sbuf_tensor("group_no", [P, 2, NG], F32) as group_no,
        nc.sbuf_tensor("bounds_row", [P, 2, NG], F32) as bounds_row,
        nc.sbuf_tensor("touch", [P, 3, NG], F32) as touch,
        nc.sbuf_tensor("ends", [P, 4], F32) as ends,
        nc.psum_tensor("turn_ps", [P, 4, 4, P], F32) as ps,
        nc.Block() as block,
    ):
        @block.sync
        def _(sp):
            sp.dma_start(edge_i[0:NG, 0, :], src.rearrange("(p e) -> p e", p=NG)).then_inc(edges_in, 16)
            sp.dma_start(edge_i[0:NG, 1, :], dst.rearrange("(p e) -> p e", p=NG)).then_inc(edges_in, 16)
            sp.dma_start(m.x[:, 0:full, :], x[0:full * P, :].rearrange("(t p) d -> p t d", p=P)).then_inc(main_in, 16)
            sp.wait_ge(tail_zeroed, 1)
            sp.dma_start(m.x[0:N - full * P, full, :], x[full * P:N, :]).then_inc(tail_in, 16)
            sp.wait_ge(main_in, 16)
            sp.wait_ge(tail_in, 16)

        @block.gpsimd
        def _(pool):
            own = Steps(pool, made)
            pool.memset(m.x[:, full, :], 0.0).then_inc(tail_zeroed, 1)
            own.step(pool.memset(m.ones[:, :], 1.0))
            own.join(pool.memset(m.ident[:, :], 0.0))
            own.join(pool.affine_select(out=m.ident[:, :], in_=m.ident[:, :], compare_op=ALU.not_equal, fill=1.0,
                                        base=0, pattern=[[-1, P]], channel_multiplier=1))
            own.step(pool.iota(m.src_no[:, :], pattern=[[1, NP]], base=-HALF, channel_multiplier=0,
                               allow_small_or_imprecise_dtypes=True))
            own.step(pool.iota(m.expert_no[:, :, :], pattern=[[0, NT], [1, 8]], base=-8, channel_multiplier=0,
                               allow_small_or_imprecise_dtypes=True))
            own.step(pool.iota(m.part_no[:, :], pattern=[[0, 1]], base=0, channel_multiplier=1,
                               allow_small_or_imprecise_dtypes=True))
            own.step(pool.iota(tile_low[:, 0:1], pattern=[[0, 1]], base=0, channel_multiplier=P,
                               allow_small_or_imprecise_dtypes=True))
            own.step(pool.iota(tile_low[:, 1:2], pattern=[[0, 1]], base=P, channel_multiplier=P,
                               allow_small_or_imprecise_dtypes=True))
            own.step(pool.iota(group_no[:, 0, :], pattern=[[1, NG]], base=-NG, channel_multiplier=0,
                               allow_small_or_imprecise_dtypes=True))
            own.step(pool.iota(group_no[:, 1, :], pattern=[[1, NG]], base=1, channel_multiplier=0,
                               allow_small_or_imprecise_dtypes=True))

        @block.vector
        def _(dve):
            own = Steps(dve, dve_own)
            dve.wait_ge(edges_in, 32)
            dve.memset(m.zeros16[:, :], 0.0)
            own.step(dve.tensor_scalar(edge_f[0:NG, 0, :], edge_i[0:NG, 0, :], -float(HALF), None, ALU.add))
            own.join(dve.tensor_copy(edge_f[0:NG, 1, :], edge_i[0:NG, 1, :]))
            own.step(dve.tensor_reduce(ends[0:NG, 0:1], edge_f[0:NG, 1, :], AX.X, ALU.min))
            own.join(dve.tensor_reduce(ends[0:NG, 1:2], edge_f[0:NG, 1, :], AX.X, ALU.max))
            own.join(dve.tensor_copy(bounds[0:NG, :, :], ends[0:NG, 0:2].unsqueeze(2).to_broadcast([NG, 2, NT])))
            dve.wait_ge(turned, 2 * GC)
            for i, col in enumerate((m.src_col, m.dst_col)):
                for k in range(GC):
                    n = i * GC + k
                    own.step(dve.tensor_copy(col[:, k:k + GC * (NG - 1) + 1:GC], ps[:, n // 4, n % 4, 0:NG]))
            dve.wait_ge(turned_rng, 2)
            dve.wait_ge(made, 10)
            own.join(dve.tensor_copy(bounds_row[0:NT, :, :], ps[0:NT, 3, 0:2, 0:NG]))
            own.step(dve.tensor_scalar(touch[0:NT, 0, :], bounds_row[0:NT, 0, :], tile_low[0:NT, 1:2], None, ALU.is_lt))
            own.join(dve.tensor_scalar(touch[0:NT, 1, :], bounds_row[0:NT, 1, :], tile_low[0:NT, 0:1], None, ALU.is_ge))
            own.join(dve.tensor_tensor(touch[0:NT, 0, :], touch[0:NT, 0, :], touch[0:NT, 1, :], ALU.mult))
            own.step(dve.tensor_tensor(touch[0:NT, 1, :], touch[0:NT, 0, :], group_no[0:NT, 0, :], ALU.mult))
            own.join(dve.tensor_tensor(touch[0:NT, 2, :], touch[0:NT, 0, :], group_no[0:NT, 1, :], ALU.mult))
            own.step(dve.tensor_reduce(ends[0:NT, 0:1], touch[0:NT, 1, :], AX.X, ALU.min))
            own.join(dve.tensor_reduce(ends[0:NT, 1:2], touch[0:NT, 2, :], AX.X, ALU.max))
            own.join(dve.tensor_scalar(ends[0:NT, 2:3], ends[0:NT, 0:1], float(NG), float(NG - 1), ALU.add, ALU.min))
            own.join(dve.tensor_scalar(ends[0:NT, 3:4], ends[0:NT, 2:3], 1.0, ends[0:NT, 1:2], ALU.add, ALU.max))
            dve.wait_ge(turned_row, 2)
            own.join(dve.tensor_copy(m.ranges[0:1, :, :], ps[0:1, 3, 2:4, 0:NT]))

        @block.tensor
        def _(pe):
            pe.wait_ge(made, 3)
            pe.wait_ge(dve_own, 2)
            for i in range(2):
                for k in range(GC):
                    n = i * GC + k
                    pe.transpose(ps[:, n // 4, n % 4, 0:NG], edge_f[0:NG, i, k * P:(k + 1) * P],
                                 m.ident[0:NG, 0:NG]).then_inc(turned, 1)
            pe.wait_ge(dve_own, 5)
            for i in range(2):
                pe.transpose(ps[0:NT, 3, i, 0:NG], bounds[0:NG, i, :], m.ident[0:NG, 0:NG]).then_inc(turned_rng, 1)
            pe.wait_ge(dve_own, 15 + 10)
            for i in range(2):
                pe.transpose(ps[0:1, 3, 2 + i, 0:NT], ends[0:NT, 2 + i:3 + i], m.ident[0:NT, 0:NT]).then_inc(turned_row, 1)



def phase_counts(nc, m):
    sem = nc.alloc_semaphore
    built, slot_free, summed = sem("onehots_built"), sem("onehots_used"), sem("counts_summed")
    row_out, turned, turned_out = sem("counts_copied"), sem("counts_turned"), sem("turned_copied")
    row_stored, turned_stored, moved = sem("counts_stored"), sem("turned_stored"), sem("dst_moved")
    with (
        nc.sbuf_tensor("hot_dst", [P, GC, P], F16) as hot_dst,
        nc.sbuf_tensor("hot_src", [P, GC, NP], F16) as hot_src,
        nc.sbuf_tensor("count_row", [P, NP], F32) as count_row,
        nc.sbuf_tensor("count_turn", [P, NT, P], F32) as count_turn,
        nc.psum_tensor("count_ps", [P, NB, BLK], F32) as acc,
        nc.psum_tensor("cturn_ps", [P, 3, TB, P], F32) as tps,
        nc.Block() as block,
    ):
        dst_no = m.src_no[:, HALF:HALF + P]

        @block.vector
        def _(dve):
            used = dve.alloc_register("groups_built")
            dve.reg_mov(used, 0)
            with dve.Fori(0, NT) as t:
                first = dve.value_load(m.ranges[0:1, 0, ds(t, 1)], min_val=0, max_val=NG - 1)
                last = dve.value_load(m.ranges[0:1, 1, ds(t, 1)], min_val=1, max_val=NG)
                with dve.Fori(first, last) as g:
                    n = dve.snap(used)
                    for j in range(GC):
                        dve.wait_ge(slot_free, n * GC + (j + 1))
                        dve.tensor_scalar(hot_dst[:, j, :], dst_no, m.dst_col[:, ds(g * GC + j, 1)], None, ALU.is_equal)
                        dve.tensor_scalar(hot_src[:, j, :], m.src_no[:, :], m.src_col[:, ds(g * GC + j, 1)], None,
                                          ALU.is_equal).then_inc(built, 1)
                    dve.reg_add(used, used, 1)
                dve.wait_ge(built, dve.snap(used) * GC)
                dve.tensor_scalar(m.dst_col[:, :], m.dst_col[:, :], -float(P), None, ALU.add).then_inc(moved, 1)
                dve.wait_ge(moved, t + 1)

        @block.tensor
        def _(pe):
            used = pe.alloc_register("groups_used")
            pe.reg_mov(used, 0)
            pe.sem_inc(slot_free, GC)
            with pe.Fori(0, NT) as t:
                pe.wait_ge(row_out, t + 1)
                for b in range(NB):
                    pe.matmul(acc[:, b, :], m.zeros16[:, :], m.src_no[:, b * BLK:(b + 1) * BLK],
                              start=True, stop=False, skip_group_check=True)
                first = pe.value_load(m.ranges[0:1, 0, ds(t, 1)], min_val=0, max_val=NG - 1)
                last = pe.value_load(m.ranges[0:1, 1, ds(t, 1)], min_val=1, max_val=NG)
                with pe.Fori(first, last) as g:
                    n = pe.snap(used)
                    for j in range(GC):
                        pe.wait_ge(built, n * GC + (j + 1))
                        for b in range(NB):
                            mm = pe.matmul(acc[:, b, :], hot_dst[:, j, :], hot_src[:, j, b * BLK:(b + 1) * BLK],
                                           start=False, stop=False, skip_group_check=True)
                        mm.then_inc(slot_free, 1)
                    pe.reg_add(used, used, 1)
                for b in range(NB):
                    mm = pe.matmul(acc[:, b, :], m.zeros16[:, :], m.src_no[:, b * BLK:(b + 1) * BLK],
                                   start=False, stop=True, skip_group_check=True)
                mm.then_inc(summed, 1)
                pe.wait_ge(row_out, t + 2)
                for b in range(NB):
                    pe.wait_ge(turned_out, t * NB + max(1, b - 1))
                    for q in range(TB):
                        s = b * TB + q
                        mm = pe.transpose(tps[:, b % 3, q, :], count_row[:, s * P:(s + 1) * P], m.ident[:, :])
                    mm.then_inc(turned, 1)

        @block.scalar
        def _(act):
            act.sem_inc(row_out, 1)
            act.sem_inc(turned_out, 1)
            with act.Fori(0, NT) as t:
                act.wait_ge(summed, t + 1)
                act.activation(count_row[:, :], acc[:, :, :].rearrange("p b n -> p (b n)"), ACT.Copy,
                               accum_out=m.deg[:, ds(t, 1)]).then_inc(row_out, 1)
                for b in range(NB):
                    act.wait_ge(turned, t * NB + (b + 1))
                    act.activation(count_turn[:, b * TB:(b + 1) * TB, :], tps[:, b % 3, :, :], ACT.Copy).then_inc(turned_out, 1)
                act.wait_ge(row_stored, t * 16 + 16)
                act.wait_ge(turned_stored, t * 16 + 16)

        @block.sync
        def _(sp):
            with sp.Fori(0, NT) as t:
                sp.wait_ge(row_out, t + 2)
                sp.dma_start(m.A[ds(t, 1), :, :].rearrange("a p n -> (a p) n"), count_row[:, :]).then_inc(row_stored, 16)
                sp.wait_ge(turned_out, (t + 1) * NB + 1)
                sp.dma_start(m.AT[ds(t, 1), :, :].rearrange("a p n -> (a p) n"),
                             count_turn[:, :, :].rearrange("p s n -> p (s n)")).then_inc(turned_stored, 16)
            sp.wait_ge(row_stored, NT * 16)
            sp.wait_ge(turned_stored, NT * 16)



def stats_steps(own, dve, st, mean, var, tmp):
    own.step(dve.tensor_tensor(mean, st[:, :, 1], st[:, :, 4], ALU.add))
    own.step(dve.tensor_tensor(tmp, st[:, :, 1], st[:, :, 4], ALU.subtract))
    own.join(dve.tensor_tensor(var, st[:, :, 2], st[:, :, 5], ALU.add))
    own.step(dve.tensor_scalar(mean, mean, 0.5, None, ALU.mult))
    own.step(dve.tensor_scalar(var, var, 1.0 / D, EPS, ALU.mult, ALU.add))
    own.join(dve.tensor_tensor(tmp, tmp, tmp, ALU.mult))
    own.join(dve.scalar_tensor_tensor(var, tmp, 0.25, var, ALU.mult, ALU.add))


def phase_norm(nc, m, name, src, out, outT=None, gamma=None, beta=None, scale=None, finish=None):
    sem = nc.alloc_semaphore
    dve_own, want_root, root, ready = (sem(f"{name}_{s}") for s in ("dve", "want_root", "root", "ready"))
    turned, turned_out, affine_in = (sem(f"{name}_{s}") for s in ("turned", "turned_out", "affine_in"))
    with (
        nc.sbuf_tensor(f"{name}_st", [P, NT, 6], F32) as st,
        nc.sbuf_tensor(f"{name}_mean", [P, NT], F32) as mean,
        nc.sbuf_tensor(f"{name}_var", [P, NT], F32) as var,
        nc.sbuf_tensor(f"{name}_tmp", [P, NT], F32) as tmp,
        nc.sbuf_tensor(f"{name}_gb", [P, 2, D], F32) as gb,
        nc.psum_tensor(f"{name}_ps", [P, 4, TB, P], F32) as ps,
        nc.Block() as block,
    ):
        @block.sync
        def _(sp):
            if gamma is not None:
                sp.dma_start(gb[:, 0, :], gamma.partition_broadcast(P)).then_inc(affine_in, 16)
                sp.dma_start(gb[:, 1, :], beta.partition_broadcast(P)).then_inc(affine_in, 16)

        @block.vector
        def _(dve):
            own = Steps(dve, dve_own)
            with dve.Fori(0, NT) as t:
                dve.bn_stats(st[:, ds(t, 1), :].rearrange("p a s -> p (a s)"),
                             src[:, ds(t, 1), :].rearrange("p a d -> p (a d)")).then_inc(dve_own, 1)
            own.n = NT
            dve.wait_ge(dve_own, NT)
            stats_steps(own, dve, st, mean[:, :], var[:, :], tmp[:, :])
            dve.tensor_copy(var[:, :], var[:, :]).then_inc(want_root, 1)
            dve.wait_ge(root, 1)
            own.join(dve.reciprocal(tmp[:, :], var[:, :]))
            if gamma is not None:
                dve.wait_ge(affine_in, 32)
            for t in range(NT):
                if t:
                    pass
                if gamma is None:
                    dve.tensor_scalar(out[:, t, :], src[:, t, :], mean[:, t:t + 1], tmp[:, t:t + 1],
                                      ALU.subtract, ALU.mult).then_inc(ready, 1)
                    continue
                own.join(dve.tensor_scalar(out[:, t, :], src[:, t, :], mean[:, t:t + 1], tmp[:, t:t + 1],
                                           ALU.subtract, ALU.mult))
                own.join(dve.tensor_tensor(out[:, t, :], out[:, t, :], gb[:, 0, :], ALU.mult))
                last = dve.tensor_tensor(out[:, t, :], out[:, t, :], gb[:, 1, :], ALU.add)
                if finish:
                    own.join(last)
                    if finish == "relu_add":
                        last = dve.scalar_tensor_tensor(m.x[:, t, :], out[:, t, :], 0.0, m.x[:, t, :], ALU.max, ALU.add)
                    else:
                        last = dve.tensor_tensor(m.x[:, t, :], out[:, t, :], m.x[:, t, :], ALU.add)
                last.then_inc(ready, 1)
            if scale is not None:
                dve.wait_ge(turned, NB * DK)
                for t in range(NT):
                    dve.tensor_scalar(out[:, t, :], out[:, t, :], scale[:, t:t + 1], None, ALU.mult)

        @block.scalar
        def _(act):
            act.wait_ge(want_root, 1)
            act.activation(var[:, :], var[:, :], ACT.Sqrt).then_inc(root, 1)
            if outT is not None:
                for b in range(NB):
                    for k in range(DK):
                        n = b * DK + k
                        act.wait_ge(turned, n + 1)
                        act.activation(outT[:, k, b * BLK:(b + 1) * BLK],
                                       ps[:, n % 4, :, :].rearrange("p q n -> p (q n)"), ACT.Copy).then_inc(turned_out, 1)

        @block.tensor
        def _(pe):
            if outT is not None:
                for b in range(NB):
                    pe.wait_ge(ready, (b + 1) * TB)
                    for k in range(DK):
                        n = b * DK + k
                        if n >= 4:
                            pe.wait_ge(turned_out, n - 3)
                        for q in range(TB):
                            mm = pe.transpose(ps[:, n % 4, q, :], out[:, b * TB + q, k * P:(k + 1) * P], m.ident[:, :])
                        mm.then_inc(turned, 1)



def phase_degrees(nc, m):
    sem = nc.alloc_semaphore
    dve_own, root, spread, diag, copied = (sem(f"deg_{s}") for s in ("dve", "root", "spread", "diag", "copied"))
    with (
        nc.sbuf_tensor("deg_t", [P, 4, NT], F32) as t4,
        nc.sbuf_tensor("deg_diag", [P, 2, TB, P], F32) as dg,
        nc.psum_tensor("deg_ps", [P, 2, BLK], F32) as ps,
        nc.Block() as block,
    ):
        @block.vector
        def _(dve):
            own = Steps(dve, dve_own)
            own.step(dve.tensor_scalar(t4[:, 0, :], m.deg[:, :], 1.0, None, ALU.max))
            own.step(dve.tensor_scalar(t4[:, 1, :], m.deg[:, :], 1.0, None, ALU.add))
            own.step(dve.tensor_scalar(t4[:, 2, :], m.deg[:, :], 1e-12, None, ALU.max))
            own.join(dve.tensor_scalar(t4[:, 3, :], m.deg[:, :], 0.0, None, ALU.is_gt))
            own.step(dve.reciprocal(m.inv_count[:, :], t4[:, 0, :]))
            dve.wait_ge(root, 1)
            own.step(dve.reciprocal(m.dinv_loop[:, :], t4[:, 1, :]))
            own.join(dve.reciprocal(t4[:, 2, :], t4[:, 2, :]))
            own.join(dve.tensor_tensor(m.dinv[:, :], t4[:, 2, :], t4[:, 3, :], ALU.mult))
            for b in range(NB):
                if b >= 2:
                    dve.wait_ge(spread, b - 1)
                for q in range(TB):
                    t = b * TB + q
                    ins = dve.tensor_scalar(dg[:, b % 2, q, :], m.ident[:, :], m.dinv[:, t:t + 1], None, ALU.mult)
                ins.then_inc(diag, 1)

        @block.scalar
        def _(act):
            act.wait_ge(dve_own, 4)
            act.activation(t4[:, 1:3, :], t4[:, 1:3, :], ACT.Sqrt).then_inc(root, 1)
            for b in range(NB):
                act.wait_ge(spread, b + 1)
                act.activation(m.dinv_row[:, b * BLK:(b + 1) * BLK], ps[:, b % 2, :], ACT.Copy).then_inc(copied, 1)

        @block.tensor
        def _(pe):
            for b in range(NB):
                pe.wait_ge(diag, b + 1)
                if b >= 2:
                    pe.wait_ge(copied, b - 1)
                pe.matmul(ps[:, b % 2, :], m.ones[:, :], dg[:, b % 2, :, :].rearrange("p q n -> p (q n)"),
                          start=True, stop=True).then_inc(spread, 1)


def phase_transpose_weights(nc, m, mats):
    sem = nc.alloc_semaphore
    loaded, turned, copied = (sem(f"wturn_{s}") for s in ("loaded", "turned", "copied"))
    with (
        nc.sbuf_tensor("wturn_in", [P, len(mats), DK, D], F32) as w_in,
        nc.psum_tensor("wturn_ps", [P, 2, DK, D], F32) as ps,
        nc.Block() as block,
    ):
        @block.sync
        def _(sp):
            for i, (w, _o) in enumerate(mats):
                sp.dma_start(w_in[:, i, :, :], rows(w)).then_inc(loaded, 16)

        @block.tensor
        def _(pe):
            pe.wait_ge(loaded, 16 * len(mats))
            for i in range(len(mats)):
                if i >= 2:
                    pe.wait_ge(copied, i - 1)
                for ko in range(DK):
                    for ki in range(DK):
                        mm = pe.transpose(ps[:, i % 2, ki, ko * P:(ko + 1) * P], w_in[:, i, ko, ki * P:(ki + 1) * P],
                                          m.ident[:, :])
                mm.then_inc(turned, 1)

        @block.vector
        def _(dve):
            for i, (_w, out_sb) in enumerate(mats):
                dve.wait_ge(turned, i + 1)
                dve.tensor_copy(out_sb[:, :, :], ps[:, i % 2, :, :]).then_inc(copied, 1)


def phase_gather(nc, m, name, y, kind, w=None, w_self=None, bias=None):
    sem = nc.alloc_semaphore
    at_in = [sem(f"{name}_at_in{i}") for i in range(2)]
    agg_mm, agg_out, lin_mm, lin_out, bias_in, looped, selfed = (
        sem(f"{name}_{s}") for s in ("agg_mm", "agg_out", "lin_mm", "lin_out", "bias_in", "looped", "selfed"))
    with (
        nc.sbuf_tensor(f"{name}_at", [P, 2, TB, NT, P], F32) as at,
        nc.sbuf_tensor(f"{name}_agg", [P, DK, BLK], F32) as agg,
        nc.sbuf_tensor(f"{name}_self", [P, DK, BLK], F32) as own_x,
        nc.sbuf_tensor(f"{name}_bias", [P, D], F32) as bias_sb,
        nc.psum_tensor(f"{name}_ps", [P, DK, BLK], F32) as ps,
        nc.psum_tensor(f"{name}_lin", [P, TB, D], F32) as lin,
        nc.psum_tensor(f"{name}_lin2", [P, TB, D], F32) as lin2,
        nc.Block() as block,
    ):
        @block.sync
        def _(sp):
            if bias is not None:
                sp.dma_start(bias_sb[:, :], bias.partition_broadcast(P)).then_inc(bias_in, 16)
            for b in range(NB):
                if b >= 2:
                    sp.wait_ge(agg_mm, b - 1)
                sp.dma_start(at[:, b % 2, :, :, :].rearrange("p q s n -> p q (s n)"),
                             m.AT[b * TB:(b + 1) * TB, :, :].rearrange("t p n -> p t n")).then_inc(at_in[b % 2], 16)

        @block.gpsimd
        def _(pool):
            if kind == "loop":
                for b in range(NB):
                    pool.wait_ge(at_in[b % 2], 16 * (b // 2 + 1))
                    for q in range(TB):
                        spot = at[:, b % 2, q, b * TB + q, :]
                        pool.tensor_tensor(spot, spot, m.ident[:, :], ALU.add).then_inc(looped, 1)

        @block.tensor
        def _(pe):
            for b in range(NB):
                pe.wait_ge(at_in[b % 2], 16 * (b // 2 + 1))
                if kind == "loop":
                    pe.wait_ge(looped, TB * (b + 1))
                pe.wait_ge(agg_out, b)
                for k in range(DK):
                    for s in range(NT):
                        mm = pe.matmul(ps[:, k, :], y[:, s, k * P:(k + 1) * P], at[:, b % 2, :, s, :],
                                       start=(s == 0), stop=(s == NT - 1))
                mm.then_inc(agg_mm, 1)
                if kind == "keep":
                    continue
                pe.wait_ge(lin_out, b)
                if kind == "mean":
                    pe.wait_ge(selfed, b + 1)
                    for q in range(TB):
                        for k in range(DK):
                            pe.matmul(lin2[:, q, :], own_x[:, k, q * P:(q + 1) * P], w_self[:, k, :],
                                      start=(k == 0), stop=(k == DK - 1))
                pe.wait_ge(agg_out, b + 1)
                for q in range(TB):
                    for k in range(DK):
                        mm = pe.matmul(lin[:, q, :], agg[:, k, q * P:(q + 1) * P], w[:, k, :],
                                       start=(k == 0), stop=(k == DK - 1))
                mm.then_inc(lin_mm, 1)

        @block.scalar
        def _(act):
            if kind == "keep":
                return
            for b in range(NB):
                act.wait_ge(lin_mm, b)
                if kind == "mean":
                    act.activation(own_x[:, :, :], m.xT[:, :, b * BLK:(b + 1) * BLK], ACT.Copy).then_inc(selfed, 1)
                act.wait_ge(agg_mm, b + 1)
                act.activation(agg[:, :, :], ps[:, :, :], ACT.Copy).then_inc(agg_out, 1)

        @block.vector
        def _(dve):
            if bias is not None:
                dve.wait_ge(bias_in, 16)
            own = Steps(dve, sem(f"{name}_dve"))
            for b in range(NB):
                if kind == "keep":
                    dve.wait_ge(agg_mm, b + 1)
                    cut = slice(b * BLK, (b + 1) * BLK)
                    dve.tensor_tensor(m.xT[:, :, cut], ps[:, :, :],
                                      m.dinv_row[:, cut].unsqueeze(1).to_broadcast([P, DK, BLK]), ALU.mult).then_inc(agg_out, 1)
                    continue
                dve.wait_ge(lin_mm, b + 1)
                for q in range(TB):
                    t = b * TB + q
                    if kind == "mean":
                        own.join(dve.scalar_tensor_tensor(m.x[:, t, :], lin[:, q, :], m.inv_count[:, t:t + 1],
                                                          m.x[:, t, :], ALU.mult, ALU.add))
                        own.join(dve.tensor_tensor(m.x[:, t, :], lin2[:, q, :], m.x[:, t, :], ALU.add))
                        ins = dve.tensor_tensor(m.x[:, t, :], m.x[:, t, :], bias_sb[:, :], ALU.add)
                    else:
                        ins = dve.scalar_tensor_tensor(m.o[:, t, :], lin[:, q, :], m.dinv_loop[:, t:t + 1],
                                                       bias_sb[:, :], ALU.mult, ALU.add)
                ins.then_inc(lin_out, 1)



def softmax_steps(own, dve, exp, lg, top, tmp, T, EX):
    def wide(a):
        return a.unsqueeze(2).to_broadcast([P, T, EX])
    own.join(dve.tensor_reduce(top, lg, AX.X, ALU.max))
    own.join(dve.tensor_tensor(lg, lg, wide(top), ALU.subtract))
    exp()
    own.join(dve.tensor_reduce(tmp, lg, AX.X, ALU.add))
    own.join(dve.reciprocal(tmp, tmp))
    own.join(dve.tensor_tensor(lg, lg, wide(tmp), ALU.mult))


def top2_steps(own, dve, exp, lg, s, no, wd, T, EX):
    def wide(a):
        return a.unsqueeze(2).to_broadcast([P, T, EX])

    def pick(vals, top, at, hot):
        own.join(dve.tensor_reduce(top, vals, AX.X, ALU.max))
        own.join(dve.tensor_tensor(hot, vals, wide(top), ALU.is_equal))
        own.join(dve.tensor_tensor(hot, hot, no, ALU.mult))
        own.join(dve.tensor_reduce(at, hot, AX.X, ALU.min))
        own.join(dve.tensor_tensor(hot, no, wide(at), ALU.is_equal))

    pick(lg, s.m1, s.i1, s.hot1)
    own.join(dve.scalar_tensor_tensor(s.rest, s.hot1, -BIG, lg, ALU.mult, ALU.add))
    pick(s.rest, s.m2, s.i2, s.hot2)
    own.join(dve.tensor_tensor(s.d, s.m2, s.m1, ALU.subtract))
    exp()
    own.join(dve.tensor_scalar(s.w1, s.d, 1.0, None, ALU.add))
    own.join(dve.reciprocal(s.w1, s.w1))
    own.join(dve.tensor_tensor(s.w2, s.w1, s.d, ALU.mult))
    own.join(dve.tensor_tensor(s.hot1, s.hot1, wide(s.w1), ALU.mult))
    own.join(dve.tensor_tensor(s.hot2, s.hot2, wide(s.w2), ALU.mult))
    own.join(dve.tensor_tensor(wd, s.hot1, s.hot2, ALU.add))


def phase_route(nc, m, name, kind, EX, wr, br, bout, dest, base, wr1=None, br1=None):
    sem = nc.alloc_semaphore
    T = 1 if kind == "mean" else NT
    loaded, dve_own, act_own, want_exp, exped, pe_own, pe_hid, act_hid, w_ready, mixed, added, w_turned = (
        sem(f"{name}_{s}") for s in ("loaded", "dve", "act", "want_exp", "exped", "pe", "pe_hid", "act_hid",
                                     "w_ready", "mixed", "added", "w_turned"))
    KR = 1 if kind == "mlp" else DK
    s = Mem()
    with ExitStack() as ctx:
        sb = lambda n, shape, dt=F32: ctx.enter_context(nc.sbuf_tensor(f"{name}_{n}", shape, dt))
        wr_sb = sb("wr", [P, KR, EX])
        br_sb = sb("br", [P, EX])
        bo_sb = sb("bo", [P, D])
        lg = sb("lg", [P, T, EX])
        s.m1, s.i1, s.m2, s.i2, s.d, s.w1, s.w2, s.tmp = (
            sb(n, [P, T])[:, :] for n in ("m1", "i1", "m2", "i2", "d", "w1", "w2", "tmp"))
        s.hot1, s.hot2, s.rest = (sb(n, [P, T, EX])[:, :, :] for n in ("hot1", "hot2", "rest"))
        wT = sb("wT", [P, NT, P])
        mean = sb("mean", [P, DK])
        mean_w = sb("mean_w", [P, DK, P])
        w1_sb = sb("w_hid", [P, DK, P])
        b1_sb = sb("b_hid", [P, 1])
        hid = sb("hid", [P, NP]) if kind == "mlp" else None
        psl = ctx.enter_context(nc.psum_tensor(f"{name}_psl", [P, NT, EX], F32))
        psh = ctx.enter_context(nc.psum_tensor(f"{name}_psh", [P, 2, BLK], F32))
        pst = ctx.enter_context(nc.psum_tensor(f"{name}_pst", [P, 2, TB, P], F32))
        psm = ctx.enter_context(nc.psum_tensor(f"{name}_psm", [P, 2, BLK], F32))
        block = ctx.enter_context(nc.Block())
        nload = 5 if kind == "mlp" else 3
        no = m.expert_no[:, 0:T, 0:EX]

        @block.sync
        def _(sp):
            sp.dma_start(wr_sb[:, :, :], rows(wr)).then_inc(loaded, 16)
            sp.dma_start(br_sb[:, :], br.partition_broadcast(P)).then_inc(loaded, 16)
            sp.dma_start(bo_sb[0:EX, :], bout).then_inc(loaded, 16)
            if kind == "mlp":
                sp.dma_start(w1_sb[:, :, :], rows(wr1)).then_inc(loaded, 16)
                sp.dma_start(b1_sb[:, :], per_partition(br1), allow_slow_non_contiguous=True).then_inc(loaded, 16)

        @block.tensor
        def _(pe):
            pe.wait_ge(loaded, 16 * nload)
            if kind == "mean":
                pe.wait_ge(w_ready, 1)
                for k in range(DK):
                    mm = pe.matmul(psl[:, 0, :], mean_w[:, k, :], wr_sb[:, k, :], start=(k == 0), stop=(k == DK - 1))
                mm.then_inc(pe_own, 1)
            elif kind == "mlp":
                for b in range(NB):
                    if b >= 2:
                        pe.wait_ge(act_hid, b - 1)
                    for k in range(DK):
                        mm = pe.matmul(psh[:, b % 2, :], w1_sb[:, k, :], m.xT[:, k, b * BLK:(b + 1) * BLK],
                                       start=(k == 0), stop=(k == DK - 1))
                    mm.then_inc(pe_hid, 1)
                for t in range(NT):
                    pe.wait_ge(act_hid, t // TB + 1)
                    mm = pe.matmul(psl[:, t, :], hid[:, t * P:(t + 1) * P], wr_sb[:, 0, :], start=True, stop=True)
                mm.then_inc(pe_own, 1)
            else:
                for t in range(NT):
                    for k in range(DK):
                        mm = pe.matmul(psl[:, t, :], m.xT[:, k, t * P:(t + 1) * P], wr_sb[:, k, :],
                                       start=(k == 0), stop=(k == DK - 1))
                mm.then_inc(pe_own, 1)
            pe.wait_ge(w_ready, 2 if kind == "mean" else 1)
            for b in range(NB):
                if b >= 2:
                    pe.wait_ge(w_turned, b - 1)
                for q in range(TB):
                    mm = pe.transpose(pst[0:EX, b % 2, q, :], m.wd[:, b * TB + q, 0:EX], m.ident[:, :])
                mm.then_inc(pe_own, 1)
            for t in range(NT):
                pe.wait_ge(w_turned, t // TB + 1)
                if t >= 2:
                    pe.wait_ge(added, t - 1)
                pe.matmul(psm[:, t % 2, 0:D], wT[0:EX, t, :], bo_sb[0:EX, :], start=True, stop=True).then_inc(mixed, 1)

        @block.scalar
        def _(act):
            if kind == "mlp":
                act.wait_ge(loaded, 16 * nload)
                for b in range(NB):
                    act.wait_ge(pe_hid, b + 1)
                    act.activation(hid[:, b * BLK:(b + 1) * BLK], psh[:, b % 2, :], ACT.Relu,
                                   bias=b1_sb[:, 0:1]).then_inc(act_hid, 1)
            exps = {"mean": [lg, lg, s.d], "mlp": [lg, s.d], "top": [s.d], "dense": [lg]}[kind]
            for i, what in enumerate(exps):
                ap = what if what is s.d else lg[:, :, :]
                act.wait_ge(want_exp, i + 1)
                act.activation(ap, ap, ACT.Exp).then_inc(exped, 1)
            for b in range(NB):
                act.wait_ge(pe_own, 1 + b + 1)
                act.activation(wT[0:EX, b * TB:(b + 1) * TB, :], pst[0:EX, b % 2, :, :], ACT.Copy).then_inc(w_turned, 1)

        @block.vector
        def _(dve):
            own = Steps(dve, dve_own)
            asked = [0]

            def exp():
                dve.sem_inc(want_exp, 1)
                asked[0] += 1
                dve.wait_ge(exped, asked[0])

            L = lg[:, :, :]
            if kind == "mean":
                for k in range(DK):
                    own.join(dve.tensor_reduce(mean[:, k:k + 1], m.xT[:, k, 0:N], AX.X, ALU.add))
                own.join(dve.tensor_scalar(mean[:, :], mean[:, :], 1.0 / N, None, ALU.mult))
                own.join(dve.tensor_copy(mean_w[:, :, :], mean[:, :].unsqueeze(2).to_broadcast([P, DK, P])))
                dve.sem_inc(w_ready, 1)
            dve.wait_ge(loaded, 16 * nload)
            dve.wait_ge(pe_own, 1)
            own.join(dve.tensor_tensor(L, psl[:, 0:T, :], br_sb[:, :].unsqueeze(1).to_broadcast([P, T, EX]), ALU.add))
            if kind != "top":
                softmax_steps(own, dve, exp, L, s.m1, s.tmp, T, EX)
            if kind == "mean":
                capacity = float(-(-N * 5 // (4 * EX)))
                own.join(dve.tensor_scalar(s.rest, L, float(N), None, ALU.mult))
                own.join(dve.reciprocal(s.rest, s.rest))
                own.join(dve.tensor_scalar(s.rest, s.rest, capacity, 1.0, ALU.mult, ALU.min))
                own.join(dve.tensor_tensor(L, L, s.rest, ALU.mult))
                softmax_steps(own, dve, exp, L, s.m1, s.tmp, T, EX)
            wd = m.wd[:, 0:T, 0:EX]
            if kind == "dense":
                own.join(dve.tensor_copy(wd, L))
            else:
                top2_steps(own, dve, exp, L, s, no, wd, T, EX)
            if kind == "mean":
                own.join(dve.tensor_copy(m.wd[:, 1:NT, 0:EX], m.wd[:, 0:1, 0:EX].to_broadcast([P, NT - 1, EX])))
                own.step(dve.tensor_copy(m.pair_w[:, 0:1], s.w1))
                own.step(dve.tensor_copy(m.pair_w[:, 1:2], s.w2))
                for i, at in enumerate((s.i1, s.i2)):
                    for c in range(DK):
                        own.join(dve.tensor_scalar(s.tmp, at, 8.0, float(D), ALU.add, ALU.mult))
                        own.join(dve.tensor_scalar(s.tmp, s.tmp, m.part_no[:, 0:1], float(c * P), ALU.add, ALU.add))
                        own.join(dve.tensor_copy(m.w1_rows[:, i, c:c + 1], s.tmp))
                    for c in range(FH // P):
                        own.join(dve.tensor_scalar(s.tmp, at, 8.0, float(FH), ALU.add, ALU.mult))
                        own.join(dve.tensor_scalar(s.tmp, s.tmp, m.part_no[:, 0:1], float(c * P), ALU.add, ALU.add))
                        own.join(dve.tensor_copy(m.w2_rows[:, i, c:c + 1], s.tmp))
            dve.sem_inc(w_ready, 1)
            for t in range(NT):
                dve.wait_ge(mixed, t + 1)
                dve.tensor_tensor(dest[:, t, :], psm[:, t % 2, 0:D], base[:, t, :], ALU.add).then_inc(added, 1)



def phase_experts(nc, m, name, EX, func, widths, mats, biases, dest, weight=None, picked=False, bn=None):
    sem = nc.alloc_semaphore
    NH = len(widths)
    FT = [w // P for w in widths]
    KT = [DK] + FT
    NL = NH + 1
    YC, HC = TB + 1, FT[-1] + 1
    w_in = [sem(f"{name}_w_in{u}") for u in range(2)]
    h_mm = [sem(f"{name}_h{i}_mm") for i in range(NH)]
    h_act = [sem(f"{name}_h{i}_act") for i in range(NH)]
    y_mm, y_add, bn_in, bn_dve, bn_root = (sem(f"{name}_{s}") for s in ("y_mm", "y_add", "bn_in", "bn_dve", "bn_root"))
    nload = NL + NH
    bn_kept = sem(f"{name}_bn_kept")
    if picked:
        nload = DK + 2 * FT[0]
    with ExitStack() as ctx:
        sb = lambda n, shape, dt=F32: ctx.enter_context(nc.sbuf_tensor(f"{name}_{n}", shape, dt))
        outs = widths + [D]
        w_sb = [sb(f"w{i}", [P, 2, KT[i], outs[i]]) for i in range(NL)]
        b_sb = [sb(f"b{i}", [P, 2, 2, FT[i]]) for i in range(NH)]
        h_sb = [sb(f"h{i}", [P, 3, FT[i], BLK]) for i in range(NH)]
        if bn is not None:
            v_rows = [sb(f"vr{i}", [EX * FT[i], 5, P]) for i in range(NH)]
            v_sb = [sb(f"v{i}", [P, 5, EX * FT[i]]) for i in range(NH)]
            kept = [nc.dram_tensor(f"{name}_kept{i}", (P, 2, EX * FT[i]), F32, kind="Internal").ap() for i in range(NH)]
        h_ps = [ctx.enter_context(nc.psum_tensor(f"{name}_hps{i}", [P, FT[i], BLK], F32)) for i in range(NH)]
        y_ps = ctx.enter_context(nc.psum_tensor(f"{name}_yps", [P, TB, BLK], F32))
        block = ctx.enter_context(nc.Block())
        per_pair = 2 * NB
        pairs = EX // 2

        def load_pair(eng, e2):
            for u in range(2):
                e = e2 * 2 + u
                if picked:
                    for k in range(DK):
                        eng.indirect_dma_start(w_sb[0][:, u, k, :], None, mats[0], bass.IndirectOffsetOnAxis(
                            ap=m.w1_rows[:, u, k:k + 1], axis=0)).then_inc(w_in[u], 16)
                    for k in range(FT[0]):
                        at = bass.IndirectOffsetOnAxis(ap=m.w2_rows[:, u, k:k + 1], axis=0)
                        eng.indirect_dma_start(w_sb[1][:, u, k, :], None, mats[1], at).then_inc(w_in[u], 16)
                        eng.indirect_dma_start(b_sb[0][:, u, 0, k:k + 1], None, biases[0], at).then_inc(w_in[u], 16)
                    continue
                if not isinstance(e2, int) or e2:
                    eng.wait_ge(y_mm, (e - 1) * (NB * TB) + YC)
                for i in range(NL):
                    eng.dma_start(w_sb[i][:, u, :, :], mats[i](e)).then_inc(w_in[u], 16)
                for i in range(NH):
                    if bn is None:
                        eng.dma_start(b_sb[i][:, u, 0, :], biases[i](e), allow_slow_non_contiguous=True).then_inc(w_in[u], 16)
                    else:
                        eng.dma_start(b_sb[i][:, u, :, :], kept[i][:, :, ds(e * FT[i], FT[i])]).then_inc(w_in[u], 16)

        @block.sync
        def _(sp):
            if picked:
                return
            if bn is not None:
                for i in range(NH):
                    for j, v in enumerate((biases[i],) + bn[i]):
                        sp.dma_start(v_rows[i][:, j, :], v.rearrange("e (f p) -> (e f) p", p=P)).then_inc(bn_in, 16)
                sp.wait_ge(bn_dve, 3)
                for i in range(NH):
                    sp.dma_start(kept[i], v_sb[i][:, 0:2, :]).then_inc(bn_kept, 16)
                sp.wait_ge(bn_kept, 16 * NH)
            load_pair(sp, 0)
            if pairs > 1:
                with sp.Fori(1, pairs) as e2:
                    load_pair(sp, e2)

        @block.gpsimd
        def _(pool):
            if picked:
                load_pair(pool, 0)

        @block.tensor
        def _(pe):
            def layer0(e2, v):
                u, b = v // NB, v % NB
                n = e2 * per_pair + v
                if b == 0:
                    pe.wait_ge(w_in[u], (e2 + 1) * (16 * nload))
                for f in range(FT[0]):
                    pe.wait_ge(h_act[0], n * FT[0] + (f + 1))
                    for k in range(DK):
                        mm = pe.matmul(h_ps[0][:, f, :], w_sb[0][:, u, k, f * P:(f + 1) * P],
                                       m.xT[:, k, b * BLK:(b + 1) * BLK], start=(k == 0), stop=(k == DK - 1))
                    mm.then_inc(h_mm[0], 1)

            def layer1(e2, v):
                u, b = v // NB, v % NB
                n = e2 * per_pair + v
                pe.wait_ge(h_act[0], (n + 2) * FT[0])
                for f in range(FT[1]):
                    pe.wait_ge(h_act[1], n * FT[1] + (f + 1))
                    for k in range(FT[0]):
                        mm = pe.matmul(h_ps[1][:, f, :], w_sb[1][:, u, k, f * P:(f + 1) * P], h_sb[0][:, b % 3, k, :],
                                       start=(k == 0), stop=(k == FT[0] - 1))
                    mm.then_inc(h_mm[1], 1)

            def last(e2, v):
                u, b = v // NB, v % NB
                n = e2 * per_pair + v
                pe.wait_ge(h_act[-1], (n + 2) * FT[-1])
                for q in range(TB):
                    pe.wait_ge(y_add, n * TB + (q + 1))
                    for k in range(FT[-1]):
                        mm = pe.matmul(y_ps[:, q, 0:D], h_sb[-1][:, b % 3, k, q * P:(q + 1) * P], w_sb[-1][:, u, k, :],
                                       start=(k == 0), stop=(k == FT[-1] - 1))
                    mm.then_inc(y_mm, 1)

            def pair(e2, more):
                for v in range(per_pair):
                    if NH == 2:
                        layer1(e2, v)
                    if v + 1 < per_pair:
                        layer0(e2, v + 1)
                    elif more:
                        layer0(e2 + 1, 0)
                    last(e2, v)

            if bn is not None:
                pe.wait_ge(bn_in, 16 * 5 * NH)
                for i in range(NH):
                    R = EX * FT[i]
                    for j in range(5):
                        pe.transpose(y_ps[:, i, j * R:(j + 1) * R], v_rows[i][:, j, :], m.ident[0:R, 0:R]).then_inc(bn_root, 1)
                pe.wait_ge(bn_dve, 1)
            pe.sem_inc(y_mm, YC)
            if NH == 2:
                pe.sem_inc(h_mm[1], HC)
            layer0(0, 0)
            if pairs > 1:
                with pe.Fori(0, pairs - 1) as e2:
                    pair(e2, True)
            pair(pairs - 1, False)

        @block.scalar
        def _(act):
            for i in range(NH):
                act.sem_inc(h_act[i], FT[i])
            if bn is not None:
                act.wait_ge(bn_dve, 2)
                for i in range(NH):
                    act.activation(v_sb[i][:, 4, :], v_sb[i][:, 4, :], ACT.Sqrt).then_inc(bn_root, 1)

            def hidden(i, e2, v):
                u, b = v // NB, v % NB
                n = e2 * per_pair + v
                if i == NH - 1:
                    act.wait_ge(y_mm, n * TB + (YC - TB))
                else:
                    act.wait_ge(h_mm[i + 1], n * FT[i + 1] + (HC - FT[i + 1]))
                if b == 0:
                    act.wait_ge(w_in[u], (e2 + 1) * (16 * nload))
                for f in range(FT[i]):
                    act.wait_ge(h_mm[i], n * FT[i] + (f + 1 + (HC if i else 0)))
                    bias = b_sb[i][:, u, 0, f:f + 1]
                    scale = 1.0 if bn is None else b_sb[i][:, u, 1, f:f + 1]
                    act.activation(h_sb[i][:, b % 3, f, :], h_ps[i][:, f, :], func, bias=bias,
                                   scale=scale).then_inc(h_act[i], 1)

            def pair(e2, more):
                for v in range(per_pair):
                    if NH == 2:
                        hidden(1, e2, v)
                    if v + 1 < per_pair:
                        hidden(0, e2, v + 1)
                    elif more:
                        hidden(0, e2 + 1, 0)

            hidden(0, 0, 0)
            if pairs > 1:
                with act.Fori(0, pairs - 1) as e2:
                    pair(e2, True)
            pair(pairs - 1, False)

        @block.vector
        def _(dve):
            dve.sem_inc(y_add, TB)
            own = Steps(dve, sem(f"{name}_dve"))
            if bn is not None:
                dve.wait_ge(bn_root, 5 * NH)
                for i in range(NH):
                    R = EX * FT[i]
                    own.join(dve.tensor_copy(v_sb[i][:, :, :].rearrange("p j r -> p (j r)"), y_ps[:, i, 0:5 * R]))
                dve.sem_inc(bn_dve, 1)
                for i in range(NH):
                    own.join(dve.tensor_scalar(v_sb[i][:, 4, :], v_sb[i][:, 4, :], 1e-3, None, ALU.add))
                dve.sem_inc(bn_dve, 1)
                dve.wait_ge(bn_root, 6 * NH)
                for i in range(NH):
                    b_, g_, be_, mu_, sd = (v_sb[i][:, j, :] for j in range(5))
                    own.join(dve.reciprocal(sd, sd))
                    own.join(dve.tensor_tensor(g_, g_, sd, ALU.mult))
                    own.join(dve.tensor_tensor(b_, b_, mu_, ALU.subtract))
                    own.join(dve.tensor_tensor(b_, b_, g_, ALU.mult))
                    own.join(dve.tensor_tensor(b_, b_, be_, ALU.add))
                dve.sem_inc(bn_dve, 1)

            def pair(e2):
                for v in range(per_pair):
                    u, b = v // NB, v % NB
                    n = e2 * per_pair + v
                    for q in range(TB):
                        t = b * TB + q
                        dve.wait_ge(y_mm, n * TB + (q + 1 + YC))
                        if picked:
                            w = m.pair_w[:, u:u + 1]
                        elif weight is None:
                            w = m.ones[:, 0:1]
                        else:
                            w = weight[:, t, ds(e2 * 2 + u, 1)]
                        dve.scalar_tensor_tensor(dest[:, t, :], y_ps[:, q, 0:D], w, dest[:, t, :], ALU.mult,
                                                 ALU.add).then_inc(y_add, 1)

            if pairs > 1:
                with dve.Fori(0, pairs) as e2:
                    pair(e2)
            else:
                pair(0)


def phase_add_row(nc, m, name, row):
    sem = nc.alloc_semaphore
    row_in = sem(f"{name}_in")
    with nc.sbuf_tensor(f"{name}_row", [P, D], F32) as r, nc.Block() as block:
        @block.sync
        def _(sp):
            sp.dma_start(r[:, :], row.partition_broadcast(P)).then_inc(row_in, 16)

        @block.vector
        def _(dve):
            dve.wait_ge(row_in, 16)
            dve.tensor_tensor(m.x[:, :, :], m.x[:, :, :], r[:, :].unsqueeze(1).to_broadcast([P, NT, D]), ALU.add)



def phase_attention(nc, m, W, Wl, Wr, b):
    H, DO = 4, 64
    sem = nc.alloc_semaphore
    q_ = Mem()
    q_.w_in, q_.pe, q_.act, q_.dve, q_.xaug = (sem(f"att_{n}") for n in ("w_in", "pe", "act", "dve", "xaug"))
    q_.z, q_.lrelu, q_.exped, q_.scored = (sem(f"att_{n}") for n in ("z", "lrelu", "exped", "scored"))
    q_.o_mm, q_.o_out, q_.o_turn, q_.fin = (sem(f"att_{n}") for n in ("o_mm", "o_out", "o_turn", "fin"))
    q_.spread, q_.spread_out, q_.min, q_.elu, q_.eluxp = (
        sem(f"att_{n}") for n in ("spread", "spread_out", "min", "elu", "eluxp"))
    a_in = [sem(f"att_a_in{i}") for i in range(2)]
    with ExitStack() as ctx:
        sb = lambda n, shape, dt=F32: ctx.enter_context(nc.sbuf_tensor(f"att_{n}", shape, dt))
        w_sb = sb("w", [P, DK, DO])
        wlr = sb("wlr", [DO, 2, H])
        wl_wide = sb("wl_wide", [DO, H, P])
        xlT = sb("xlT", [DO, NP])
        xaug = sb("xaug", [P, NT, DO + 1])
        er = sb("er", [P, NT, H])
        elB = sb("elB", [P, H, NP])
        a_sb = sb("a", [P, 2, NT // 4, BLK])
        z = m.o[:, 0:4 * H, :].rearrange("p (a h c) d -> p a h (c d)", a=2, h=H)
        ex = m.xn[:, 0:4 * H, :].rearrange("p (a h c) d -> p a h (c d)", a=2, h=H)
        oT = sb("oT", [DO + 1, H, BLK])
        bias = sb("bias", [P, DO])
        fin = sb("fin", [P, H, DO])
        neg = sb("neg", [P, H, DO])
        rs = sb("rs", [P, H])
        ps = ctx.enter_context(nc.psum_tensor("att_ps", [P, 8, BLK], F32))

        with nc.Block() as block:
            @block.sync
            def _(sp):
                sp.dma_start(w_sb[:, :, :], rows(W)).then_inc(q_.w_in, 16)
                for i, w in enumerate((Wl, Wr)):
                    sp.dma_start(wlr[:, i, :], w.rearrange("h d -> d h"), allow_slow_non_contiguous=True).then_inc(q_.w_in, 16)
                sp.dma_start(bias[:, :], b.partition_broadcast(P)).then_inc(q_.w_in, 16)

            @block.tensor
            def _(pe):
                pe.wait_ge(q_.w_in, 64)
                for c in range(NB):
                    if c >= 2:
                        pe.wait_ge(q_.act, c - 1)
                    for k in range(DK):
                        mm = pe.matmul(ps[0:DO, c % 2, :], w_sb[:, k, :], m.xT[:, k, c * BLK:(c + 1) * BLK],
                                       start=(k == 0), stop=(k == DK - 1))
                    mm.then_inc(q_.pe, 1)
                for t in range(NT):
                    pe.wait_ge(q_.act, t // TB + 1)
                    pe.transpose(ps[:, 2 + t // 8, (t % 8) * DO:(t % 8 + 1) * DO], xlT[:, t * P:(t + 1) * P],
                                 m.ident[0:DO, 0:DO])
                    mm = pe.matmul(ps[:, 5, t * H:(t + 1) * H], xlT[:, t * P:(t + 1) * P], wlr[:, 1, :],
                                   start=True, stop=True)
                mm.then_inc(q_.xaug, 1)
                pe.wait_ge(q_.dve, 1)
                for h in range(H):
                    for c in range(NB):
                        n = h * NB + c
                        if n >= 2:
                            pe.wait_ge(q_.spread_out, n - 1)
                        pe.matmul(ps[:, 6 + n % 2, :], wl_wide[:, h, :], xlT[:, c * BLK:(c + 1) * BLK],
                                  start=True, stop=True).then_inc(q_.spread, 1)

            @block.scalar
            def _(act):
                for c in range(NB):
                    act.wait_ge(q_.pe, c + 1)
                    act.activation(xlT[:, c * BLK:(c + 1) * BLK], ps[0:DO, c % 2, :], ACT.Copy).then_inc(q_.act, 1)
                for h in range(H):
                    for c in range(NB):
                        act.wait_ge(q_.spread, h * NB + c + 1)
                        act.activation(elB[:, h, c * BLK:(c + 1) * BLK], ps[:, 6 + (h * NB + c) % 2, :],
                                       ACT.Copy).then_inc(q_.spread_out, 1)

            @block.vector
            def _(dve):
                dve.wait_ge(q_.w_in, 64)
                dve.tensor_copy(wl_wide[:, :, :], wlr[:, 0, :].unsqueeze(2).to_broadcast([DO, H, P])).then_inc(q_.dve, 1)
                dve.memset(xaug[:, :, DO:DO + 1], 1.0)
                dve.wait_ge(q_.xaug, 1)
                dve.tensor_copy(xaug[:, 0:16, 0:DO], ps[:, 2:4, :].rearrange("p a (t d) -> p (a t) d", d=DO))
                dve.tensor_copy(xaug[:, 16:NT, 0:DO], ps[:, 4, 0:(NT - 16) * DO].rearrange("p (t d) -> p t d", d=DO))
                dve.tensor_copy(er[:, :, :], ps[:, 5, 0:NT * H].rearrange("p (t h) -> p t h", h=H))

        QN = NT // 4
        with nc.Block() as block:
            @block.sync
            def _(sp):
                with sp.Fori(0, NB) as c:
                    for i in range(4):
                        sp.wait_ge(q_.scored, c * NT + (i * QN + 1))
                        sp.dma_start(a_sb[:, i % 2, :, :],
                                     m.A[i * QN:(i + 1) * QN, :, ds(c * BLK, BLK)].rearrange("t p n -> p t n")
                                     ).then_inc(a_in[i % 2], 16)

            @block.vector
            def _(dve):
                own = Steps(dve, q_.elu)
                dve.sem_inc(q_.scored, QN + 1)
                with dve.Fori(0, NB) as c:
                    def scores(s):
                        n = c * NT + s
                        for h in range(H):
                            dve.tensor_scalar(z[:, s % 2, h, :], elB[:, h, ds(c * BLK, BLK)], er[:, s, h:h + 1], EXP_TOP,
                                              ALU.add, ALU.min).then_inc(q_.z, 1)
                        dve.wait_ge(q_.z, (n + 1) * H)
                        dve.wait_ge(q_.o_mm, n * H + 1)
                        dve.scalar_tensor_tensor(ex[:, s % 2, :, :].rearrange("p h n -> p (h n)"),
                                                 z[:, s % 2, :, :].rearrange("p h n -> p (h n)"), 0.2,
                                                 z[:, s % 2, :, :].rearrange("p h n -> p (h n)"),
                                                 ALU.mult, ALU.max).then_inc(q_.lrelu, 1)

                    def mask(s):
                        n = c * NT + s
                        dve.wait_ge(q_.exped, n + 1)
                        if s % QN == 0:
                            dve.wait_ge(a_in[s // QN % 2], c * 32 + 16 * (s // QN // 2 + 1))
                        dve.tensor_tensor(ex[:, s % 2, :, :], ex[:, s % 2, :, :],
                                          a_sb[:, s // QN % 2, s % QN, :].unsqueeze(1).to_broadcast([P, H, BLK]),
                                          ALU.mult).then_inc(q_.scored, 1)

                    scores(0)
                    for s in range(NT):
                        if s + 1 < NT:
                            scores(s + 1)
                        mask(s)
                    for q in range(TB):
                        j = c * TB + q
                        dve.wait_ge(q_.o_turn, j + 1)
                        o = ps[:, 4 + 2 * (q % 2), 0:H * (DO + 1)].rearrange("p (h d) -> p h d", h=H)
                        k = (c * TB + q) * 6
                        own.n = k
                        own.join(dve.tensor_scalar(rs[:, :], o[:, :, DO], 1e-12, None, ALU.max))
                        own.join(dve.reciprocal(rs[:, :], rs[:, :]))
                        own.join(dve.tensor_tensor(fin[:, :, :], o[:, :, 0:DO], rs[:, :].unsqueeze(2).to_broadcast([P, H, DO]), ALU.mult))
                        own.join(dve.tensor_tensor(fin[:, :, :], fin[:, :, :], bias[:, :].unsqueeze(1).to_broadcast([P, H, DO]), ALU.add))
                        dve.tensor_scalar(neg[:, :, :], fin[:, :, :], 0.0, None, ALU.min).then_inc(q_.min, 1)
                        dve.wait_ge(q_.eluxp, j + 1)
                        own.join(dve.scalar_tensor_tensor(fin[:, :, :], fin[:, :, :], 0.0, neg[:, :, :], ALU.max, ALU.add))
                        xt = m.x[:, ds(j, 1), :].rearrange("p a d -> p (a d)")
                        own.join(dve.scalar_tensor_tensor(xt, fin[:, :, :].rearrange("p h d -> p (h d)"), -1.0, xt, ALU.add, ALU.add))
                        dve.sem_inc(q_.fin, 1)

            @block.scalar
            def _(act):
                act.sem_inc(q_.o_out, 1)
                with act.Fori(0, NB) as c:
                    for s in range(NT):
                        act.wait_ge(q_.lrelu, c * NT + (s + 1))
                        v = ex[:, s % 2, :, :]
                        act.activation(v, v, ACT.Exp).then_inc(q_.exped, 1)
                    act.wait_ge(q_.o_mm, (c + 1) * (NT * H) + (H + 1))
                    act.activation(oT[:, :, :], ps[0:DO + 1, 0:H, :], ACT.Copy).then_inc(q_.o_out, 1)
                    for q in range(TB):
                        act.wait_ge(q_.min, c * TB + (q + 1))
                        act.activation(neg[:, :, :], neg[:, :, :], ACT.Exp).then_inc(q_.eluxp, 1)

            @block.tensor
            def _(pe):
                pe.sem_inc(q_.o_mm, H + 1)
                with pe.Fori(0, NB) as c:
                    pe.wait_ge(q_.o_out, c + 1)
                    for s in range(NT):
                        pe.wait_ge(q_.scored, c * NT + (s + 2 + QN))
                        for h in range(H):
                            pe.matmul(ps[0:DO + 1, h, :], xaug[:, s, :], ex[:, s % 2, h, :],
                                      start=(s == 0), stop=(s == NT - 1)).then_inc(q_.o_mm, 1)
                    pe.wait_ge(q_.o_out, c + 2)
                    for q in range(TB):
                        if q >= 2:
                            pe.wait_ge(q_.fin, c * TB + (q - 1))
                        for h in range(H):
                            mm = pe.transpose(ps[:, 4 + 2 * (q % 2), h * (DO + 1):(h + 1) * (DO + 1)],
                                              oT[:, h, q * P:(q + 1) * P], m.ident[0:DO + 1, 0:DO + 1])
                        mm.then_inc(q_.o_turn, 1)


def phase_store(nc, m, out):
    stored = nc.alloc_semaphore("stored")
    full = N // P
    with nc.Block() as block:
        @block.sync
        def _(sp):
            sp.dma_start(out[0:full * P, :].rearrange("(t p) d -> p t d", p=P), m.x[:, 0:full, :]).then_inc(stored, 16)
            sp.dma_start(out[full * P:N, :], m.x[0:N - full * P, full, :]).then_inc(stored, 16)
            sp.wait_ge(stored, 32)


def program(nc, i, out, upto=99):
    m = Mem()
    m.A = nc.dram_tensor("counts", (NT, P, NP), F32, kind="Internal").ap()
    m.AT = nc.dram_tensor("counts_t", (NT, P, NP), F32, kind="Internal").ap()
    with ExitStack() as ctx:
        def sb(name, shape, dt=F32):
            return ctx.enter_context(nc.sbuf_tensor(name, shape, dt))

        m.x = sb("x_tok", [P, NT, D])
        m.xn = sb("xn_tok", [P, NT, D])
        m.xT = sb("x_feat", [P, DK, NP])
        m.o = sb("o_tok", [P, NT, D])
        m.ident, m.ones = sb("ident", [P, P]), sb("ones", [P, P])
        m.zeros16 = sb("zeros16", [P, P], F16)
        m.src_no = sb("src_no", [P, NP], F16)
        m.expert_no = sb("expert_no", [P, NT, 8])
        m.part_no = sb("part_no", [P, 1])
        m.src_col, m.dst_col = sb("src_col", [P, GC * NG]), sb("dst_col", [P, GC * NG])
        m.ranges = sb("ranges", [1, 2, NT], I32)
        m.deg, m.inv_count, m.dinv_loop, m.dinv = (sb(n, [P, NT]) for n in ("deg", "inv_count", "dinv_loop", "dinv"))
        m.dinv_row = sb("dinv_row", [P, NP])
        m.wd = sb("route_w", [P, NT, 8])
        m.pair_w = sb("pair_w", [P, 2])
        m.w1_rows, m.w2_rows = sb("w1_rows", [P, 2, DK], I32), sb("w2_rows", [P, 2, FH // P], I32)
        m.wl, m.wr, m.wg = (sb(n, [P, DK, D]) for n in ("wl_t", "wr_t", "wg_t"))

        def expert_mats(*ws):
            return [lambda e, w=w: w[ds(e, 1), :, :].rearrange("a (k p) n -> p (a k) n", p=P) for w in ws]

        def expert_bias(*bs):
            return [lambda e, b=b: b[ds(e, 1), :].rearrange("a (k p) -> p (a k)", p=P) for b in bs]

        phases = [
            lambda: phase_setup(nc, m, i["x"], i["src"], i["dst"]),
            lambda: phase_counts(nc, m),
            lambda: phase_degrees(nc, m),
            lambda: phase_transpose_weights(nc, m, [(i["L0_gnn_W_l"], m.wl), (i["L0_gnn_W_r"], m.wr), (i["L1_gnn_W"], m.wg)]),
            lambda: phase_norm(nc, m, "n0", m.x, m.xn, m.xT),
            lambda: phase_gather(nc, m, "g0", m.xn, "mean", m.wl, m.wr, i["L0_gnn_b_r"]),
            lambda: phase_norm(nc, m, "n1", m.x, m.xn, m.xT),
            lambda: phase_route(nc, m, "r0", "mean", 8, i["L0_ffn_Wr"], i["L0_ffn_br"], i["L0_ffn_b2"], m.o, m.xn),
            lambda: phase_experts(nc, m, "e0", 2, ACT.Gelu, [FH],
                                  [i["L0_ffn_W1"].rearrange("e d f -> (e d) f"), i["L0_ffn_W2"].rearrange("e f d -> (e f) d")],
                                  [i["L0_ffn_b1"].rearrange("e (f a) -> (e f) a", a=1)], m.o, picked=True),
            lambda: phase_norm(nc, m, "n2", m.o, m.o, gamma=i["L0_ffn_gamma"], beta=i["L0_ffn_beta"], finish="add"),
            lambda: phase_norm(nc, m, "n3", m.x, m.xn, m.xT, scale=m.dinv_loop),
            lambda: phase_gather(nc, m, "g1", m.xn, "loop", m.wg, bias=i["L1_gnn_b"]),
            lambda: phase_norm(nc, m, "n4", m.o, m.o, gamma=i["L1_gnn_gamma"], beta=i["L1_gnn_beta"], finish="relu_add"),
            lambda: phase_norm(nc, m, "n5", m.x, m.xn, m.xT),
            lambda: phase_route(nc, m, "r1", "mlp", 6, i["L1_ffn_router_w2"], i["L1_ffn_router_b2"], i["L1_ffn_expert_b3"],
                                m.x, m.x, i["L1_ffn_router_w1"], i["L1_ffn_router_b1"]),
            lambda: phase_experts(nc, m, "e1", 6, ACT.Relu, [256, 256],
                                  expert_mats(i["L1_ffn_expert_w1"], i["L1_ffn_expert_w2"], i["L1_ffn_expert_w3"]),
                                  expert_bias(i["L1_ffn_expert_b1"], i["L1_ffn_expert_b2"]), m.x, weight=m.wd),
            lambda: phase_norm(nc, m, "n6", m.x, m.xn, m.xT, scale=m.dinv),
            lambda: phase_gather(nc, m, "g2", m.xn, "keep"),
            lambda: phase_experts(nc, m, "e2", 2, ACT.Gelu, [FH],
                                  [lambda e: rows(i["L2_gnn_W1"][:, e * FH:(e + 1) * FH]),
                                   lambda e: rows(i["L2_gnn_W2"][e * FH:(e + 1) * FH, :])],
                                  [lambda e: per_partition(i["L2_gnn_b1"][e * FH:(e + 1) * FH])], m.x),
            lambda: phase_add_row(nc, m, "b2", i["L2_gnn_b2"]),
            lambda: phase_norm(nc, m, "n7", m.x, m.xn),
            lambda: phase_norm(nc, m, "n8", m.xn, m.o, m.xT, gamma=i["L2_ffn_gamma"], beta=i["L2_ffn_beta"]),
            lambda: phase_route(nc, m, "r2", "top", 8, i["L2_ffn_Wr"], i["L2_ffn_br"], i["L2_ffn_b2"], m.x, m.x),
            lambda: phase_experts(nc, m, "e3", 8, ACT.Gelu, [FH], expert_mats(i["L2_ffn_W1"], i["L2_ffn_W2"]),
                                  expert_bias(i["L2_ffn_b1"]), m.x, weight=m.wd),
            lambda: phase_norm(nc, m, "n9", m.x, m.xn, m.xT),
            lambda: phase_attention(nc, m, i["L3_gnn_W"], i["L3_gnn_Wl"], i["L3_gnn_Wr"], i["L3_gnn_b"]),
            lambda: phase_norm(nc, m, "n10", m.x, m.xn, m.xT),
            lambda: phase_route(nc, m, "r3", "dense", 8, i["L3_ffn_Wr"], i["L3_ffn_br"], i["L3_ffn_bo"], m.x, m.x),
            lambda: phase_experts(nc, m, "e4", 8, ACT.Relu, [256, 256],
                                  expert_mats(i["L3_ffn_W1"], i["L3_ffn_W2"], i["L3_ffn_Wo"]),
                                  [i["L3_ffn_b1"], i["L3_ffn_b2"]], m.x, weight=m.wd,
                                  bn=[tuple(i[f"L3_ffn_{v}{n}"] for v in ("g", "be", "m", "v")) for n in (1, 2)]),
        ]
        for phase in phases[:upto]:
            with nc.cleanup_on_exit():
                phase()
        phase_store(nc, m, out)


def kernel(**inputs):
    import numpy as _np
    import concourse.bacc as _bacc
    from concourse import mybir as _mybir
    from concourse.bass_utils import run_bass_kernel_spmd as _run

    nc = _bacc.Bacc("TRN2", target_bir_lowering=False, num_devices=1)
    arrays, views = {}, {}
    for name, value in inputs.items():
        a = _np.ascontiguousarray(value)
        arrays[f"in_{name}"] = a
        views[name] = nc.dram_tensor(f"in_{name}", a.shape, _mybir.dt.from_np(a.dtype), kind="ExternalInput").ap()
    out = nc.dram_tensor("out_x", (N, D), F32, kind="ExternalOutput").ap()
    program(nc, views, out)
    r = _run(nc, [arrays], core_ids=[0])
    return r.results[0]["out_x"]
```

```python
from contextlib import ExitStack

import concourse.bass as bass
from concourse import mybir

F32 = mybir.dt.float32
F16 = mybir.dt.float16
I32 = mybir.dt.int32
ALU = mybir.AluOpType
ACT = mybir.ActivationFunctionType
AX = mybir.AxisListType

P = 128
N = 2500
D = 256
DK = D // P
NT = -(-N // P)
NP = NT * P
BLK = 512
NB = NP // BLK
TB = BLK // P
E = 80000
GC = 5
NG = E // (GC * P)
HALF = NP // 2
FH = 512
EPS = 1e-5
EXP_TOP = 88.7
BIG = 3.0e38
ds = bass.ds


class Steps:

    def __init__(self, eng, sem, base=0):
        self.eng, self.sem, self.n = eng, sem, base

    def step(self, ins):
        ins.then_inc(self.sem, 1)
        self.n = self.n + 1

    def join(self, ins):
        self.step(ins)
        self.eng.wait_ge(self.sem, self.n)


class Mem:
    pass


def rows(ap):
    return ap.rearrange("(k p) n -> p k n", p=P)


def per_partition(ap):
    return ap.rearrange("(k p) -> p k", p=P)



def phase_setup(nc, m, x, src, dst):
    sem = nc.alloc_semaphore
    main_in, tail_in, edges_in = sem("main_in"), sem("tail_in"), sem("edges_in")
    tail_zeroed, made, dve_own = sem("tail_zeroed"), sem("consts_made"), sem("setup_dve")
    turned, turned_rng, turned_row = sem("edges_turned"), sem("range_turned"), sem("range_row")
    full = N // P
    with (
        nc.sbuf_tensor("edge_i", [P, 2, GC * P], I32) as edge_i,
        nc.sbuf_tensor("edge_f", [P, 2, GC * P], F32) as edge_f,
        nc.sbuf_tensor("bounds", [P, 2, NT], F32) as bounds,
        nc.sbuf_tensor("tile_low", [P, 2], F32) as tile_low,
        nc.sbuf_tensor("group_no", [P, 2, NG], F32) as group_no,
        nc.sbuf_tensor("bounds_row", [P, 2, NG], F32) as bounds_row,
        nc.sbuf_tensor("touch", [P, 3, NG], F32) as touch,
        nc.sbuf_tensor("ends", [P, 4], F32) as ends,
        nc.psum_tensor("turn_ps", [P, 4, 4, P], F32) as ps,
        nc.Block() as block,
    ):
        @block.sync
        def _(sp):
            sp.dma_start(edge_i[0:NG, 0, :], src.rearrange("(p e) -> p e", p=NG)).then_inc(edges_in, 16)
            sp.dma_start(edge_i[0:NG, 1, :], dst.rearrange("(p e) -> p e", p=NG)).then_inc(edges_in, 16)
            sp.dma_start(m.x[:, 0:full, :], x[0:full * P, :].rearrange("(t p) d -> p t d", p=P)).then_inc(main_in, 16)
            sp.wait_ge(tail_zeroed, 1)
            sp.dma_start(m.x[0:N - full * P, full, :], x[full * P:N, :]).then_inc(tail_in, 16)
            sp.wait_ge(main_in, 16)
            sp.wait_ge(tail_in, 16)

        @block.gpsimd
        def _(pool):
            own = Steps(pool, made)
            pool.memset(m.x[:, full, :], 0.0).then_inc(tail_zeroed, 1)
            own.step(pool.memset(m.ones[:, :], 1.0))
            own.join(pool.memset(m.ident[:, :], 0.0))
            own.join(pool.affine_select(out=m.ident[:, :], in_=m.ident[:, :], compare_op=ALU.not_equal, fill=1.0,
                                        base=0, pattern=[[-1, P]], channel_multiplier=1))
            own.step(pool.iota(m.src_no[:, :], pattern=[[1, NP]], base=-HALF, channel_multiplier=0,
                               allow_small_or_imprecise_dtypes=True))
            own.step(pool.iota(m.expert_no[:, :, :], pattern=[[0, NT], [1, 8]], base=-8, channel_multiplier=0,
                               allow_small_or_imprecise_dtypes=True))
            own.step(pool.iota(m.part_no[:, :], pattern=[[0, 1]], base=0, channel_multiplier=1,
                               allow_small_or_imprecise_dtypes=True))
            own.step(pool.iota(tile_low[:, 0:1], pattern=[[0, 1]], base=0, channel_multiplier=P,
                               allow_small_or_imprecise_dtypes=True))
            own.step(pool.iota(tile_low[:, 1:2], pattern=[[0, 1]], base=P, channel_multiplier=P,
                               allow_small_or_imprecise_dtypes=True))
            own.step(pool.iota(group_no[:, 0, :], pattern=[[1, NG]], base=-NG, channel_multiplier=0,
                               allow_small_or_imprecise_dtypes=True))
            own.step(pool.iota(group_no[:, 1, :], pattern=[[1, NG]], base=1, channel_multiplier=0,
                               allow_small_or_imprecise_dtypes=True))

        @block.vector
        def _(dve):
            own = Steps(dve, dve_own)
            dve.wait_ge(edges_in, 32)
            dve.memset(m.zeros16[:, :], 0.0)
            own.step(dve.tensor_scalar(edge_f[0:NG, 0, :], edge_i[0:NG, 0, :], -float(HALF), None, ALU.add))
            own.join(dve.tensor_copy(edge_f[0:NG, 1, :], edge_i[0:NG, 1, :]))
            own.step(dve.tensor_reduce(ends[0:NG, 0:1], edge_f[0:NG, 1, :], AX.X, ALU.min))
            own.join(dve.tensor_reduce(ends[0:NG, 1:2], edge_f[0:NG, 1, :], AX.X, ALU.max))
            own.join(dve.tensor_copy(bounds[0:NG, :, :], ends[0:NG, 0:2].unsqueeze(2).to_broadcast([NG, 2, NT])))
            dve.wait_ge(turned, 2 * GC)
            for i, col in enumerate((m.src_col, m.dst_col)):
                for k in range(GC):
                    n = i * GC + k
                    own.step(dve.tensor_copy(col[:, k:k + GC * (NG - 1) + 1:GC], ps[:, n // 4, n % 4, 0:NG]))
            dve.wait_ge(turned_rng, 2)
            dve.wait_ge(made, 10)
            own.join(dve.tensor_copy(bounds_row[0:NT, :, :], ps[0:NT, 3, 0:2, 0:NG]))
            own.step(dve.tensor_scalar(touch[0:NT, 0, :], bounds_row[0:NT, 0, :], tile_low[0:NT, 1:2], None, ALU.is_lt))
            own.join(dve.tensor_scalar(touch[0:NT, 1, :], bounds_row[0:NT, 1, :], tile_low[0:NT, 0:1], None, ALU.is_ge))
            own.join(dve.tensor_tensor(touch[0:NT, 0, :], touch[0:NT, 0, :], touch[0:NT, 1, :], ALU.mult))
            own.step(dve.tensor_tensor(touch[0:NT, 1, :], touch[0:NT, 0, :], group_no[0:NT, 0, :], ALU.mult))
            own.join(dve.tensor_tensor(touch[0:NT, 2, :], touch[0:NT, 0, :], group_no[0:NT, 1, :], ALU.mult))
            own.step(dve.tensor_reduce(ends[0:NT, 0:1], touch[0:NT, 1, :], AX.X, ALU.min))
            own.join(dve.tensor_reduce(ends[0:NT, 1:2], touch[0:NT, 2, :], AX.X, ALU.max))
            own.join(dve.tensor_scalar(ends[0:NT, 2:3], ends[0:NT, 0:1], float(NG), float(NG - 1), ALU.add, ALU.min))
            own.join(dve.tensor_scalar(ends[0:NT, 3:4], ends[0:NT, 2:3], 1.0, ends[0:NT, 1:2], ALU.add, ALU.max))
            dve.wait_ge(turned_row, 2)
            own.join(dve.tensor_copy(m.ranges[0:1, :, :], ps[0:1, 3, 2:4, 0:NT]))

        @block.tensor
        def _(pe):
            pe.wait_ge(made, 3)
            pe.wait_ge(dve_own, 2)
            for i in range(2):
                for k in range(GC):
                    n = i * GC + k
                    pe.transpose(ps[:, n // 4, n % 4, 0:NG], edge_f[0:NG, i, k * P:(k + 1) * P],
                                 m.ident[0:NG, 0:NG]).then_inc(turned, 1)
            pe.wait_ge(dve_own, 5)
            for i in range(2):
                pe.transpose(ps[0:NT, 3, i, 0:NG], bounds[0:NG, i, :], m.ident[0:NG, 0:NG]).then_inc(turned_rng, 1)
            pe.wait_ge(dve_own, 15 + 10)
            for i in range(2):
                pe.transpose(ps[0:1, 3, 2 + i, 0:NT], ends[0:NT, 2 + i:3 + i], m.ident[0:NT, 0:NT]).then_inc(turned_row, 1)



def phase_counts(nc, m):
    sem = nc.alloc_semaphore
    built, slot_free, summed = sem("onehots_built"), sem("onehots_used"), sem("counts_summed")
    row_out, turned, turned_out = sem("counts_copied"), sem("counts_turned"), sem("turned_copied")
    row_stored, turned_stored, moved = sem("counts_stored"), sem("turned_stored"), sem("dst_moved")
    with (
        nc.sbuf_tensor("hot_dst", [P, GC, P], F16) as hot_dst,
        nc.sbuf_tensor("hot_src", [P, GC, NP], F16) as hot_src,
        nc.sbuf_tensor("count_row", [P, NP], F32) as count_row,
        nc.sbuf_tensor("count_turn", [P, NT, P], F32) as count_turn,
        nc.psum_tensor("count_ps", [P, NB, BLK], F32) as acc,
        nc.psum_tensor("cturn_ps", [P, 3, TB, P], F32) as tps,
        nc.Block() as block,
    ):
        dst_no = m.src_no[:, HALF:HALF + P]

        @block.vector
        def _(dve):
            used = dve.alloc_register("groups_built")
            dve.reg_mov(used, 0)
            with dve.Fori(0, NT) as t:
                first = dve.value_load(m.ranges[0:1, 0, ds(t, 1)], min_val=0, max_val=NG - 1)
                last = dve.value_load(m.ranges[0:1, 1, ds(t, 1)], min_val=1, max_val=NG)
                with dve.Fori(first, last) as g:
                    n = dve.snap(used)
                    for j in range(GC):
                        dve.wait_ge(slot_free, n * GC + (j + 1))
                        dve.tensor_scalar(hot_dst[:, j, :], dst_no, m.dst_col[:, ds(g * GC + j, 1)], None, ALU.is_equal)
                        dve.tensor_scalar(hot_src[:, j, :], m.src_no[:, :], m.src_col[:, ds(g * GC + j, 1)], None,
                                          ALU.is_equal).then_inc(built, 1)
                    dve.reg_add(used, used, 1)
                dve.wait_ge(built, dve.snap(used) * GC)
                dve.tensor_scalar(m.dst_col[:, :], m.dst_col[:, :], -float(P), None, ALU.add).then_inc(moved, 1)
                dve.wait_ge(moved, t + 1)

        @block.tensor
        def _(pe):
            used = pe.alloc_register("groups_used")
            pe.reg_mov(used, 0)
            pe.sem_inc(slot_free, GC)
            with pe.Fori(0, NT) as t:
                pe.wait_ge(row_out, t + 1)
                for b in range(NB):
                    pe.matmul(acc[:, b, :], m.zeros16[:, :], m.src_no[:, b * BLK:(b + 1) * BLK],
                              start=True, stop=False, skip_group_check=True)
                first = pe.value_load(m.ranges[0:1, 0, ds(t, 1)], min_val=0, max_val=NG - 1)
                last = pe.value_load(m.ranges[0:1, 1, ds(t, 1)], min_val=1, max_val=NG)
                with pe.Fori(first, last) as g:
                    n = pe.snap(used)
                    for j in range(GC):
                        pe.wait_ge(built, n * GC + (j + 1))
                        for b in range(NB):
                            mm = pe.matmul(acc[:, b, :], hot_dst[:, j, :], hot_src[:, j, b * BLK:(b + 1) * BLK],
                                           start=False, stop=False, skip_group_check=True)
                        mm.then_inc(slot_free, 1)
                    pe.reg_add(used, used, 1)
                for b in range(NB):
                    mm = pe.matmul(acc[:, b, :], m.zeros16[:, :], m.src_no[:, b * BLK:(b + 1) * BLK],
                                   start=False, stop=True, skip_group_check=True)
                mm.then_inc(summed, 1)
                pe.wait_ge(row_out, t + 2)
                for b in range(NB):
                    pe.wait_ge(turned_out, t * NB + max(1, b - 1))
                    for q in range(TB):
                        s = b * TB + q
                        mm = pe.transpose(tps[:, b % 3, q, :], count_row[:, s * P:(s + 1) * P], m.ident[:, :])
                    mm.then_inc(turned, 1)

        @block.scalar
        def _(act):
            act.sem_inc(row_out, 1)
            act.sem_inc(turned_out, 1)
            with act.Fori(0, NT) as t:
                act.wait_ge(summed, t + 1)
                act.activation(count_row[:, :], acc[:, :, :].rearrange("p b n -> p (b n)"), ACT.Copy,
                               accum_out=m.deg[:, ds(t, 1)]).then_inc(row_out, 1)
                for b in range(NB):
                    act.wait_ge(turned, t * NB + (b + 1))
                    act.activation(count_turn[:, b * TB:(b + 1) * TB, :], tps[:, b % 3, :, :], ACT.Copy).then_inc(turned_out, 1)
                act.wait_ge(row_stored, t * 16 + 16)
                act.wait_ge(turned_stored, t * 16 + 16)

        @block.sync
        def _(sp):
            with sp.Fori(0, NT) as t:
                sp.wait_ge(row_out, t + 2)
                sp.dma_start(m.A[ds(t, 1), :, :].rearrange("a p n -> (a p) n"), count_row[:, :]).then_inc(row_stored, 16)
                sp.wait_ge(turned_out, (t + 1) * NB + 1)
                sp.dma_start(m.AT[ds(t, 1), :, :].rearrange("a p n -> (a p) n"),
                             count_turn[:, :, :].rearrange("p s n -> p (s n)")).then_inc(turned_stored, 16)
            sp.wait_ge(row_stored, NT * 16)
            sp.wait_ge(turned_stored, NT * 16)



def stats_steps(own, dve, st, mean, var, tmp):
    own.step(dve.tensor_tensor(mean, st[:, :, 1], st[:, :, 4], ALU.add))
    own.step(dve.tensor_tensor(tmp, st[:, :, 1], st[:, :, 4], ALU.subtract))
    own.join(dve.tensor_tensor(var, st[:, :, 2], st[:, :, 5], ALU.add))
    own.step(dve.tensor_scalar(mean, mean, 0.5, None, ALU.mult))
    own.step(dve.tensor_scalar(var, var, 1.0 / D, EPS, ALU.mult, ALU.add))
    own.join(dve.tensor_tensor(tmp, tmp, tmp, ALU.mult))
    own.join(dve.scalar_tensor_tensor(var, tmp, 0.25, var, ALU.mult, ALU.add))


def phase_norm(nc, m, name, src, out, outT=None, gamma=None, beta=None, scale=None, finish=None):
    sem = nc.alloc_semaphore
    dve_own, want_root, root, ready = (sem(f"{name}_{s}") for s in ("dve", "want_root", "root", "ready"))
    turned, turned_out, affine_in = (sem(f"{name}_{s}") for s in ("turned", "turned_out", "affine_in"))
    with (
        nc.sbuf_tensor(f"{name}_st", [P, NT, 6], F32) as st,
        nc.sbuf_tensor(f"{name}_mean", [P, NT], F32) as mean,
        nc.sbuf_tensor(f"{name}_var", [P, NT], F32) as var,
        nc.sbuf_tensor(f"{name}_tmp", [P, NT], F32) as tmp,
        nc.sbuf_tensor(f"{name}_gb", [P, 2, D], F32) as gb,
        nc.psum_tensor(f"{name}_ps", [P, 4, TB, P], F32) as ps,
        nc.Block() as block,
    ):
        @block.sync
        def _(sp):
            if gamma is not None:
                sp.dma_start(gb[:, 0, :], gamma.partition_broadcast(P)).then_inc(affine_in, 16)
                sp.dma_start(gb[:, 1, :], beta.partition_broadcast(P)).then_inc(affine_in, 16)

        @block.vector
        def _(dve):
            own = Steps(dve, dve_own)
            with dve.Fori(0, NT) as t:
                dve.bn_stats(st[:, ds(t, 1), :].rearrange("p a s -> p (a s)"),
                             src[:, ds(t, 1), :].rearrange("p a d -> p (a d)")).then_inc(dve_own, 1)
            own.n = NT
            dve.wait_ge(dve_own, NT)
            stats_steps(own, dve, st, mean[:, :], var[:, :], tmp[:, :])
            dve.tensor_copy(var[:, :], var[:, :]).then_inc(want_root, 1)
            dve.wait_ge(root, 1)
            own.join(dve.reciprocal(tmp[:, :], var[:, :]))
            if gamma is not None:
                dve.wait_ge(affine_in, 32)
            for t in range(NT):
                if t:
                    pass
                if gamma is None:
                    dve.tensor_scalar(out[:, t, :], src[:, t, :], mean[:, t:t + 1], tmp[:, t:t + 1],
                                      ALU.subtract, ALU.mult).then_inc(ready, 1)
                    continue
                own.join(dve.tensor_scalar(out[:, t, :], src[:, t, :], mean[:, t:t + 1], tmp[:, t:t + 1],
                                           ALU.subtract, ALU.mult))
                own.join(dve.tensor_tensor(out[:, t, :], out[:, t, :], gb[:, 0, :], ALU.mult))
                last = dve.tensor_tensor(out[:, t, :], out[:, t, :], gb[:, 1, :], ALU.add)
                if finish:
                    own.join(last)
                    if finish == "relu_add":
                        last = dve.scalar_tensor_tensor(m.x[:, t, :], out[:, t, :], 0.0, m.x[:, t, :], ALU.max, ALU.add)
                    else:
                        last = dve.tensor_tensor(m.x[:, t, :], out[:, t, :], m.x[:, t, :], ALU.add)
                last.then_inc(ready, 1)
            if scale is not None:
                dve.wait_ge(turned, NB * DK)
                for t in range(NT):
                    dve.tensor_scalar(out[:, t, :], out[:, t, :], scale[:, t:t + 1], None, ALU.mult)

        @block.scalar
        def _(act):
            act.wait_ge(want_root, 1)
            act.activation(var[:, :], var[:, :], ACT.Sqrt).then_inc(root, 1)
            if outT is not None:
                for b in range(NB):
                    for k in range(DK):
                        n = b * DK + k
                        act.wait_ge(turned, n + 1)
                        act.activation(outT[:, k, b * BLK:(b + 1) * BLK],
                                       ps[:, n % 4, :, :].rearrange("p q n -> p (q n)"), ACT.Copy).then_inc(turned_out, 1)

        @block.tensor
        def _(pe):
            if outT is not None:
                for b in range(NB):
                    pe.wait_ge(ready, (b + 1) * TB)
                    for k in range(DK):
                        n = b * DK + k
                        if n >= 4:
                            pe.wait_ge(turned_out, n - 3)
                        for q in range(TB):
                            mm = pe.transpose(ps[:, n % 4, q, :], out[:, b * TB + q, k * P:(k + 1) * P], m.ident[:, :])
                        mm.then_inc(turned, 1)



def phase_degrees(nc, m):
    sem = nc.alloc_semaphore
    dve_own, root, spread, diag, copied = (sem(f"deg_{s}") for s in ("dve", "root", "spread", "diag", "copied"))
    with (
        nc.sbuf_tensor("deg_t", [P, 4, NT], F32) as t4,
        nc.sbuf_tensor("deg_diag", [P, 2, TB, P], F32) as dg,
        nc.psum_tensor("deg_ps", [P, 2, BLK], F32) as ps,
        nc.Block() as block,
    ):
        @block.vector
        def _(dve):
            own = Steps(dve, dve_own)
            own.step(dve.tensor_scalar(t4[:, 0, :], m.deg[:, :], 1.0, None, ALU.max))
            own.step(dve.tensor_scalar(t4[:, 1, :], m.deg[:, :], 1.0, None, ALU.add))
            own.step(dve.tensor_scalar(t4[:, 2, :], m.deg[:, :], 1e-12, None, ALU.max))
            own.join(dve.tensor_scalar(t4[:, 3, :], m.deg[:, :], 0.0, None, ALU.is_gt))
            own.step(dve.reciprocal(m.inv_count[:, :], t4[:, 0, :]))
            dve.wait_ge(root, 1)
            own.step(dve.reciprocal(m.dinv_loop[:, :], t4[:, 1, :]))
            own.join(dve.reciprocal(t4[:, 2, :], t4[:, 2, :]))
            own.join(dve.tensor_tensor(m.dinv[:, :], t4[:, 2, :], t4[:, 3, :], ALU.mult))
            for b in range(NB):
                if b >= 2:
                    dve.wait_ge(spread, b - 1)
                for q in range(TB):
                    t = b * TB + q
                    ins = dve.tensor_scalar(dg[:, b % 2, q, :], m.ident[:, :], m.dinv[:, t:t + 1], None, ALU.mult)
                ins.then_inc(diag, 1)

        @block.scalar
        def _(act):
            act.wait_ge(dve_own, 4)
            act.activation(t4[:, 1:3, :], t4[:, 1:3, :], ACT.Sqrt).then_inc(root, 1)
            for b in range(NB):
                act.wait_ge(spread, b + 1)
                act.activation(m.dinv_row[:, b * BLK:(b + 1) * BLK], ps[:, b % 2, :], ACT.Copy).then_inc(copied, 1)

        @block.tensor
        def _(pe):
            for b in range(NB):
                pe.wait_ge(diag, b + 1)
                if b >= 2:
                    pe.wait_ge(copied, b - 1)
                pe.matmul(ps[:, b % 2, :], m.ones[:, :], dg[:, b % 2, :, :].rearrange("p q n -> p (q n)"),
                          start=True, stop=True).then_inc(spread, 1)


def phase_transpose_weights(nc, m, mats):
    sem = nc.alloc_semaphore
    loaded, turned, copied = (sem(f"wturn_{s}") for s in ("loaded", "turned", "copied"))
    with (
        nc.sbuf_tensor("wturn_in", [P, len(mats), DK, D], F32) as w_in,
        nc.psum_tensor("wturn_ps", [P, 2, DK, D], F32) as ps,
        nc.Block() as block,
    ):
        @block.sync
        def _(sp):
            for i, (w, _o) in enumerate(mats):
                sp.dma_start(w_in[:, i, :, :], rows(w)).then_inc(loaded, 16)

        @block.tensor
        def _(pe):
            pe.wait_ge(loaded, 16 * len(mats))
            for i in range(len(mats)):
                if i >= 2:
                    pe.wait_ge(copied, i - 1)
                for ko in range(DK):
                    for ki in range(DK):
                        mm = pe.transpose(ps[:, i % 2, ki, ko * P:(ko + 1) * P], w_in[:, i, ko, ki * P:(ki + 1) * P],
                                          m.ident[:, :])
                mm.then_inc(turned, 1)

        @block.vector
        def _(dve):
            for i, (_w, out_sb) in enumerate(mats):
                dve.wait_ge(turned, i + 1)
                dve.tensor_copy(out_sb[:, :, :], ps[:, i % 2, :, :]).then_inc(copied, 1)


def phase_gather(nc, m, name, y, kind, w=None, w_self=None, bias=None):
    sem = nc.alloc_semaphore
    at_in = [sem(f"{name}_at_in{i}") for i in range(2)]
    agg_mm, agg_out, lin_mm, lin_out, bias_in, looped, selfed = (
        sem(f"{name}_{s}") for s in ("agg_mm", "agg_out", "lin_mm", "lin_out", "bias_in", "looped", "selfed"))
    with (
        nc.sbuf_tensor(f"{name}_at", [P, 2, TB, NT, P], F32) as at,
        nc.sbuf_tensor(f"{name}_agg", [P, DK, BLK], F32) as agg,
        nc.sbuf_tensor(f"{name}_self", [P, DK, BLK], F32) as own_x,
        nc.sbuf_tensor(f"{name}_bias", [P, D], F32) as bias_sb,
        nc.psum_tensor(f"{name}_ps", [P, DK, BLK], F32) as ps,
        nc.psum_tensor(f"{name}_lin", [P, TB, D], F32) as lin,
        nc.psum_tensor(f"{name}_lin2", [P, TB, D], F32) as lin2,
        nc.Block() as block,
    ):
        @block.sync
        def _(sp):
            if bias is not None:
                sp.dma_start(bias_sb[:, :], bias.partition_broadcast(P)).then_inc(bias_in, 16)
            for b in range(NB):
                if b >= 2:
                    sp.wait_ge(agg_mm, b - 1)
                sp.dma_start(at[:, b % 2, :, :, :].rearrange("p q s n -> p q (s n)"),
                             m.AT[b * TB:(b + 1) * TB, :, :].rearrange("t p n -> p t n")).then_inc(at_in[b % 2], 16)

        @block.gpsimd
        def _(pool):
            if kind == "loop":
                for b in range(NB):
                    pool.wait_ge(at_in[b % 2], 16 * (b // 2 + 1))
                    for q in range(TB):
                        spot = at[:, b % 2, q, b * TB + q, :]
                        pool.tensor_tensor(spot, spot, m.ident[:, :], ALU.add).then_inc(looped, 1)

        @block.tensor
        def _(pe):
            for b in range(NB):
                pe.wait_ge(at_in[b % 2], 16 * (b // 2 + 1))
                if kind == "loop":
                    pe.wait_ge(looped, TB * (b + 1))
                pe.wait_ge(agg_out, b)
                for k in range(DK):
                    for s in range(NT):
                        mm = pe.matmul(ps[:, k, :], y[:, s, k * P:(k + 1) * P], at[:, b % 2, :, s, :],
                                       start=(s == 0), stop=(s == NT - 1))
                mm.then_inc(agg_mm, 1)
                if kind == "keep":
                    continue
                pe.wait_ge(lin_out, b)
                if kind == "mean":
                    pe.wait_ge(selfed, b + 1)
                    for q in range(TB):
                        for k in range(DK):
                            pe.matmul(lin2[:, q, :], own_x[:, k, q * P:(q + 1) * P], w_self[:, k, :],
                                      start=(k == 0), stop=(k == DK - 1))
                pe.wait_ge(agg_out, b + 1)
                for q in range(TB):
                    for k in range(DK):
                        mm = pe.matmul(lin[:, q, :], agg[:, k, q * P:(q + 1) * P], w[:, k, :],
                                       start=(k == 0), stop=(k == DK - 1))
                mm.then_inc(lin_mm, 1)

        @block.scalar
        def _(act):
            if kind == "keep":
                return
            for b in range(NB):
                act.wait_ge(lin_mm, b)
                if kind == "mean":
                    act.activation(own_x[:, :, :], m.xT[:, :, b * BLK:(b + 1) * BLK], ACT.Copy).then_inc(selfed, 1)
                act.wait_ge(agg_mm, b + 1)
                act.activation(agg[:, :, :], ps[:, :, :], ACT.Copy).then_inc(agg_out, 1)

        @block.vector
        def _(dve):
            if bias is not None:
                dve.wait_ge(bias_in, 16)
            own = Steps(dve, sem(f"{name}_dve"))
            for b in range(NB):
                if kind == "keep":
                    dve.wait_ge(agg_mm, b + 1)
                    cut = slice(b * BLK, (b + 1) * BLK)
                    dve.tensor_tensor(m.xT[:, :, cut], ps[:, :, :],
                                      m.dinv_row[:, cut].unsqueeze(1).to_broadcast([P, DK, BLK]), ALU.mult).then_inc(agg_out, 1)
                    continue
                dve.wait_ge(lin_mm, b + 1)
                for q in range(TB):
                    t = b * TB + q
                    if kind == "mean":
                        own.join(dve.scalar_tensor_tensor(m.x[:, t, :], lin[:, q, :], m.inv_count[:, t:t + 1],
                                                          m.x[:, t, :], ALU.mult, ALU.add))
                        own.join(dve.tensor_tensor(m.x[:, t, :], lin2[:, q, :], m.x[:, t, :], ALU.add))
                        ins = dve.tensor_tensor(m.x[:, t, :], m.x[:, t, :], bias_sb[:, :], ALU.add)
                    else:
                        ins = dve.scalar_tensor_tensor(m.o[:, t, :], lin[:, q, :], m.dinv_loop[:, t:t + 1],
                                                       bias_sb[:, :], ALU.mult, ALU.add)
                ins.then_inc(lin_out, 1)



def softmax_steps(own, dve, exp, lg, top, tmp, T, EX):
    def wide(a):
        return a.unsqueeze(2).to_broadcast([P, T, EX])
    own.join(dve.tensor_reduce(top, lg, AX.X, ALU.max))
    own.join(dve.tensor_tensor(lg, lg, wide(top), ALU.subtract))
    exp()
    own.join(dve.tensor_reduce(tmp, lg, AX.X, ALU.add))
    own.join(dve.reciprocal(tmp, tmp))
    own.join(dve.tensor_tensor(lg, lg, wide(tmp), ALU.mult))


def top2_steps(own, dve, exp, lg, s, no, wd, T, EX):
    def wide(a):
        return a.unsqueeze(2).to_broadcast([P, T, EX])

    def pick(vals, top, at, hot):
        own.join(dve.tensor_reduce(top, vals, AX.X, ALU.max))
        own.join(dve.tensor_tensor(hot, vals, wide(top), ALU.is_equal))
        own.join(dve.tensor_tensor(hot, hot, no, ALU.mult))
        own.join(dve.tensor_reduce(at, hot, AX.X, ALU.min))
        own.join(dve.tensor_tensor(hot, no, wide(at), ALU.is_equal))

    pick(lg, s.m1, s.i1, s.hot1)
    own.join(dve.scalar_tensor_tensor(s.rest, s.hot1, -BIG, lg, ALU.mult, ALU.add))
    pick(s.rest, s.m2, s.i2, s.hot2)
    own.join(dve.tensor_tensor(s.d, s.m2, s.m1, ALU.subtract))
    exp()
    own.join(dve.tensor_scalar(s.w1, s.d, 1.0, None, ALU.add))
    own.join(dve.reciprocal(s.w1, s.w1))
    own.join(dve.tensor_tensor(s.w2, s.w1, s.d, ALU.mult))
    own.join(dve.tensor_tensor(s.hot1, s.hot1, wide(s.w1), ALU.mult))
    own.join(dve.tensor_tensor(s.hot2, s.hot2, wide(s.w2), ALU.mult))
    own.join(dve.tensor_tensor(wd, s.hot1, s.hot2, ALU.add))


def phase_route(nc, m, name, kind, EX, wr, br, bout, dest, base, wr1=None, br1=None):
    sem = nc.alloc_semaphore
    T = 1 if kind == "mean" else NT
    loaded, dve_own, act_own, want_exp, exped, pe_own, pe_hid, act_hid, w_ready, mixed, added, w_turned = (
        sem(f"{name}_{s}") for s in ("loaded", "dve", "act", "want_exp", "exped", "pe", "pe_hid", "act_hid",
                                     "w_ready", "mixed", "added", "w_turned"))
    KR = 1 if kind == "mlp" else DK
    s = Mem()
    with ExitStack() as ctx:
        sb = lambda n, shape, dt=F32: ctx.enter_context(nc.sbuf_tensor(f"{name}_{n}", shape, dt))
        wr_sb = sb("wr", [P, KR, EX])
        br_sb = sb("br", [P, EX])
        bo_sb = sb("bo", [P, D])
        lg = sb("lg", [P, T, EX])
        s.m1, s.i1, s.m2, s.i2, s.d, s.w1, s.w2, s.tmp = (
            sb(n, [P, T])[:, :] for n in ("m1", "i1", "m2", "i2", "d", "w1", "w2", "tmp"))
        s.hot1, s.hot2, s.rest = (sb(n, [P, T, EX])[:, :, :] for n in ("hot1", "hot2", "rest"))
        wT = sb("wT", [P, NT, P])
        mean = sb("mean", [P, DK])
        mean_w = sb("mean_w", [P, DK, P])
        w1_sb = sb("w_hid", [P, DK, P])
        b1_sb = sb("b_hid", [P, 1])
        hid = sb("hid", [P, NP]) if kind == "mlp" else None
        psl = ctx.enter_context(nc.psum_tensor(f"{name}_psl", [P, NT, EX], F32))
        psh = ctx.enter_context(nc.psum_tensor(f"{name}_psh", [P, 2, BLK], F32))
        pst = ctx.enter_context(nc.psum_tensor(f"{name}_pst", [P, 2, TB, P], F32))
        psm = ctx.enter_context(nc.psum_tensor(f"{name}_psm", [P, 2, BLK], F32))
        block = ctx.enter_context(nc.Block())
        nload = 5 if kind == "mlp" else 3
        no = m.expert_no[:, 0:T, 0:EX]

        @block.sync
        def _(sp):
            sp.dma_start(wr_sb[:, :, :], rows(wr)).then_inc(loaded, 16)
            sp.dma_start(br_sb[:, :], br.partition_broadcast(P)).then_inc(loaded, 16)
            sp.dma_start(bo_sb[0:EX, :], bout).then_inc(loaded, 16)
            if kind == "mlp":
                sp.dma_start(w1_sb[:, :, :], rows(wr1)).then_inc(loaded, 16)
                sp.dma_start(b1_sb[:, :], per_partition(br1), allow_slow_non_contiguous=True).then_inc(loaded, 16)

        @block.tensor
        def _(pe):
            pe.wait_ge(loaded, 16 * nload)
            if kind == "mean":
                pe.wait_ge(w_ready, 1)
                for k in range(DK):
                    mm = pe.matmul(psl[:, 0, :], mean_w[:, k, :], wr_sb[:, k, :], start=(k == 0), stop=(k == DK - 1))
                mm.then_inc(pe_own, 1)
            elif kind == "mlp":
                for b in range(NB):
                    if b >= 2:
                        pe.wait_ge(act_hid, b - 1)
                    for k in range(DK):
                        mm = pe.matmul(psh[:, b % 2, :], w1_sb[:, k, :], m.xT[:, k, b * BLK:(b + 1) * BLK],
                                       start=(k == 0), stop=(k == DK - 1))
                    mm.then_inc(pe_hid, 1)
                for t in range(NT):
                    pe.wait_ge(act_hid, t // TB + 1)
                    mm = pe.matmul(psl[:, t, :], hid[:, t * P:(t + 1) * P], wr_sb[:, 0, :], start=True, stop=True)
                mm.then_inc(pe_own, 1)
            else:
                for t in range(NT):
                    for k in range(DK):
                        mm = pe.matmul(psl[:, t, :], m.xT[:, k, t * P:(t + 1) * P], wr_sb[:, k, :],
                                       start=(k == 0), stop=(k == DK - 1))
                mm.then_inc(pe_own, 1)
            pe.wait_ge(w_ready, 2 if kind == "mean" else 1)
            for b in range(NB):
                if b >= 2:
                    pe.wait_ge(w_turned, b - 1)
                for q in range(TB):
                    mm = pe.transpose(pst[0:EX, b % 2, q, :], m.wd[:, b * TB + q, 0:EX], m.ident[:, :])
                mm.then_inc(pe_own, 1)
            for t in range(NT):
                pe.wait_ge(w_turned, t // TB + 1)
                if t >= 2:
                    pe.wait_ge(added, t - 1)
                pe.matmul(psm[:, t % 2, 0:D], wT[0:EX, t, :], bo_sb[0:EX, :], start=True, stop=True).then_inc(mixed, 1)

        @block.scalar
        def _(act):
            if kind == "mlp":
                act.wait_ge(loaded, 16 * nload)
                for b in range(NB):
                    act.wait_ge(pe_hid, b + 1)
                    act.activation(hid[:, b * BLK:(b + 1) * BLK], psh[:, b % 2, :], ACT.Relu,
                                   bias=b1_sb[:, 0:1]).then_inc(act_hid, 1)
            exps = {"mean": [lg, lg, s.d], "mlp": [lg, s.d], "top": [s.d], "dense": [lg]}[kind]
            for i, what in enumerate(exps):
                ap = what if what is s.d else lg[:, :, :]
                act.wait_ge(want_exp, i + 1)
                act.activation(ap, ap, ACT.Exp).then_inc(exped, 1)
            for b in range(NB):
                act.wait_ge(pe_own, 1 + b + 1)
                act.activation(wT[0:EX, b * TB:(b + 1) * TB, :], pst[0:EX, b % 2, :, :], ACT.Copy).then_inc(w_turned, 1)

        @block.vector
        def _(dve):
            own = Steps(dve, dve_own)
            asked = [0]

            def exp():
                dve.sem_inc(want_exp, 1)
                asked[0] += 1
                dve.wait_ge(exped, asked[0])

            L = lg[:, :, :]
            if kind == "mean":
                for k in range(DK):
                    own.join(dve.tensor_reduce(mean[:, k:k + 1], m.xT[:, k, 0:N], AX.X, ALU.add))
                own.join(dve.tensor_scalar(mean[:, :], mean[:, :], 1.0 / N, None, ALU.mult))
                own.join(dve.tensor_copy(mean_w[:, :, :], mean[:, :].unsqueeze(2).to_broadcast([P, DK, P])))
                dve.sem_inc(w_ready, 1)
            dve.wait_ge(loaded, 16 * nload)
            dve.wait_ge(pe_own, 1)
            own.join(dve.tensor_tensor(L, psl[:, 0:T, :], br_sb[:, :].unsqueeze(1).to_broadcast([P, T, EX]), ALU.add))
            if kind != "top":
                softmax_steps(own, dve, exp, L, s.m1, s.tmp, T, EX)
            if kind == "mean":
                capacity = float(-(-N * 5 // (4 * EX)))
                own.join(dve.tensor_scalar(s.rest, L, float(N), None, ALU.mult))
                own.join(dve.reciprocal(s.rest, s.rest))
                own.join(dve.tensor_scalar(s.rest, s.rest, capacity, 1.0, ALU.mult, ALU.min))
                own.join(dve.tensor_tensor(L, L, s.rest, ALU.mult))
                softmax_steps(own, dve, exp, L, s.m1, s.tmp, T, EX)
            wd = m.wd[:, 0:T, 0:EX]
            if kind == "dense":
                own.join(dve.tensor_copy(wd, L))
            else:
                top2_steps(own, dve, exp, L, s, no, wd, T, EX)
            if kind == "mean":
                own.join(dve.tensor_copy(m.wd[:, 1:NT, 0:EX], m.wd[:, 0:1, 0:EX].to_broadcast([P, NT - 1, EX])))
                own.step(dve.tensor_copy(m.pair_w[:, 0:1], s.w1))
                own.step(dve.tensor_copy(m.pair_w[:, 1:2], s.w2))
                for i, at in enumerate((s.i1, s.i2)):
                    for c in range(DK):
                        own.join(dve.tensor_scalar(s.tmp, at, 8.0, float(D), ALU.add, ALU.mult))
                        own.join(dve.tensor_scalar(s.tmp, s.tmp, m.part_no[:, 0:1], float(c * P), ALU.add, ALU.add))
                        own.join(dve.tensor_copy(m.w1_rows[:, i, c:c + 1], s.tmp))
                    for c in range(FH // P):
                        own.join(dve.tensor_scalar(s.tmp, at, 8.0, float(FH), ALU.add, ALU.mult))
                        own.join(dve.tensor_scalar(s.tmp, s.tmp, m.part_no[:, 0:1], float(c * P), ALU.add, ALU.add))
                        own.join(dve.tensor_copy(m.w2_rows[:, i, c:c + 1], s.tmp))
            dve.sem_inc(w_ready, 1)
            for t in range(NT):
                dve.wait_ge(mixed, t + 1)
                dve.tensor_tensor(dest[:, t, :], psm[:, t % 2, 0:D], base[:, t, :], ALU.add).then_inc(added, 1)



def phase_experts(nc, m, name, EX, func, widths, mats, biases, dest, weight=None, picked=False, bn=None):
    sem = nc.alloc_semaphore
    NH = len(widths)
    FT = [w // P for w in widths]
    KT = [DK] + FT
    NL = NH + 1
    YC, HC = TB + 1, FT[-1] + 1
    w_in = [sem(f"{name}_w_in{u}") for u in range(2)]
    h_mm = [sem(f"{name}_h{i}_mm") for i in range(NH)]
    h_act = [sem(f"{name}_h{i}_act") for i in range(NH)]
    y_mm, y_add, bn_in, bn_dve, bn_root = (sem(f"{name}_{s}") for s in ("y_mm", "y_add", "bn_in", "bn_dve", "bn_root"))
    nload = NL + NH
    bn_kept = sem(f"{name}_bn_kept")
    if picked:
        nload = DK + 2 * FT[0]
    with ExitStack() as ctx:
        sb = lambda n, shape, dt=F32: ctx.enter_context(nc.sbuf_tensor(f"{name}_{n}", shape, dt))
        outs = widths + [D]
        w_sb = [sb(f"w{i}", [P, 2, KT[i], outs[i]]) for i in range(NL)]
        b_sb = [sb(f"b{i}", [P, 2, 2, FT[i]]) for i in range(NH)]
        h_sb = [sb(f"h{i}", [P, 3, FT[i], BLK]) for i in range(NH)]
        if bn is not None:
            v_rows = [sb(f"vr{i}", [EX * FT[i], 5, P]) for i in range(NH)]
            v_sb = [sb(f"v{i}", [P, 5, EX * FT[i]]) for i in range(NH)]
            kept = [nc.dram_tensor(f"{name}_kept{i}", (P, 2, EX * FT[i]), F32, kind="Internal").ap() for i in range(NH)]
        h_ps = [ctx.enter_context(nc.psum_tensor(f"{name}_hps{i}", [P, FT[i], BLK], F32)) for i in range(NH)]
        y_ps = ctx.enter_context(nc.psum_tensor(f"{name}_yps", [P, TB, BLK], F32))
        block = ctx.enter_context(nc.Block())
        per_pair = 2 * NB
        pairs = EX // 2

        def load_pair(eng, e2):
            for u in range(2):
                e = e2 * 2 + u
                if picked:
                    for k in range(DK):
                        eng.indirect_dma_start(w_sb[0][:, u, k, :], None, mats[0], bass.IndirectOffsetOnAxis(
                            ap=m.w1_rows[:, u, k:k + 1], axis=0)).then_inc(w_in[u], 16)
                    for k in range(FT[0]):
                        at = bass.IndirectOffsetOnAxis(ap=m.w2_rows[:, u, k:k + 1], axis=0)
                        eng.indirect_dma_start(w_sb[1][:, u, k, :], None, mats[1], at).then_inc(w_in[u], 16)
                        eng.indirect_dma_start(b_sb[0][:, u, 0, k:k + 1], None, biases[0], at).then_inc(w_in[u], 16)
                    continue
                if not isinstance(e2, int) or e2:
                    eng.wait_ge(y_mm, (e - 1) * (NB * TB) + YC)
                for i in range(NL):
                    eng.dma_start(w_sb[i][:, u, :, :], mats[i](e)).then_inc(w_in[u], 16)
                for i in range(NH):
                    if bn is None:
                        eng.dma_start(b_sb[i][:, u, 0, :], biases[i](e), allow_slow_non_contiguous=True).then_inc(w_in[u], 16)
                    else:
                        eng.dma_start(b_sb[i][:, u, :, :], kept[i][:, :, ds(e * FT[i], FT[i])]).then_inc(w_in[u], 16)

        @block.sync
        def _(sp):
            if picked:
                return
            if bn is not None:
                for i in range(NH):
                    for j, v in enumerate((biases[i],) + bn[i]):
                        sp.dma_start(v_rows[i][:, j, :], v.rearrange("e (f p) -> (e f) p", p=P)).then_inc(bn_in, 16)
                sp.wait_ge(bn_dve, 3)
                for i in range(NH):
                    sp.dma_start(kept[i], v_sb[i][:, 0:2, :]).then_inc(bn_kept, 16)
                sp.wait_ge(bn_kept, 16 * NH)
            load_pair(sp, 0)
            if pairs > 1:
                with sp.Fori(1, pairs) as e2:
                    load_pair(sp, e2)

        @block.gpsimd
        def _(pool):
            if picked:
                load_pair(pool, 0)

        @block.tensor
        def _(pe):
            def layer0(e2, v):
                u, b = v // NB, v % NB
                n = e2 * per_pair + v
                if b == 0:
                    pe.wait_ge(w_in[u], (e2 + 1) * (16 * nload))
                for f in range(FT[0]):
                    pe.wait_ge(h_act[0], n * FT[0] + (f + 1))
                    for k in range(DK):
                        mm = pe.matmul(h_ps[0][:, f, :], w_sb[0][:, u, k, f * P:(f + 1) * P],
                                       m.xT[:, k, b * BLK:(b + 1) * BLK], start=(k == 0), stop=(k == DK - 1))
                    mm.then_inc(h_mm[0], 1)

            def layer1(e2, v):
                u, b = v // NB, v % NB
                n = e2 * per_pair + v
                pe.wait_ge(h_act[0], (n + 2) * FT[0])
                for f in range(FT[1]):
                    pe.wait_ge(h_act[1], n * FT[1] + (f + 1))
                    for k in range(FT[0]):
                        mm = pe.matmul(h_ps[1][:, f, :], w_sb[1][:, u, k, f * P:(f + 1) * P], h_sb[0][:, b % 3, k, :],
                                       start=(k == 0), stop=(k == FT[0] - 1))
                    mm.then_inc(h_mm[1], 1)

            def last(e2, v):
                u, b = v // NB, v % NB
                n = e2 * per_pair + v
                pe.wait_ge(h_act[-1], (n + 2) * FT[-1])
                for q in range(TB):
                    pe.wait_ge(y_add, n * TB + (q + 1))
                    for k in range(FT[-1]):
                        mm = pe.matmul(y_ps[:, q, 0:D], h_sb[-1][:, b % 3, k, q * P:(q + 1) * P], w_sb[-1][:, u, k, :],
                                       start=(k == 0), stop=(k == FT[-1] - 1))
                    mm.then_inc(y_mm, 1)

            def pair(e2, more):
                for v in range(per_pair):
                    if NH == 2:
                        layer1(e2, v)
                    if v + 1 < per_pair:
                        layer0(e2, v + 1)
                    elif more:
                        layer0(e2 + 1, 0)
                    last(e2, v)

            if bn is not None:
                pe.wait_ge(bn_in, 16 * 5 * NH)
                for i in range(NH):
                    R = EX * FT[i]
                    for j in range(5):
                        pe.transpose(y_ps[:, i, j * R:(j + 1) * R], v_rows[i][:, j, :], m.ident[0:R, 0:R]).then_inc(bn_root, 1)
                pe.wait_ge(bn_dve, 1)
            pe.sem_inc(y_mm, YC)
            if NH == 2:
                pe.sem_inc(h_mm[1], HC)
            layer0(0, 0)
            if pairs > 1:
                with pe.Fori(0, pairs - 1) as e2:
                    pair(e2, True)
            pair(pairs - 1, False)

        @block.scalar
        def _(act):
            for i in range(NH):
                act.sem_inc(h_act[i], FT[i])
            if bn is not None:
                act.wait_ge(bn_dve, 2)
                for i in range(NH):
                    act.activation(v_sb[i][:, 4, :], v_sb[i][:, 4, :], ACT.Sqrt).then_inc(bn_root, 1)

            def hidden(i, e2, v):
                u, b = v // NB, v % NB
                n = e2 * per_pair + v
                if i == NH - 1:
                    act.wait_ge(y_mm, n * TB + (YC - TB))
                else:
                    act.wait_ge(h_mm[i + 1], n * FT[i + 1] + (HC - FT[i + 1]))
                if b == 0:
                    act.wait_ge(w_in[u], (e2 + 1) * (16 * nload))
                for f in range(FT[i]):
                    act.wait_ge(h_mm[i], n * FT[i] + (f + 1 + (HC if i else 0)))
                    bias = b_sb[i][:, u, 0, f:f + 1]
                    scale = 1.0 if bn is None else b_sb[i][:, u, 1, f:f + 1]
                    act.activation(h_sb[i][:, b % 3, f, :], h_ps[i][:, f, :], func, bias=bias,
                                   scale=scale).then_inc(h_act[i], 1)

            def pair(e2, more):
                for v in range(per_pair):
                    if NH == 2:
                        hidden(1, e2, v)
                    if v + 1 < per_pair:
                        hidden(0, e2, v + 1)
                    elif more:
                        hidden(0, e2 + 1, 0)

            hidden(0, 0, 0)
            if pairs > 1:
                with act.Fori(0, pairs - 1) as e2:
                    pair(e2, True)
            pair(pairs - 1, False)

        @block.vector
        def _(dve):
            dve.sem_inc(y_add, TB)
            own = Steps(dve, sem(f"{name}_dve"))
            if bn is not None:
                dve.wait_ge(bn_root, 5 * NH)
                for i in range(NH):
                    R = EX * FT[i]
                    own.join(dve.tensor_copy(v_sb[i][:, :, :].rearrange("p j r -> p (j r)"), y_ps[:, i, 0:5 * R]))
                dve.sem_inc(bn_dve, 1)
                for i in range(NH):
                    own.join(dve.tensor_scalar(v_sb[i][:, 4, :], v_sb[i][:, 4, :], 1e-3, None, ALU.add))
                dve.sem_inc(bn_dve, 1)
                dve.wait_ge(bn_root, 6 * NH)
                for i in range(NH):
                    b_, g_, be_, mu_, sd = (v_sb[i][:, j, :] for j in range(5))
                    own.join(dve.reciprocal(sd, sd))
                    own.join(dve.tensor_tensor(g_, g_, sd, ALU.mult))
                    own.join(dve.tensor_tensor(b_, b_, mu_, ALU.subtract))
                    own.join(dve.tensor_tensor(b_, b_, g_, ALU.mult))
                    own.join(dve.tensor_tensor(b_, b_, be_, ALU.add))
                dve.sem_inc(bn_dve, 1)

            def pair(e2):
                for v in range(per_pair):
                    u, b = v // NB, v % NB
                    n = e2 * per_pair + v
                    for q in range(TB):
                        t = b * TB + q
                        dve.wait_ge(y_mm, n * TB + (q + 1 + YC))
                        if picked:
                            w = m.pair_w[:, u:u + 1]
                        elif weight is None:
                            w = m.ones[:, 0:1]
                        else:
                            w = weight[:, t, ds(e2 * 2 + u, 1)]
                        dve.scalar_tensor_tensor(dest[:, t, :], y_ps[:, q, 0:D], w, dest[:, t, :], ALU.mult,
                                                 ALU.add).then_inc(y_add, 1)

            if pairs > 1:
                with dve.Fori(0, pairs) as e2:
                    pair(e2)
            else:
                pair(0)


def phase_add_row(nc, m, name, row):
    sem = nc.alloc_semaphore
    row_in = sem(f"{name}_in")
    with nc.sbuf_tensor(f"{name}_row", [P, D], F32) as r, nc.Block() as block:
        @block.sync
        def _(sp):
            sp.dma_start(r[:, :], row.partition_broadcast(P)).then_inc(row_in, 16)

        @block.vector
        def _(dve):
            dve.wait_ge(row_in, 16)
            dve.tensor_tensor(m.x[:, :, :], m.x[:, :, :], r[:, :].unsqueeze(1).to_broadcast([P, NT, D]), ALU.add)



def phase_attention(nc, m, W, Wl, Wr, b):
    H, DO = 4, 64
    DA = DO + 1
    QN = NT // 4
    sem = nc.alloc_semaphore
    w_in, xl_mm, xl_out, xl_done, wide_done, own_sem, el_mm, el_out, ask, told = (
        sem(f"att_{n}") for n in ("w_in", "xl_mm", "xl_out", "xl_done", "wide_done", "dve", "el_mm", "el_out", "ask", "told"))
    gained, scored_d, scored_p, o_mm, o_out, o_turn, fin_done, min_done, exp_done, tail = (
        sem(f"att_{n}") for n in ("gained", "scored_d", "scored_p", "o_mm", "o_out", "o_turn", "fin", "min", "exp", "tail"))
    a_in = [sem(f"att_a_in{i}") for i in range(2)]
    with ExitStack() as ctx:
        def sb(n, shape, dt=F32):
            return ctx.enter_context(nc.sbuf_tensor(f"att_{n}", shape, dt))

        w_sb = sb("w", [P, DK, DO])
        wlr = sb("wlr", [DO, 2, H])
        wl_wide = sb("wl_wide", [DO, H, P])
        xlT = sb("xlT", [DO, NP])
        xl1 = sb("xl1", [P, NT, DA])
        xF = sb("xF", [P, NT, H, DA])
        e_tok = sb("e_tok", [P, NT, 2, H])
        F_src, F_dst, G_dst = sb("F_src", [P, NT, H]), sb("F_dst", [P, NT, H]), sb("G_dst", [P, NT, H])
        top = sb("top", [P, H])
        G_src = sb("G_src", [P, H, NP])
        a_sb = m.xT[:, :, :].rearrange("p a (t n) -> p a t n", t=QN)
        gain = m.o[:, 0:4 * H, :].rearrange("p (a h c) d -> p a h (c d)", a=2, h=H)
        S = m.xn[:, 0:4 * H, :].rearrange("p (a h c) d -> p a h (c d)", a=2, h=H)
        oT = sb("oT", [DA, H, BLK])
        bias = sb("bias", [P, DO])
        fin = sb("fin", [P, H, DO])
        neg = sb("neg", [P, H, DO])
        rs = sb("rs", [P, 2, H])
        ps = ctx.enter_context(nc.psum_tensor("att_ps", [P, 8, BLK], F32))

        with nc.Block() as block:
            @block.sync
            def _(sp):
                sp.dma_start(w_sb[:, :, :], rows(W)).then_inc(w_in, 16)
                for i, w in enumerate((Wl, Wr)):
                    sp.dma_start(wlr[:, i, :], w.rearrange("h d -> d h"), allow_slow_non_contiguous=True).then_inc(w_in, 16)
                sp.dma_start(bias[:, :], b.partition_broadcast(P)).then_inc(w_in, 16)

            @block.tensor
            def _(pe):
                pe.wait_ge(w_in, 64)
                for c in range(NB):
                    if c >= 2:
                        pe.wait_ge(xl_out, c - 1)
                    for k in range(DK):
                        mm = pe.matmul(ps[0:DO, c % 2, :], w_sb[:, k, :], m.xT[:, k, c * BLK:(c + 1) * BLK],
                                       start=(k == 0), stop=(k == DK - 1))
                    mm.then_inc(xl_mm, 1)
                pe.wait_ge(wide_done, 1)
                for h in range(H):
                    for c in range(NB):
                        n = h * NB + c
                        pe.wait_ge(xl_out, c + 1)
                        if n >= 2:
                            pe.wait_ge(el_out, n - 1)
                        pe.matmul(ps[:, 6 + n % 2, :], wl_wide[:, h, :], xlT[:, c * BLK:(c + 1) * BLK],
                                  start=True, stop=True).then_inc(el_mm, 1)
                for t in range(NT):
                    pe.transpose(ps[:, 2 + t // 8, (t % 8) * DO:(t % 8 + 1) * DO], xlT[:, t * P:(t + 1) * P],
                                 m.ident[0:DO, 0:DO])
                    mm = pe.matmul(ps[:, 5, t * 2 * H:(t + 1) * 2 * H], xlT[:, t * P:(t + 1) * P],
                                   wlr[:, :, :].rearrange("p i h -> p (i h)"), start=True, stop=True)
                mm.then_inc(xl_done, 1)

            @block.scalar
            def _(act):
                for c in range(NB):
                    act.wait_ge(xl_mm, c + 1)
                    act.activation(xlT[:, c * BLK:(c + 1) * BLK], ps[0:DO, c % 2, :], ACT.Copy).then_inc(xl_out, 1)
                for h in range(H):
                    for c in range(NB):
                        act.wait_ge(el_mm, h * NB + c + 1)
                        act.activation(G_src[:, h, c * BLK:(c + 1) * BLK], ps[:, 6 + (h * NB + c) % 2, :],
                                       ACT.Copy).then_inc(el_out, 1)
                for i, v in enumerate((G_dst[:, :, :], F_dst[:, :, :], F_src[:, :, :])):
                    act.wait_ge(ask, i + 1)
                    act.activation(v, v, ACT.Exp).then_inc(told, 1)
                for h in range(H):
                    act.wait_ge(ask, 4 + h)
                    act.activation(G_src[:, h, :], G_src[:, h, :], ACT.Exp).then_inc(told, 1)

            @block.vector
            def _(dve):
                own = Steps(dve, own_sem)

                def wide(v):
                    return v.unsqueeze(1).to_broadcast([P, NT, H])
                dve.wait_ge(w_in, 64)
                dve.tensor_copy(wl_wide[:, :, :], wlr[:, 0, :].unsqueeze(2).to_broadcast([DO, H, P])).then_inc(wide_done, 1)
                own.step(dve.memset(xl1[:, :, DO:DA], 1.0))
                for h in range(H):
                    dve.wait_ge(el_out, (h + 1) * NB)
                    own.step(dve.tensor_reduce(top[:, h:h + 1], G_src[:, h, 0:N], AX.X, ALU.max))
                dve.wait_ge(xl_done, 1)
                own.step(dve.tensor_copy(xl1[:, 0:16, 0:DO], ps[:, 2:4, :].rearrange("p a (t d) -> p (a t) d", d=DO)))
                own.step(dve.tensor_copy(xl1[:, 16:NT, 0:DO], ps[:, 4, 0:(NT - 16) * DO].rearrange("p (t d) -> p t d", d=DO)))
                own.join(dve.tensor_copy(e_tok[:, :, :, :], ps[:, 5, 0:NT * 2 * H].rearrange("p (t i h) -> p t i h", i=2, h=H)))
                own.join(dve.tensor_tensor(e_tok[:, :, 1, :], e_tok[:, :, 1, :], wide(top[:, :]), ALU.add))
                own.join(dve.tensor_tensor(e_tok[:, :, 0, :], e_tok[:, :, 0, :], wide(top[:, :]), ALU.subtract))
                dve.tensor_scalar(G_dst[:, :, :], e_tok[:, :, 1, :], 0.8, EXP_TOP, ALU.mult, ALU.min).then_inc(ask, 1)
                dve.tensor_scalar(F_dst[:, :, :], e_tok[:, :, 1, :], 0.2, EXP_TOP, ALU.mult, ALU.min).then_inc(ask, 1)
                dve.tensor_scalar(F_src[:, :, :], e_tok[:, :, 0, :], 0.2, EXP_TOP, ALU.mult, ALU.min).then_inc(ask, 1)
                for h in range(H):
                    own.join(dve.tensor_scalar(G_src[:, h, :], G_src[:, h, :], top[:, h:h + 1], 0.8, ALU.subtract, ALU.mult))
                    dve.tensor_scalar(G_src[:, h, :], G_src[:, h, :], EXP_TOP, None, ALU.min).then_inc(ask, 1)
                dve.wait_ge(told, 2)
                for h in range(H):
                    dve.tensor_tensor(xF[:, :, h, :], xl1[:, :, :], F_dst[:, :, h:h + 1].to_broadcast([P, NT, DA]), ALU.mult)

        with nc.Block() as block:
            @block.sync
            def _(sp):
                with sp.Fori(0, NB) as c:
                    for i in range(4):
                        sp.wait_ge(scored_d, c * NT + (i * QN + 1))
                        sp.wait_ge(scored_p, c * NT + (i * QN + 1))
                        sp.dma_start(a_sb[:, i % 2, :, :],
                                     m.A[i * QN:(i + 1) * QN, :, ds(c * BLK, BLK)].rearrange("t p n -> p t n")
                                     ).then_inc(a_in[i % 2], 16)

            def score(eng, c, s, lo, hi, scored):
                if s % QN == 0:
                    eng.wait_ge(a_in[s // QN % 2], c * 32 + 16 * (s // QN // 2 + 1))
                eng.tensor_tensor(S[:, s % 2, lo:hi, :], gain[:, s % 2, lo:hi, :],
                                  a_sb[:, s // QN % 2, s % QN, :].unsqueeze(1).to_broadcast([P, hi - lo, BLK]),
                                  ALU.mult).then_inc(scored, 1)

            HD = 2

            @block.vector
            def _(dve):
                dve.sem_inc(scored_d, QN + 1)
                dve.sem_inc(fin_done, 1)

                def gains(c, s):
                    dve.wait_ge(scored_p, c * NT + (s + QN))
                    dve.wait_ge(scored_d, c * NT + (s + QN))
                    for h in reversed(range(H)):
                        dve.tensor_scalar(gain[:, s % 2, h, :], G_src[:, h, ds(c * BLK, BLK)], G_dst[:, s, h:h + 1], 1.0,
                                          ALU.mult, ALU.max).then_inc(gained, 1)

                def finish(c, q):
                    own = Steps(dve, tail, base=(c * TB + q) * 7)
                    j = c * TB + q
                    dve.wait_ge(o_turn, j + 1)
                    o = ps[:, 4 + q % 2, 0:H * DA].rearrange("p (h d) -> p h d", h=H)
                    Fs = F_src[:, ds(j, 1), :].rearrange("p a h -> p (a h)")
                    own.join(dve.tensor_tensor(rs[:, 0, :], o[:, :, DO], Fs, ALU.mult))
                    own.join(dve.tensor_scalar(rs[:, 0, :], rs[:, 0, :], 1e-12, None, ALU.max))
                    own.join(dve.reciprocal(rs[:, 1, :], rs[:, 0, :]))
                    own.join(dve.tensor_tensor(rs[:, 1, :], rs[:, 1, :], Fs, ALU.mult))
                    own.join(dve.tensor_tensor(fin[:, :, :], o[:, :, 0:DO], rs[:, 1, :].unsqueeze(2).to_broadcast([P, H, DO]), ALU.mult))
                    own.join(dve.tensor_tensor(fin[:, :, :], fin[:, :, :], bias[:, :].unsqueeze(1).to_broadcast([P, H, DO]), ALU.add))
                    dve.tensor_scalar(neg[:, :, :], fin[:, :, :], 0.0, None, ALU.min).then_inc(min_done, 1)
                    dve.wait_ge(exp_done, j + 1)
                    own.join(dve.scalar_tensor_tensor(fin[:, :, :], fin[:, :, :], 0.0, neg[:, :, :], ALU.max, ALU.add))
                    xt = m.x[:, ds(j, 1), :].rearrange("p a d -> p (a d)")
                    dve.scalar_tensor_tensor(xt, fin[:, :, :].rearrange("p h d -> p (h d)"), -1.0, xt, ALU.add,
                                             ALU.add).then_inc(fin_done, 1)

                def one_block(c, before):
                    gains(c, 0)
                    for s in range(NT):
                        if s + 1 < NT:
                            gains(c, s + 1)
                        dve.wait_ge(gained, c * (NT * H) + (s + 1) * H)
                        dve.wait_ge(o_mm, c * (NT * H) + (s * H + 1))
                        score(dve, c, s, 0, HD, scored_d)
                        if before and s % 4 == 3 and s // 4 < TB:
                            finish(c - 1, s // 4)

                one_block(0, False)
                with dve.Fori(1, NB) as c:
                    one_block(c, True)
                for q in range(TB):
                    finish(NB - 1, q)

            @block.gpsimd
            def _(pool):
                pool.sem_inc(scored_p, QN + 1)
                with pool.Fori(0, NB) as c:
                    for s in range(NT):
                        pool.wait_ge(gained, c * (NT * H) + (s * H + (H - HD)))
                        pool.wait_ge(o_mm, c * (NT * H) + (s * H + 1))
                        score(pool, c, s, HD, H, scored_p)

            @block.scalar
            def _(act):
                act.sem_inc(o_out, 1)

                def exps(c):
                    for q in range(TB):
                        act.wait_ge(min_done, c * TB + (q + 1))
                        act.activation(neg[:, :, :], neg[:, :, :], ACT.Exp).then_inc(exp_done, 1)

                def copy(c):
                    act.wait_ge(o_mm, c * (NT * H) + (NT * H + H + 1))
                    act.activation(oT[:, :, :], ps[0:DA, 0:H, :], ACT.Copy).then_inc(o_out, 1)

                copy(0)
                with act.Fori(1, NB) as c:
                    exps(c - 1)
                    copy(c)
                exps(NB - 1)

            @block.tensor
            def _(pe):
                pe.sem_inc(o_mm, H + 1)

                def turn(c, q):
                    pe.wait_ge(fin_done, c * TB + max(0, q - 1) + (1 if q else 0))
                    for h in range(H):
                        mm = pe.transpose(ps[:, 4 + q % 2, h * DA:(h + 1) * DA], oT[:, h, q * P:(q + 1) * P],
                                          m.ident[0:DA, 0:DA])
                    mm.then_inc(o_turn, 1)

                def one_block(c, before):
                    pe.wait_ge(o_out, c + 1)
                    for s in range(NT):
                        pe.wait_ge(scored_d, c * NT + (s + 2 + QN))
                        pe.wait_ge(scored_p, c * NT + (s + 2 + QN))
                        for h in range(H):
                            pe.matmul(ps[0:DA, h, :], xF[:, s, h, :], S[:, s % 2, h, :],
                                      start=(s == 0), stop=(s == NT - 1)).then_inc(o_mm, 1)
                        if before and s % 4 == 1 and s // 4 < TB:
                            turn(c - 1, s // 4)

                one_block(0, False)
                with pe.Fori(1, NB) as c:
                    one_block(c, True)
                pe.wait_ge(o_out, NB + 1)
                for q in range(TB):
                    turn(NB - 1, q)


def phase_store(nc, m, out):
    stored = nc.alloc_semaphore("stored")
    full = N // P
    with nc.Block() as block:
        @block.sync
        def _(sp):
            sp.dma_start(out[0:full * P, :].rearrange("(t p) d -> p t d", p=P), m.x[:, 0:full, :]).then_inc(stored, 16)
            sp.dma_start(out[full * P:N, :], m.x[0:N - full * P, full, :]).then_inc(stored, 16)
            sp.wait_ge(stored, 32)


def program(nc, i, out, upto=99):
    m = Mem()
    m.A = nc.dram_tensor("counts", (NT, P, NP), F32, kind="Internal").ap()
    m.AT = nc.dram_tensor("counts_t", (NT, P, NP), F32, kind="Internal").ap()
    with ExitStack() as ctx:
        def sb(name, shape, dt=F32):
            return ctx.enter_context(nc.sbuf_tensor(name, shape, dt))

        m.x = sb("x_tok", [P, NT, D])
        m.xn = sb("xn_tok", [P, NT, D])
        m.xT = sb("x_feat", [P, DK, NP])
        m.o = sb("o_tok", [P, NT, D])
        m.ident, m.ones = sb("ident", [P, P]), sb("ones", [P, P])
        m.zeros16 = sb("zeros16", [P, P], F16)
        m.src_no = sb("src_no", [P, NP], F16)
        m.expert_no = sb("expert_no", [P, NT, 8])
        m.part_no = sb("part_no", [P, 1])
        m.src_col, m.dst_col = sb("src_col", [P, GC * NG]), sb("dst_col", [P, GC * NG])
        m.ranges = sb("ranges", [1, 2, NT], I32)
        m.deg, m.inv_count, m.dinv_loop, m.dinv = (sb(n, [P, NT]) for n in ("deg", "inv_count", "dinv_loop", "dinv"))
        m.dinv_row = sb("dinv_row", [P, NP])
        m.wd = sb("route_w", [P, NT, 8])
        m.pair_w = sb("pair_w", [P, 2])
        m.w1_rows, m.w2_rows = sb("w1_rows", [P, 2, DK], I32), sb("w2_rows", [P, 2, FH // P], I32)
        m.wl, m.wr, m.wg = (sb(n, [P, DK, D]) for n in ("wl_t", "wr_t", "wg_t"))

        def expert_mats(*ws):
            return [lambda e, w=w: w[ds(e, 1), :, :].rearrange("a (k p) n -> p (a k) n", p=P) for w in ws]

        def expert_bias(*bs):
            return [lambda e, b=b: b[ds(e, 1), :].rearrange("a (k p) -> p (a k)", p=P) for b in bs]

        phases = [
            lambda: phase_setup(nc, m, i["x"], i["src"], i["dst"]),
            lambda: phase_counts(nc, m),
            lambda: phase_degrees(nc, m),
            lambda: phase_transpose_weights(nc, m, [(i["L0_gnn_W_l"], m.wl), (i["L0_gnn_W_r"], m.wr), (i["L1_gnn_W"], m.wg)]),
            lambda: phase_norm(nc, m, "n0", m.x, m.xn, m.xT),
            lambda: phase_gather(nc, m, "g0", m.xn, "mean", m.wl, m.wr, i["L0_gnn_b_r"]),
            lambda: phase_norm(nc, m, "n1", m.x, m.xn, m.xT),
            lambda: phase_route(nc, m, "r0", "mean", 8, i["L0_ffn_Wr"], i["L0_ffn_br"], i["L0_ffn_b2"], m.o, m.xn),
            lambda: phase_experts(nc, m, "e0", 2, ACT.Gelu, [FH],
                                  [i["L0_ffn_W1"].rearrange("e d f -> (e d) f"), i["L0_ffn_W2"].rearrange("e f d -> (e f) d")],
                                  [i["L0_ffn_b1"].rearrange("e (f a) -> (e f) a", a=1)], m.o, picked=True),
            lambda: phase_norm(nc, m, "n2", m.o, m.o, gamma=i["L0_ffn_gamma"], beta=i["L0_ffn_beta"], finish="add"),
            lambda: phase_norm(nc, m, "n3", m.x, m.xn, m.xT, scale=m.dinv_loop),
            lambda: phase_gather(nc, m, "g1", m.xn, "loop", m.wg, bias=i["L1_gnn_b"]),
            lambda: phase_norm(nc, m, "n4", m.o, m.o, gamma=i["L1_gnn_gamma"], beta=i["L1_gnn_beta"], finish="relu_add"),
            lambda: phase_norm(nc, m, "n5", m.x, m.xn, m.xT),
            lambda: phase_route(nc, m, "r1", "mlp", 6, i["L1_ffn_router_w2"], i["L1_ffn_router_b2"], i["L1_ffn_expert_b3"],
                                m.x, m.x, i["L1_ffn_router_w1"], i["L1_ffn_router_b1"]),
            lambda: phase_experts(nc, m, "e1", 6, ACT.Relu, [256, 256],
                                  expert_mats(i["L1_ffn_expert_w1"], i["L1_ffn_expert_w2"], i["L1_ffn_expert_w3"]),
                                  expert_bias(i["L1_ffn_expert_b1"], i["L1_ffn_expert_b2"]), m.x, weight=m.wd),
            lambda: phase_norm(nc, m, "n6", m.x, m.xn, m.xT, scale=m.dinv),
            lambda: phase_gather(nc, m, "g2", m.xn, "keep"),
            lambda: phase_experts(nc, m, "e2", 2, ACT.Gelu, [FH],
                                  [lambda e: rows(i["L2_gnn_W1"][:, e * FH:(e + 1) * FH]),
                                   lambda e: rows(i["L2_gnn_W2"][e * FH:(e + 1) * FH, :])],
                                  [lambda e: per_partition(i["L2_gnn_b1"][e * FH:(e + 1) * FH])], m.x),
            lambda: phase_add_row(nc, m, "b2", i["L2_gnn_b2"]),
            lambda: phase_norm(nc, m, "n7", m.x, m.xn),
            lambda: phase_norm(nc, m, "n8", m.xn, m.o, m.xT, gamma=i["L2_ffn_gamma"], beta=i["L2_ffn_beta"]),
            lambda: phase_route(nc, m, "r2", "top", 8, i["L2_ffn_Wr"], i["L2_ffn_br"], i["L2_ffn_b2"], m.x, m.x),
            lambda: phase_experts(nc, m, "e3", 8, ACT.Gelu, [FH], expert_mats(i["L2_ffn_W1"], i["L2_ffn_W2"]),
                                  expert_bias(i["L2_ffn_b1"]), m.x, weight=m.wd),
            lambda: phase_norm(nc, m, "n9", m.x, m.xn, m.xT),
            lambda: phase_attention(nc, m, i["L3_gnn_W"], i["L3_gnn_Wl"], i["L3_gnn_Wr"], i["L3_gnn_b"]),
            lambda: phase_norm(nc, m, "n10", m.x, m.xn, m.xT),
            lambda: phase_route(nc, m, "r3", "dense", 8, i["L3_ffn_Wr"], i["L3_ffn_br"], i["L3_ffn_bo"], m.x, m.x),
            lambda: phase_experts(nc, m, "e4", 8, ACT.Relu, [256, 256],
                                  expert_mats(i["L3_ffn_W1"], i["L3_ffn_W2"], i["L3_ffn_Wo"]),
                                  [i["L3_ffn_b1"], i["L3_ffn_b2"]], m.x, weight=m.wd,
                                  bn=[tuple(i[f"L3_ffn_{v}{n}"] for v in ("g", "be", "m", "v")) for n in (1, 2)]),
        ]
        for phase in phases[:upto]:
            with nc.cleanup_on_exit():
                phase()
        phase_store(nc, m, out)


def kernel(**inputs):
    import numpy as _np
    import concourse.bacc as _bacc
    from concourse import mybir as _mybir
    from concourse.bass_utils import run_bass_kernel_spmd as _run

    nc = _bacc.Bacc("TRN2", target_bir_lowering=False, num_devices=1)
    arrays, views = {}, {}
    for name, value in inputs.items():
        a = _np.ascontiguousarray(value)
        arrays[f"in_{name}"] = a
        views[name] = nc.dram_tensor(f"in_{name}", a.shape, _mybir.dt.from_np(a.dtype), kind="ExternalInput").ap()
    out = nc.dram_tensor("out_x", (N, D), F32, kind="ExternalOutput").ap()
    program(nc, views, out)
    r = _run(nc, [arrays], core_ids=[0])
    return r.results[0]["out_x"]
```

```python
from contextlib import ExitStack

import concourse.bass as bass
from concourse import mybir

F32 = mybir.dt.float32
F32R = mybir.dt.float32r
F16 = mybir.dt.float16
I32 = mybir.dt.int32
ALU = mybir.AluOpType
ACT = mybir.ActivationFunctionType
AX = mybir.AxisListType

P = 128
N = 2500
D = 256
DK = D // P
NT = -(-N // P)
NP = NT * P
BLK = 512
NB = NP // BLK
TB = BLK // P
E = 80000
GC = 5
NG = E // (GC * P)
HALF = NP // 2
FH = 512
EXACT16 = 2048.0
Y_SCALE = 2048.0
AGG_SCALE = 2.0 / Y_SCALE
EPS = 1e-5
EXP_TOP = 88.7
BIG = 3.0e38
ds = bass.ds


class Steps:

    def __init__(self, eng, sem, base=0):
        self.eng, self.sem, self.n = eng, sem, base

    def step(self, ins):
        ins.then_inc(self.sem, 1)
        self.n = self.n + 1

    def join(self, ins):
        self.step(ins)
        self.eng.wait_ge(self.sem, self.n)


class Mem:
    pass


def rows(ap):
    return ap.rearrange("(k p) n -> p k n", p=P)


def per_partition(ap):
    return ap.rearrange("(k p) -> p k", p=P)



def phase_setup(nc, m, x, src, dst):
    sem = nc.alloc_semaphore
    main_in, tail_in, edges_in = sem("main_in"), sem("tail_in"), sem("edges_in")
    tail_zeroed, made, dve_own = sem("tail_zeroed"), sem("consts_made"), sem("setup_dve")
    turned, turned_rng, turned_row = sem("edges_turned"), sem("range_turned"), sem("range_row")
    full = N // P
    with (
        nc.sbuf_tensor("edge_i", [P, 2, GC * P], I32) as edge_i,
        nc.sbuf_tensor("edge_f", [P, 2, GC * P], F32) as edge_f,
        nc.sbuf_tensor("bounds", [P, 2, NT], F32) as bounds,
        nc.sbuf_tensor("tile_low", [P, 2], F32) as tile_low,
        nc.sbuf_tensor("group_no", [P, 2, NG], F32) as group_no,
        nc.sbuf_tensor("bounds_row", [P, 2, NG], F32) as bounds_row,
        nc.sbuf_tensor("touch", [P, 3, NG], F32) as touch,
        nc.sbuf_tensor("ends", [P, 4], F32) as ends,
        nc.psum_tensor("turn_ps", [P, 4, 4, P], F32) as ps,
        nc.Block() as block,
    ):
        @block.sync
        def _(sp):
            sp.dma_start(edge_i[0:NG, 0, :], src.rearrange("(p e) -> p e", p=NG)).then_inc(edges_in, 16)
            sp.dma_start(edge_i[0:NG, 1, :], dst.rearrange("(p e) -> p e", p=NG)).then_inc(edges_in, 16)
            sp.dma_start(m.x[:, 0:full, :], x[0:full * P, :].rearrange("(t p) d -> p t d", p=P)).then_inc(main_in, 16)
            sp.wait_ge(tail_zeroed, 1)
            sp.dma_start(m.x[0:N - full * P, full, :], x[full * P:N, :]).then_inc(tail_in, 16)
            sp.wait_ge(main_in, 16)
            sp.wait_ge(tail_in, 16)

        @block.gpsimd
        def _(pool):
            own = Steps(pool, made)
            pool.memset(m.x[:, full, :], 0.0).then_inc(tail_zeroed, 1)
            own.step(pool.memset(m.ones[:, :], 1.0))
            own.join(pool.memset(m.ident[:, :], 0.0))
            own.join(pool.affine_select(out=m.ident[:, :], in_=m.ident[:, :], compare_op=ALU.not_equal, fill=1.0,
                                        base=0, pattern=[[-1, P]], channel_multiplier=1))
            pool.tensor_scalar(m.half16[:, :], m.ident[:, :], 0.5, None, ALU.mult)
            own.step(pool.iota(m.src_no[:, :], pattern=[[1, NP]], base=-HALF, channel_multiplier=0,
                               allow_small_or_imprecise_dtypes=True))
            own.step(pool.iota(m.expert_no[:, :, :], pattern=[[0, NT], [1, 8]], base=-8, channel_multiplier=0,
                               allow_small_or_imprecise_dtypes=True))
            own.step(pool.iota(m.part_no[:, :], pattern=[[0, 1]], base=0, channel_multiplier=1,
                               allow_small_or_imprecise_dtypes=True))
            own.step(pool.iota(tile_low[:, 0:1], pattern=[[0, 1]], base=0, channel_multiplier=P,
                               allow_small_or_imprecise_dtypes=True))
            own.step(pool.iota(tile_low[:, 1:2], pattern=[[0, 1]], base=P, channel_multiplier=P,
                               allow_small_or_imprecise_dtypes=True))
            own.step(pool.iota(group_no[:, 0, :], pattern=[[1, NG]], base=-NG, channel_multiplier=0,
                               allow_small_or_imprecise_dtypes=True))
            own.step(pool.iota(group_no[:, 1, :], pattern=[[1, NG]], base=1, channel_multiplier=0,
                               allow_small_or_imprecise_dtypes=True))

        @block.vector
        def _(dve):
            own = Steps(dve, dve_own)
            dve.wait_ge(edges_in, 32)
            dve.memset(m.zeros16[:, :], 0.0)
            own.step(dve.tensor_scalar(edge_f[0:NG, 0, :], edge_i[0:NG, 0, :], -float(HALF), None, ALU.add))
            own.join(dve.tensor_copy(edge_f[0:NG, 1, :], edge_i[0:NG, 1, :]))
            own.step(dve.tensor_reduce(ends[0:NG, 0:1], edge_f[0:NG, 1, :], AX.X, ALU.min))
            own.join(dve.tensor_reduce(ends[0:NG, 1:2], edge_f[0:NG, 1, :], AX.X, ALU.max))
            own.join(dve.tensor_copy(bounds[0:NG, :, :], ends[0:NG, 0:2].unsqueeze(2).to_broadcast([NG, 2, NT])))
            dve.wait_ge(turned, 2 * GC)
            for i, col in enumerate((m.src_col, m.dst_col)):
                for k in range(GC):
                    n = i * GC + k
                    own.step(dve.tensor_copy(col[:, k:k + GC * (NG - 1) + 1:GC], ps[:, n // 4, n % 4, 0:NG]))
            dve.wait_ge(turned_rng, 2)
            dve.wait_ge(made, 10)
            own.join(dve.tensor_copy(bounds_row[0:NT, :, :], ps[0:NT, 3, 0:2, 0:NG]))
            own.step(dve.tensor_scalar(touch[0:NT, 0, :], bounds_row[0:NT, 0, :], tile_low[0:NT, 1:2], None, ALU.is_lt))
            own.join(dve.tensor_scalar(touch[0:NT, 1, :], bounds_row[0:NT, 1, :], tile_low[0:NT, 0:1], None, ALU.is_ge))
            own.join(dve.tensor_tensor(touch[0:NT, 0, :], touch[0:NT, 0, :], touch[0:NT, 1, :], ALU.mult))
            own.step(dve.tensor_tensor(touch[0:NT, 1, :], touch[0:NT, 0, :], group_no[0:NT, 0, :], ALU.mult))
            own.join(dve.tensor_tensor(touch[0:NT, 2, :], touch[0:NT, 0, :], group_no[0:NT, 1, :], ALU.mult))
            own.step(dve.tensor_reduce(ends[0:NT, 0:1], touch[0:NT, 1, :], AX.X, ALU.min))
            own.join(dve.tensor_reduce(ends[0:NT, 1:2], touch[0:NT, 2, :], AX.X, ALU.max))
            own.join(dve.tensor_scalar(ends[0:NT, 2:3], ends[0:NT, 0:1], float(NG), float(NG - 1), ALU.add, ALU.min))
            own.join(dve.tensor_scalar(ends[0:NT, 3:4], ends[0:NT, 2:3], 1.0, ends[0:NT, 1:2], ALU.add, ALU.max))
            dve.wait_ge(turned_row, 2)
            own.join(dve.tensor_copy(m.ranges[0:1, :, :], ps[0:1, 3, 2:4, 0:NT]))

        @block.tensor
        def _(pe):
            pe.wait_ge(made, 3)
            pe.wait_ge(dve_own, 2)
            for i in range(2):
                for k in range(GC):
                    n = i * GC + k
                    pe.transpose(ps[:, n // 4, n % 4, 0:NG], edge_f[0:NG, i, k * P:(k + 1) * P],
                                 m.ident[0:NG, 0:NG]).then_inc(turned, 1)
            pe.wait_ge(dve_own, 5)
            for i in range(2):
                pe.transpose(ps[0:NT, 3, i, 0:NG], bounds[0:NG, i, :], m.ident[0:NG, 0:NG]).then_inc(turned_rng, 1)
            pe.wait_ge(dve_own, 15 + 10)
            for i in range(2):
                pe.transpose(ps[0:1, 3, 2 + i, 0:NT], ends[0:NT, 2 + i:3 + i], m.ident[0:NT, 0:NT]).then_inc(turned_row, 1)



def phase_counts(nc, m):
    sem = nc.alloc_semaphore
    built, slot_free, summed = sem("onehots_built"), sem("onehots_used"), sem("counts_summed")
    row_out, turned, turned_out = sem("counts_copied"), sem("counts_turned"), sem("turned_copied")
    row_stored = [sem(f"counts_stored{u}") for u in range(2)]
    high_stored, low_stored = sem("high_stored"), sem("low_stored")
    high_done, low_done, moved = sem("high_done"), sem("low_done"), sem("dst_moved")
    with (
        nc.sbuf_tensor("hot_dst", [P, GC, P], F16) as hot_dst,
        nc.sbuf_tensor("hot_src", [P, GC, N], F16) as hot_src,
        nc.sbuf_tensor("count_row", [P, 2, NP], F32) as count_row,
        nc.sbuf_tensor("count_turn", [P, NT, P], F32) as count_turn,
        nc.sbuf_tensor("turn_high", [P, NT, P], F16) as high,
        nc.sbuf_tensor("turn_low", [P, NT, P], F16) as low,
        nc.psum_tensor("count_ps", [P, NB, BLK], F32) as acc,
        nc.psum_tensor("cturn_ps", [P, 3, TB, P], F32) as tps,
        nc.Block() as block,
    ):
        dst_no = m.src_no[:, HALF:HALF + P]

        @block.vector
        def _(dve):
            used = dve.alloc_register("groups_built")
            dve.reg_mov(used, 0)
            with dve.Fori(0, NT) as t:
                first = dve.value_load(m.ranges[0:1, 0, ds(t, 1)], min_val=0, max_val=NG - 1)
                last = dve.value_load(m.ranges[0:1, 1, ds(t, 1)], min_val=1, max_val=NG)
                with dve.Fori(first, last) as g:
                    n = dve.snap(used)
                    for j in range(GC):
                        dve.wait_ge(slot_free, n * GC + (j + 1))
                        dve.tensor_scalar(hot_dst[:, j, :], dst_no, m.dst_col[:, ds(g * GC + j, 1)], None, ALU.is_equal)
                        dve.tensor_scalar(hot_src[:, j, :], m.src_no[:, 0:N], m.src_col[:, ds(g * GC + j, 1)], None,
                                          ALU.is_equal).then_inc(built, 1)
                    dve.reg_add(used, used, 1)
                dve.wait_ge(built, dve.snap(used) * GC)
                dve.tensor_scalar(m.dst_col[:, :], m.dst_col[:, :], -float(P), None, ALU.add).then_inc(moved, 1)
                dve.wait_ge(moved, t + 1)

        @block.tensor
        def _(pe):
            used = pe.alloc_register("groups_used")
            pe.reg_mov(used, 0)
            pe.sem_inc(slot_free, GC)

            def sums(t):
                pe.wait_ge(row_out, t + 1)
                for b in range(NB):
                    pe.matmul(acc[:, b, :], m.zeros16[:, :], m.src_no[:, b * BLK:(b + 1) * BLK],
                              start=True, stop=False, skip_group_check=True)
                first = pe.value_load(m.ranges[0:1, 0, ds(t, 1)], min_val=0, max_val=NG - 1)
                last = pe.value_load(m.ranges[0:1, 1, ds(t, 1)], min_val=1, max_val=NG)
                with pe.Fori(first, last):
                    n = pe.snap(used)
                    for j in range(GC):
                        pe.wait_ge(built, n * GC + (j + 1))
                        for b in range(NB):
                            cut = slice(b * BLK, min(N, (b + 1) * BLK))
                            mm = pe.matmul(acc[:, b, 0:cut.stop - cut.start], hot_dst[:, j, :], hot_src[:, j, cut],
                                           start=False, stop=False, skip_group_check=True)
                        mm.then_inc(slot_free, 1)
                    pe.reg_add(used, used, 1)
                for b in range(NB):
                    mm = pe.matmul(acc[:, b, 0:2], m.zeros16[:, :], m.src_no[:, 0:2],
                                   start=False, stop=True, skip_group_check=True)
                mm.then_inc(summed, 1)

            def turn(t, u):
                pe.wait_ge(row_out, t + 2)
                for b in range(NB):
                    pe.wait_ge(turned_out, t * NB + max(1, b - 1))
                    for q in range(TB):
                        s = b * TB + q
                        mm = pe.transpose(tps[:, b % 3, q, :], count_row[:, u, s * P:(s + 1) * P], m.ident[:, :])
                    mm.then_inc(turned, 1)

            sums(0)
            with pe.Fori(0, NT // 2 - 1) as i:
                sums(i * 2 + 1)
                turn(i * 2, 0)
                sums(i * 2 + 2)
                turn(i * 2 + 1, 1)
            sums(NT - 1)
            turn(NT - 2, 0)
            turn(NT - 1, 1)

        @block.scalar
        def _(act):
            act.sem_inc(row_out, 1)
            act.sem_inc(turned_out, 1)

            def copy_row(t, u, stored):
                if stored is not None:
                    act.wait_ge(row_stored[u], stored)
                act.wait_ge(summed, t + 1)
                act.activation(count_row[:, u, :], acc[:, :, :].rearrange("p b n -> p (b n)"), ACT.Copy,
                               accum_out=m.deg[:, ds(t, 1)]).then_inc(row_out, 1)

            def copy_turned(t):
                act.wait_ge(low_done, t + 1)
                for b in range(NB):
                    act.wait_ge(turned, t * NB + (b + 1))
                    act.activation(count_turn[:, b * TB:(b + 1) * TB, :], tps[:, b % 3, :, :], ACT.Copy,
                                   scale=0.5).then_inc(turned_out, 1)
                act.wait_ge(turned_out, (t + 1) * NB + 1)
                act.wait_ge(high_stored, t * 16 + 16)
                act.activation(high[:, :, :], count_turn[:, :, :], ACT.Copy).then_inc(high_done, 1)

            copy_row(0, 0, None)
            with act.Fori(0, NT // 2 - 1) as i:
                copy_row(i * 2 + 1, 1, i * 16 + 16)
                copy_turned(i * 2)
                copy_row(i * 2 + 2, 0, i * 16 + 16)
                copy_turned(i * 2 + 1)
            copy_row(NT - 1, 1, NT // 2 * 16)
            copy_turned(NT - 2)
            copy_turned(NT - 1)

        @block.gpsimd
        def _(pool):
            pool.sem_inc(low_done, 1)
            with pool.Fori(0, NT) as t:
                pool.wait_ge(high_done, t + 1)
                pool.wait_ge(low_stored, t * 16 + 16)
                pool.tensor_tensor(low[:, :, :], count_turn[:, :, :], high[:, :, :], ALU.subtract).then_inc(low_done, 1)

        @block.sync
        def _(sp):
            sp.sem_inc(row_stored[1], 16)
            sp.sem_inc(high_stored, 16)
            sp.sem_inc(low_stored, 16)
            tile = sp.alloc_register("tile_stored")
            sp.reg_mov(tile, 0)
            with sp.Fori(0, NT // 2):
                for u in range(2):
                    t = sp.snap(tile)
                    sp.wait_ge(low_done, t + 2)
                    sp.dma_start(m.A[ds(t, 1), :, :].rearrange("a p n -> (a p) n"), count_row[:, u, :]).then_inc(row_stored[u], 16)
                    sp.dma_start(m.AT_high[ds(t, 1), :, :].rearrange("a p n -> (a p) n"),
                                 high[:, :, :].rearrange("p s n -> p (s n)")).then_inc(high_stored, 16)
                    sp.dma_start(m.AT_low[ds(t, 1), :, :].rearrange("a p n -> (a p) n"),
                                 low[:, :, :].rearrange("p s n -> p (s n)")).then_inc(low_stored, 16)
                    sp.reg_add(tile, tile, 1)
            sp.wait_ge(row_stored[0], NT // 2 * 16)
            sp.wait_ge(row_stored[1], NT // 2 * 16 + 16)
            sp.wait_ge(high_stored, NT * 16 + 16)
            sp.wait_ge(low_stored, NT * 16 + 16)


def stats_steps(own, dve, st, mean, var, tmp):
    own.step(dve.tensor_tensor(mean, st[:, :, 1], st[:, :, 4], ALU.add))
    own.step(dve.tensor_tensor(tmp, st[:, :, 1], st[:, :, 4], ALU.subtract))
    own.join(dve.tensor_tensor(var, st[:, :, 2], st[:, :, 5], ALU.add))
    own.step(dve.tensor_scalar(mean, mean, 0.5, None, ALU.mult))
    own.step(dve.tensor_scalar(var, var, 1.0 / D, EPS, ALU.mult, ALU.add))
    own.join(dve.tensor_tensor(tmp, tmp, tmp, ALU.mult))
    own.join(dve.scalar_tensor_tensor(var, tmp, 0.25, var, ALU.mult, ALU.add))


def phase_norm(nc, m, name, src, out, outT=None, gamma=None, beta=None, scale=None, finish=None):
    sem = nc.alloc_semaphore
    dve_own, want_root, root, ready = (sem(f"{name}_{s}") for s in ("dve", "want_root", "root", "ready"))
    turned, turned_out, affine_in = (sem(f"{name}_{s}") for s in ("turned", "turned_out", "affine_in"))
    plain, pool_own, pool_ready = (sem(f"{name}_{s}") for s in ("plain", "pool", "pool_ready"))
    PC = 2

    def affine(own, eng, b):
        v, xv = (a[:, b * TB:(b + 1) * TB, :] for a in (out, m.x))
        ga, be = (gb[:, i:i + 1, :].to_broadcast([P, TB, D]) for i in range(2))
        own.join(eng.tensor_tensor(v, v, ga, ALU.mult))
        last = eng.tensor_tensor(v, v, be, ALU.add)
        if finish:
            own.join(last)
            if finish == "relu_add":
                own.join(eng.tensor_scalar(v, v, 0.0, None, ALU.max))
            last = eng.tensor_tensor(xv, v, xv, ALU.add)
        return last

    with (
        nc.sbuf_tensor(f"{name}_st", [P, NT, 6], F32) as st,
        nc.sbuf_tensor(f"{name}_mean", [P, NT], F32) as mean,
        nc.sbuf_tensor(f"{name}_var", [P, NT], F32) as var,
        nc.sbuf_tensor(f"{name}_tmp", [P, NT], F32) as tmp,
        nc.sbuf_tensor(f"{name}_gb", [P, 2, D], F32) as gb,
        nc.psum_tensor(f"{name}_ps", [P, 4, TB, P], F32) as ps,
        nc.Block() as block,
    ):
        @block.sync
        def _(sp):
            if gamma is not None:
                sp.dma_start(gb[:, 0, :], gamma.partition_broadcast(P)).then_inc(affine_in, 16)
                sp.dma_start(gb[:, 1, :], beta.partition_broadcast(P)).then_inc(affine_in, 16)

        @block.vector
        def _(dve):
            own = Steps(dve, dve_own)
            for t in range(NT):
                dve.bn_stats(st[:, t, :], src[:, t, :]).then_inc(dve_own, 1)
            own.n = NT
            dve.wait_ge(dve_own, NT)
            stats_steps(own, dve, st, mean[:, :], var[:, :], tmp[:, :])
            dve.tensor_copy(var[:, :], var[:, :]).then_inc(want_root, 1)
            dve.wait_ge(root, 1)
            own.join(dve.reciprocal(tmp[:, :], var[:, :]))
            for t in range(NT):
                dve.tensor_scalar(out[:, t, :], src[:, t, :], mean[:, t:t + 1], tmp[:, t:t + 1],
                                  ALU.subtract, ALU.mult).then_inc(ready if gamma is None else plain, 1)
            if gamma is not None:
                dve.wait_ge(affine_in, 32)
                for b in range(PC, NB):
                    dve.wait_ge(plain, (b + 1) * TB)
                    affine(own, dve, b).then_inc(ready, TB)

        @block.gpsimd
        def _(pool):
            own = Steps(pool, pool_own)
            if gamma is not None:
                pool.wait_ge(affine_in, 32)
                for b in range(PC):
                    pool.wait_ge(plain, (b + 1) * TB)
                    affine(own, pool, b).then_inc(pool_ready, 1)
            if scale is not None:
                for b in range(NB):
                    v = out[:, b * TB:(b + 1) * TB, :]
                    pool.wait_ge(turned, (b + 1) * DK)
                    pool.tensor_tensor(v, v, scale[:, b * TB:(b + 1) * TB].unsqueeze(2).to_broadcast([P, TB, D]), ALU.mult)

        @block.scalar
        def _(act):
            act.wait_ge(want_root, 1)
            act.activation(var[:, :], var[:, :], ACT.Sqrt).then_inc(root, 1)
            if outT is not None:
                for b in range(NB):
                    for k in range(DK):
                        n = b * DK + k
                        act.wait_ge(turned, n + 1)
                        act.activation(outT[:, k, b * BLK:(b + 1) * BLK],
                                       ps[:, n % 4, :, :].rearrange("p q n -> p (q n)"), ACT.Copy).then_inc(turned_out, 1)

        @block.tensor
        def _(pe):
            if outT is not None:
                for b in range(NB):
                    if gamma is None:
                        pe.wait_ge(ready, (b + 1) * TB)
                    elif b < PC:
                        pe.wait_ge(pool_ready, b + 1)
                    else:
                        pe.wait_ge(ready, (b + 1 - PC) * TB)
                    for k in range(DK):
                        n = b * DK + k
                        if n >= 4:
                            pe.wait_ge(turned_out, n - 3)
                        for q in range(TB):
                            mm = pe.transpose(ps[:, n % 4, q, :], out[:, b * TB + q, k * P:(k + 1) * P], m.ident[:, :])
                        mm.then_inc(turned, 1)



def phase_degrees(nc, m):
    sem = nc.alloc_semaphore
    dve_own, root, spread, diag, copied, topped, top_turned = (
        sem(f"deg_{s}") for s in ("dve", "root", "spread", "diag", "copied", "topped", "top_turned"))
    with (
        nc.sbuf_tensor("deg_t", [P, 4, NT], F32) as t4,
        nc.sbuf_tensor("deg_diag", [P, 2, TB, P], F32) as dg,
        nc.sbuf_tensor("deg_top", [P, 2], F32) as top,
        nc.psum_tensor("deg_ps", [P, 2, BLK], F32) as ps,
        nc.psum_tensor("deg_top_ps", [P, BLK], F32) as top_ps,
        nc.Block() as block,
    ):
        @block.vector
        def _(dve):
            own = Steps(dve, dve_own)
            own.step(dve.tensor_scalar(t4[:, 0, :], m.deg[:, :], 1.0, None, ALU.max))
            own.step(dve.tensor_scalar(t4[:, 1, :], m.deg[:, :], 1.0, None, ALU.add))
            own.step(dve.tensor_scalar(t4[:, 2, :], m.deg[:, :], 1e-12, None, ALU.max))
            own.join(dve.tensor_scalar(t4[:, 3, :], m.deg[:, :], 0.0, None, ALU.is_gt))
            own.step(dve.reciprocal(m.inv_count[:, :], t4[:, 0, :]))
            dve.wait_ge(root, 1)
            own.step(dve.reciprocal(m.dinv_loop[:, :], t4[:, 1, :]))
            own.join(dve.reciprocal(t4[:, 2, :], t4[:, 2, :]))
            own.join(dve.tensor_tensor(m.dinv[:, :], t4[:, 2, :], t4[:, 3, :], ALU.mult))
            dve.tensor_reduce(top[:, 0:1], m.deg[:, :], AX.X, ALU.max).then_inc(topped, 1)
            dve.wait_ge(top_turned, 1)
            own.join(dve.tensor_reduce(top[0:1, 1:2], top_ps[0:1, 0:P], AX.X, ALU.max))
            own.join(dve.tensor_scalar(m.has_low[0:1, 0:1], top[0:1, 1:2], EXACT16, None, ALU.is_gt))
            for b in range(NB):
                if b >= 2:
                    dve.wait_ge(spread, b - 1)
                for q in range(TB):
                    t = b * TB + q
                    ins = dve.tensor_scalar(dg[:, b % 2, q, :], m.ident[:, :], m.dinv[:, t:t + 1], None, ALU.mult)
                ins.then_inc(diag, 1)

        @block.scalar
        def _(act):
            act.wait_ge(dve_own, 4)
            act.activation(t4[:, 1:3, :], t4[:, 1:3, :], ACT.Sqrt).then_inc(root, 1)
            for b in range(NB):
                act.wait_ge(spread, b + 1)
                act.activation(m.dinv_row[:, b * BLK:(b + 1) * BLK], ps[:, b % 2, :], ACT.Copy).then_inc(copied, 1)

        @block.tensor
        def _(pe):
            pe.wait_ge(topped, 1)
            pe.transpose(top_ps[0:1, 0:P], top[:, 0:1], m.ident[:, :]).then_inc(top_turned, 1)
            for b in range(NB):
                pe.wait_ge(diag, b + 1)
                if b >= 2:
                    pe.wait_ge(copied, b - 1)
                pe.matmul(ps[:, b % 2, :], m.ones[:, :], dg[:, b % 2, :, :].rearrange("p q n -> p (q n)"),
                          start=True, stop=True).then_inc(spread, 1)


def phase_transpose_weights(nc, m, mats):
    sem = nc.alloc_semaphore
    loaded, turned, copied = (sem(f"wturn_{s}") for s in ("loaded", "turned", "copied"))
    with (
        nc.sbuf_tensor("wturn_in", [P, len(mats), DK, D], F32) as w_in,
        nc.psum_tensor("wturn_ps", [P, 2, DK, D], F32) as ps,
        nc.Block() as block,
    ):
        @block.sync
        def _(sp):
            for i, (w, _o) in enumerate(mats):
                sp.dma_start(w_in[:, i, :, :], rows(w)).then_inc(loaded, 16)

        @block.tensor
        def _(pe):
            pe.wait_ge(loaded, 16 * len(mats))
            for i in range(len(mats)):
                if i >= 2:
                    pe.wait_ge(copied, i - 1)
                for ko in range(DK):
                    for ki in range(DK):
                        mm = pe.transpose(ps[:, i % 2, ki, ko * P:(ko + 1) * P], w_in[:, i, ko, ki * P:(ki + 1) * P],
                                          m.ident[:, :])
                mm.then_inc(turned, 1)

        @block.vector
        def _(dve):
            for i, (_w, out_sb) in enumerate(mats):
                dve.wait_ge(turned, i + 1)
                dve.tensor_copy(out_sb[:, :, :], ps[:, i % 2, :, :]).then_inc(copied, 1)


def phase_gather(nc, m, name, y, kind, w=None, w_self=None, bias=None):
    sem = nc.alloc_semaphore
    at_in = [sem(f"{name}_at_in{i}") for i in range(2)]
    first_in = [sem(f"{name}_first_in{c}") for c in range(NB)]
    agg_mm, agg_out, lin_mm, lin_out, bias_in, selfed, y_high, y_low, low_in, low_used = (
        sem(f"{name}_{s}") for s in ("agg_mm", "agg_out", "lin_mm", "lin_out", "bias_in", "selfed", "y_high", "y_low",
                                     "low_in", "low_used"))
    with (
        nc.sbuf_tensor(f"{name}_at", [P, 2, TB, NT, P], F16) as at,
        nc.sbuf_tensor(f"{name}_at_low", [P, TB, NT, P], F16) as at_low,
        nc.sbuf_tensor(f"{name}_y", [P, 2, NT, D], F16) as y2,
        nc.sbuf_tensor(f"{name}_agg", [P, DK, BLK], F32) as agg,
        nc.sbuf_tensor(f"{name}_self", [P, DK, BLK], F32) as own_x,
        nc.sbuf_tensor(f"{name}_bias", [P, D], F32) as bias_sb,
        nc.psum_tensor(f"{name}_ps", [P, DK, BLK], F32) as ps,
        nc.psum_tensor(f"{name}_lin", [P, TB, D], F32) as lin,
        nc.psum_tensor(f"{name}_lin2", [P, TB, D], F32) as lin2,
        nc.Block() as block,
    ):
        @block.sync
        def _(sp):
            def load_low(b):
                with sp.If(sp.value_load(m.has_low[0:1, 0:1], min_val=0, max_val=1) > 0):
                    if b:
                        sp.wait_ge(low_used, b)
                    sp.dma_start(at_low[:, :, :, :].rearrange("p q s n -> p q (s n)"),
                                 m.AT_low[b * TB:(b + 1) * TB, :, :].rearrange("t p n -> p t n")).then_inc(low_in, 16)

            if bias is not None:
                sp.dma_start(bias_sb[:, :], bias.partition_broadcast(P)).then_inc(bias_in, 16)
            for c in range(NB):
                cut = slice(c * TB, (c + 1) * TB)
                sp.dma_start(at[:, 0, :, cut, :], m.AT_high[0:TB, :, c * BLK:(c + 1) * BLK].rearrange(
                    "t p (s n) -> p t s n", n=P)).then_inc(first_in[c], 16)
            for b in range(NB):
                if b == 0:
                    load_low(b)
                    continue
                if b >= 2:
                    sp.wait_ge(agg_mm, b - 1)
                sp.dma_start(at[:, b % 2, :, :, :].rearrange("p q s n -> p q (s n)"),
                             m.AT_high[b * TB:(b + 1) * TB, :, :].rearrange("t p n -> p t n")).then_inc(at_in[b % 2], 16)
                load_low(b)

        @block.tensor
        def _(pe):
            for b in range(NB):
                if b:
                    pe.wait_ge(at_in[b % 2], 16 * (b // 2 + (b % 2)))
                    pe.wait_ge(agg_out, b)
                last = [(NT - 1, 1)]
                for s in range(NT):
                    if b == 0 and s % TB == 0:
                        pe.wait_ge(first_in[s // TB], 16)
                        pe.wait_ge(y_low, s // TB + 1)
                    for k in range(DK):
                        for part in range(2):
                            if (s, part) not in last:
                                pe.matmul(ps[:, k, :], y2[:, part, s, k * P:(k + 1) * P], at[:, b % 2, :, s, :],
                                          start=(s == 0 and part == 0), stop=False, skip_group_check=True)
                if kind == "loop":
                    for k in range(DK):
                        for q in range(TB):
                            for part in range(2):
                                pe.matmul(ps[:, k, q * P:(q + 1) * P], y2[:, part, b * TB + q, k * P:(k + 1) * P],
                                          m.half16[:, :], start=False, stop=False, skip_group_check=True)
                with pe.If(pe.value_load(m.has_low[0:1, 0:1], min_val=0, max_val=1) > 0):
                    pe.wait_ge(low_in, 16 * (b + 1))
                    for k in range(DK):
                        for s in range(NT):
                            for part in range(2):
                                mm = pe.matmul(ps[:, k, :], y2[:, part, s, k * P:(k + 1) * P], at_low[:, :, s, :],
                                               start=False, stop=False, skip_group_check=True)
                    mm.then_inc(low_used, 1)
                for k in range(DK):
                    for s, part in last:
                        mm = pe.matmul(ps[:, k, :], y2[:, part, s, k * P:(k + 1) * P], at[:, b % 2, :, s, :],
                                       start=False, stop=True, skip_group_check=True)
                mm.then_inc(agg_mm, 1)
                if kind == "keep":
                    continue
                pe.wait_ge(lin_out, b)
                if kind == "mean":
                    pe.wait_ge(selfed, b + 1)
                    for q in range(TB):
                        for k in range(DK):
                            pe.matmul(lin2[:, q, :], own_x[:, k, q * P:(q + 1) * P], w_self[:, k, :],
                                      start=(k == 0), stop=(k == DK - 1))
                pe.wait_ge(agg_out, b + 1)
                for q in range(TB):
                    for k in range(DK):
                        mm = pe.matmul(lin[:, q, :], agg[:, k, q * P:(q + 1) * P], w[:, k, :],
                                       start=(k == 0), stop=(k == DK - 1))
                mm.then_inc(lin_mm, 1)

        @block.scalar
        def _(act):
            for c in range(NB):
                act.activation(y2[:, 0, c * TB:(c + 1) * TB, :], y[:, c * TB:(c + 1) * TB, :], ACT.Copy,
                               scale=Y_SCALE).then_inc(y_high, 1)
            if kind == "keep":
                return
            for b in range(NB):
                act.wait_ge(lin_mm, b)
                if kind == "mean":
                    act.activation(own_x[:, :, :], m.xT[:, :, b * BLK:(b + 1) * BLK], ACT.Copy).then_inc(selfed, 1)
                act.wait_ge(agg_mm, b + 1)
                act.activation(agg[:, :, :], ps[:, :, :], ACT.Copy, scale=AGG_SCALE).then_inc(agg_out, 1)

        @block.vector
        def _(dve):
            for c in range(NB):
                dve.wait_ge(y_high, c + 1)
                dve.scalar_tensor_tensor(y2[:, 1, c * TB:(c + 1) * TB, :], y[:, c * TB:(c + 1) * TB, :], Y_SCALE,
                                         y2[:, 0, c * TB:(c + 1) * TB, :], ALU.mult, ALU.subtract).then_inc(y_low, 1)
            if bias is not None:
                dve.wait_ge(bias_in, 16)
            own = Steps(dve, sem(f"{name}_dve"))
            for b in range(NB):
                if kind == "keep":
                    dve.wait_ge(agg_mm, b + 1)
                    cut = slice(b * BLK, (b + 1) * BLK)
                    dve.scalar_tensor_tensor(m.xT[:, :, cut], ps[:, :, :], AGG_SCALE,
                                             m.dinv_row[:, cut].unsqueeze(1).to_broadcast([P, DK, BLK]), ALU.mult,
                                             ALU.mult).then_inc(agg_out, 1)
                    continue
                dve.wait_ge(lin_mm, b + 1)
                for q in range(TB):
                    t = b * TB + q
                    if kind == "mean":
                        own.join(dve.scalar_tensor_tensor(m.x[:, t, :], lin[:, q, :], m.inv_count[:, t:t + 1],
                                                          m.x[:, t, :], ALU.mult, ALU.add))
                        own.join(dve.tensor_tensor(m.x[:, t, :], lin2[:, q, :], m.x[:, t, :], ALU.add))
                        ins = dve.tensor_tensor(m.x[:, t, :], m.x[:, t, :], bias_sb[:, :], ALU.add)
                    else:
                        ins = dve.scalar_tensor_tensor(m.o[:, t, :], lin[:, q, :], m.dinv_loop[:, t:t + 1],
                                                       bias_sb[:, :], ALU.mult, ALU.add)
                ins.then_inc(lin_out, 1)



def softmax_steps(own, dve, exp, lg, top, tmp, T, EX):
    def wide(a):
        return a.unsqueeze(2).to_broadcast([P, T, EX])
    own.join(dve.tensor_reduce(top, lg, AX.X, ALU.max))
    own.join(dve.tensor_tensor(lg, lg, wide(top), ALU.subtract))
    exp()
    own.join(dve.tensor_reduce(tmp, lg, AX.X, ALU.add))
    own.join(dve.reciprocal(tmp, tmp))
    own.join(dve.tensor_tensor(lg, lg, wide(tmp), ALU.mult))


def top2_steps(own, dve, exp, lg, s, no, wd, T, EX):
    def wide(a):
        return a.unsqueeze(2).to_broadcast([P, T, EX])

    def pick(vals, top, at, hot):
        own.join(dve.tensor_reduce(top, vals, AX.X, ALU.max))
        own.join(dve.tensor_tensor(hot, vals, wide(top), ALU.is_equal))
        own.join(dve.tensor_tensor(hot, hot, no, ALU.mult))
        own.join(dve.tensor_reduce(at, hot, AX.X, ALU.min))
        own.join(dve.tensor_tensor(hot, no, wide(at), ALU.is_equal))

    pick(lg, s.m1, s.i1, s.hot1)
    own.join(dve.scalar_tensor_tensor(s.rest, s.hot1, -BIG, lg, ALU.mult, ALU.add))
    pick(s.rest, s.m2, s.i2, s.hot2)
    own.join(dve.tensor_tensor(s.d, s.m2, s.m1, ALU.subtract))
    exp()
    own.join(dve.tensor_scalar(s.w1, s.d, 1.0, None, ALU.add))
    own.join(dve.reciprocal(s.w1, s.w1))
    own.join(dve.tensor_tensor(s.w2, s.w1, s.d, ALU.mult))
    own.join(dve.tensor_tensor(s.hot1, s.hot1, wide(s.w1), ALU.mult))
    own.join(dve.tensor_tensor(s.hot2, s.hot2, wide(s.w2), ALU.mult))
    own.join(dve.tensor_tensor(wd, s.hot1, s.hot2, ALU.add))


def weight_views(m, widths):
    flat, at, views = m.xn[:, :, :].rearrange("p t d -> p (t d)"), 0, []
    for w_in, w_out in zip([D] + widths, widths + [D]):
        size = 2 * (w_in // P) * w_out
        views.append(flat[:, at:at + size].rearrange("p (u k n) -> p u k n", u=2, k=w_in // P))
        at += size
    return views


def phase_route(nc, m, name, kind, EX, wr, br, bout, dest, base, wr1=None, br1=None, ahead=None):
    sem = nc.alloc_semaphore
    T = 1 if kind == "mean" else NT
    loaded, dve_own, act_own, want_exp, exped, pe_own, pe_hid, act_hid, w_ready, mixed, added, w_turned = (
        sem(f"{name}_{s}") for s in ("loaded", "dve", "act", "want_exp", "exped", "pe", "pe_hid", "act_hid",
                                     "w_ready", "mixed", "added", "w_turned"))
    ahead_in = sem(f"{name}_ahead_in")
    KR = 1 if kind == "mlp" else DK
    s = Mem()
    with ExitStack() as ctx:
        sb = lambda n, shape, dt=F32: ctx.enter_context(nc.sbuf_tensor(f"{name}_{n}", shape, dt))
        wr_sb = sb("wr", [P, KR, EX])
        br_sb = sb("br", [P, EX])
        bo_sb = sb("bo", [P, D])
        lg = sb("lg", [P, T, EX])
        s.m1, s.i1, s.m2, s.i2, s.d, s.w1, s.w2, s.tmp = (
            sb(n, [P, T])[:, :] for n in ("m1", "i1", "m2", "i2", "d", "w1", "w2", "tmp"))
        s.hot1, s.hot2, s.rest = (sb(n, [P, T, EX])[:, :, :] for n in ("hot1", "hot2", "rest"))
        wT = sb("wT", [P, NT, P])
        mean = sb("mean", [P, DK])
        mean_w = sb("mean_w", [P, DK, P])
        w1_sb = sb("w_hid", [P, DK, P])
        b1_sb = sb("b_hid", [P, 1])
        hid = sb("hid", [P, NP]) if kind == "mlp" else None
        psl = ctx.enter_context(nc.psum_tensor(f"{name}_psl", [P, NT, EX], F32))
        psh = ctx.enter_context(nc.psum_tensor(f"{name}_psh", [P, 2, BLK], F32))
        pst = ctx.enter_context(nc.psum_tensor(f"{name}_pst", [P, 2, TB, P], F32))
        psm = ctx.enter_context(nc.psum_tensor(f"{name}_psm", [P, 2, BLK], F32))
        block = ctx.enter_context(nc.Block())
        nload = 5 if kind == "mlp" else 3
        no = m.expert_no[:, 0:T, 0:EX]

        @block.sync
        def _(sp):
            sp.dma_start(wr_sb[:, :, :], rows(wr)).then_inc(loaded, 16)
            sp.dma_start(br_sb[:, :], br.partition_broadcast(P)).then_inc(loaded, 16)
            sp.dma_start(bo_sb[0:EX, :], bout).then_inc(loaded, 16)
            if kind == "mlp":
                sp.dma_start(w1_sb[:, :, :], rows(wr1)).then_inc(loaded, 16)
                sp.dma_start(b1_sb[:, :], per_partition(br1), allow_slow_non_contiguous=True).then_inc(loaded, 16)
            if ahead is not None:
                widths, mats = ahead
                for view, w in zip(weight_views(m, widths), mats):
                    sp.dma_start(view[:, 0, :, :], w(0)).then_inc(ahead_in, 16)
                sp.wait_ge(ahead_in, 16 * len(mats))

        @block.tensor
        def _(pe):
            pe.wait_ge(loaded, 16 * nload)
            if kind == "mean":
                pe.wait_ge(w_ready, 1)
                for k in range(DK):
                    mm = pe.matmul(psl[:, 0, :], mean_w[:, k, :], wr_sb[:, k, :], start=(k == 0), stop=(k == DK - 1))
                mm.then_inc(pe_own, 1)
            elif kind == "mlp":
                for b in range(NB):
                    if b >= 2:
                        pe.wait_ge(act_hid, b - 1)
                    for k in range(DK):
                        mm = pe.matmul(psh[:, b % 2, :], w1_sb[:, k, :], m.xT[:, k, b * BLK:(b + 1) * BLK],
                                       start=(k == 0), stop=(k == DK - 1))
                    mm.then_inc(pe_hid, 1)
                for t in range(NT):
                    pe.wait_ge(act_hid, t // TB + 1)
                    mm = pe.matmul(psl[:, t, :], hid[:, t * P:(t + 1) * P], wr_sb[:, 0, :], start=True, stop=True)
                mm.then_inc(pe_own, 1)
            else:
                for t in range(NT):
                    for k in range(DK):
                        mm = pe.matmul(psl[:, t, :], m.xT[:, k, t * P:(t + 1) * P], wr_sb[:, k, :],
                                       start=(k == 0), stop=(k == DK - 1))
                mm.then_inc(pe_own, 1)
            pe.wait_ge(w_ready, 2 if kind == "mean" else 1)
            for b in range(NB):
                if b >= 2:
                    pe.wait_ge(w_turned, b - 1)
                for q in range(TB):
                    mm = pe.transpose(pst[0:EX, b % 2, q, :], m.wd[:, b * TB + q, 0:EX], m.ident[:, :])
                mm.then_inc(pe_own, 1)
            for c in range(NT // 2):
                pe.wait_ge(w_turned, 2 * c // TB + 1)
                if c >= 2:
                    pe.wait_ge(added, c - 1)
                for i in range(2):
                    mm = pe.matmul(psm[:, c % 2, i * D:(i + 1) * D], wT[0:EX, 2 * c + i, :], bo_sb[0:EX, :],
                                   start=True, stop=True)
                mm.then_inc(mixed, 1)

        @block.scalar
        def _(act):
            if kind == "mlp":
                act.wait_ge(loaded, 16 * nload)
                for b in range(NB):
                    act.wait_ge(pe_hid, b + 1)
                    act.activation(hid[:, b * BLK:(b + 1) * BLK], psh[:, b % 2, :], ACT.Relu,
                                   bias=b1_sb[:, 0:1]).then_inc(act_hid, 1)
            exps = {"mean": [lg, lg, s.d], "mlp": [lg, s.d], "top": [s.d], "dense": [lg]}[kind]
            for i, what in enumerate(exps):
                ap = what if what is s.d else lg[:, :, :]
                act.wait_ge(want_exp, i + 1)
                act.activation(ap, ap, ACT.Exp).then_inc(exped, 1)
            for b in range(NB):
                act.wait_ge(pe_own, 1 + b + 1)
                act.activation(wT[0:EX, b * TB:(b + 1) * TB, :], pst[0:EX, b % 2, :, :], ACT.Copy).then_inc(w_turned, 1)

        @block.vector
        def _(dve):
            own = Steps(dve, dve_own)
            asked = [0]

            def exp():
                dve.sem_inc(want_exp, 1)
                asked[0] += 1
                dve.wait_ge(exped, asked[0])

            L = lg[:, :, :]
            if kind == "mean":
                for k in range(DK):
                    own.join(dve.tensor_reduce(mean[:, k:k + 1], m.xT[:, k, 0:N], AX.X, ALU.add))
                own.join(dve.tensor_scalar(mean[:, :], mean[:, :], 1.0 / N, None, ALU.mult))
                own.join(dve.tensor_copy(mean_w[:, :, :], mean[:, :].unsqueeze(2).to_broadcast([P, DK, P])))
                dve.sem_inc(w_ready, 1)
            dve.wait_ge(loaded, 16 * nload)
            dve.wait_ge(pe_own, 1)
            own.join(dve.tensor_tensor(L, psl[:, 0:T, :], br_sb[:, :].unsqueeze(1).to_broadcast([P, T, EX]), ALU.add))
            if kind != "top":
                softmax_steps(own, dve, exp, L, s.m1, s.tmp, T, EX)
            if kind == "mean":
                capacity = float(-(-N * 5 // (4 * EX)))
                own.join(dve.tensor_scalar(s.rest, L, float(N), None, ALU.mult))
                own.join(dve.reciprocal(s.rest, s.rest))
                own.join(dve.tensor_scalar(s.rest, s.rest, capacity, 1.0, ALU.mult, ALU.min))
                own.join(dve.tensor_tensor(L, L, s.rest, ALU.mult))
                softmax_steps(own, dve, exp, L, s.m1, s.tmp, T, EX)
            wd = m.wd[:, 0:T, 0:EX]
            if kind == "dense":
                own.join(dve.tensor_copy(wd, L))
            else:
                top2_steps(own, dve, exp, L, s, no, wd, T, EX)
            if kind == "mean":
                own.join(dve.tensor_copy(m.wd[:, 1:NT, 0:EX], m.wd[:, 0:1, 0:EX].to_broadcast([P, NT - 1, EX])))
                own.step(dve.tensor_copy(m.pair_w[:, 0:1], s.w1))
                own.step(dve.tensor_copy(m.pair_w[:, 1:2], s.w2))
                for i, at in enumerate((s.i1, s.i2)):
                    for c in range(DK):
                        own.join(dve.tensor_scalar(s.tmp, at, 8.0, float(D), ALU.add, ALU.mult))
                        own.join(dve.tensor_scalar(s.tmp, s.tmp, m.part_no[:, 0:1], float(c * P), ALU.add, ALU.add))
                        own.join(dve.tensor_copy(m.w1_rows[:, i, c:c + 1], s.tmp))
                    for c in range(FH // P):
                        own.join(dve.tensor_scalar(s.tmp, at, 8.0, float(FH), ALU.add, ALU.mult))
                        own.join(dve.tensor_scalar(s.tmp, s.tmp, m.part_no[:, 0:1], float(c * P), ALU.add, ALU.add))
                        own.join(dve.tensor_copy(m.w2_rows[:, i, c:c + 1], s.tmp))
            dve.sem_inc(w_ready, 1)
            for c in range(NT // 2):
                dve.wait_ge(mixed, c + 1)
                dve.tensor_tensor(dest[:, 2 * c:2 * c + 2, :], psm[:, c % 2, :].rearrange("p (t d) -> p t d", t=2),
                                  base[:, 2 * c:2 * c + 2, :], ALU.add).then_inc(added, 1)



def phase_experts(nc, m, name, EX, func, widths, mats, biases, dest, weight=None, picked=False, bn=None,
                  loaded=False):
    sem = nc.alloc_semaphore
    NH = len(widths)
    FT = [w // P for w in widths]
    KT = [DK] + FT
    NL = NH + 1
    YC, HC = TB + 1, FT[-1] + 1
    w_in = [sem(f"{name}_w_in{u}") for u in range(2)]
    h_mm = [sem(f"{name}_h{i}_mm") for i in range(NH)]
    h_act = [sem(f"{name}_h{i}_act") for i in range(NH)]
    y_mm, y_add, bn_in, bn_dve, bn_root = (sem(f"{name}_{s}") for s in ("y_mm", "y_add", "bn_in", "bn_dve", "bn_root"))
    nload = NL + NH
    bn_kept = sem(f"{name}_bn_kept")
    x_high, x_low = sem(f"{name}_x_high"), sem(f"{name}_x_low")
    w_high, w_low = ([sem(f"{name}_{s}{u}") for u in range(2)] for s in ("w_high", "w_low"))
    h_low = [sem(f"{name}_h{i}_low") for i in range(NH)]
    if picked:
        nload = DK + 2 * FT[0]
    with ExitStack() as ctx:
        sb = lambda n, shape, dt=F32: ctx.enter_context(nc.sbuf_tensor(f"{name}_{n}", shape, dt))
        outs = widths + [D]
        xT_flat = m.xT[:, :, :].rearrange("p k n -> p (k n)")
        w_sb, h_sb, h_at = weight_views(m, widths), [], 0
        for i in range(NH):
            size = FT[i] * BLK
            h_sb.append(xT_flat[:, h_at:h_at + size].rearrange("p (f n) -> p f n", f=FT[i]))
            h_at += size
        b_sb = [sb(f"b{i}", [P, 2, 2, FT[i]]) for i in range(NH)]
        x_parts = [sb(f"x_{s}", [P, DK, NP], F32R) for s in ("high", "low")]
        w_parts = [[sb(f"w{i}_{s}", [P, 2, KT[i], outs[i]], F32R) for s in ("high", "low")] for i in range(NL)]
        h_parts = [[sb(f"h{i}_{s}", [P, 2, FT[i], BLK], F32R) for s in ("high", "low")] for i in range(NH)]
        PARTS = ((0, 0), (0, 1), (1, 0))

        def width(b):
            return min(BLK, N - b * BLK)

        if bn is not None:
            v_rows = [sb(f"vr{i}", [EX * FT[i], 5, P]) for i in range(NH)]
            v_sb = [sb(f"v{i}", [P, 5, EX * FT[i]]) for i in range(NH)]
            kept = [nc.dram_tensor(f"{name}_kept{i}", (P, 2, EX * FT[i]), F32, kind="Internal").ap() for i in range(NH)]
        h_ps = [ctx.enter_context(nc.psum_tensor(f"{name}_hps{i}", [P, FT[i], BLK], F32)) for i in range(NH)]
        y_ps = ctx.enter_context(nc.psum_tensor(f"{name}_yps", [P, TB, BLK], F32))
        block = ctx.enter_context(nc.Block())
        per_pair = 2 * NB
        pairs = EX // 2

        def load_pair(eng, e2):
            for u in range(2):
                e = e2 * 2 + u
                if picked:
                    for k in range(DK):
                        eng.indirect_dma_start(w_sb[0][:, u, k, :], None, mats[0], bass.IndirectOffsetOnAxis(
                            ap=m.w1_rows[:, u, k:k + 1], axis=0)).then_inc(w_in[u], 16)
                    for k in range(FT[0]):
                        at = bass.IndirectOffsetOnAxis(ap=m.w2_rows[:, u, k:k + 1], axis=0)
                        eng.indirect_dma_start(w_sb[1][:, u, k, :], None, mats[1], at).then_inc(w_in[u], 16)
                        eng.indirect_dma_start(b_sb[0][:, u, 0, k:k + 1], None, biases[0], at).then_inc(w_in[u], 16)
                    continue
                if not isinstance(e2, int) or e2:
                    eng.wait_ge(y_mm, (e - 1) * (NB * TB) + YC)
                if loaded and isinstance(e, int) and e == 0:
                    eng.sem_inc(w_in[0], 16 * NL)
                else:
                    for i in range(NL):
                        eng.dma_start(w_sb[i][:, u, :, :], mats[i](e)).then_inc(w_in[u], 16)
                for i in range(NH):
                    if bn is None:
                        eng.dma_start(b_sb[i][:, u, 0, :], biases[i](e), allow_slow_non_contiguous=True).then_inc(w_in[u], 16)
                    else:
                        eng.dma_start(b_sb[i][:, u, :, :], kept[i][:, :, ds(e * FT[i], FT[i])]).then_inc(w_in[u], 16)

        first_low = 1

        def low_weights(eng, e2, u, lo, hi=NL):
            eng.wait_ge(w_high[u], e2 * NL + hi)
            for i in range(lo, hi):
                eng.tensor_tensor(w_parts[i][1][:, u, :, :], w_sb[i][:, u, :, :], w_parts[i][0][:, u, :, :].bitcast(F32),
                                  ALU.subtract).then_inc(w_low[u], 1)

        @block.sync
        def _(sp):
            if picked:
                return
            if bn is not None:
                for i in range(NH):
                    for j, v in enumerate((biases[i],) + bn[i]):
                        sp.dma_start(v_rows[i][:, j, :], v.rearrange("e (f p) -> (e f) p", p=P)).then_inc(bn_in, 16)
                sp.wait_ge(bn_dve, 3)
                for i in range(NH):
                    sp.dma_start(kept[i], v_sb[i][:, 0:2, :]).then_inc(bn_kept, 16)
                sp.wait_ge(bn_kept, 16 * NH)
            load_pair(sp, 0)
            if pairs > 1:
                with sp.Fori(1, pairs) as e2:
                    load_pair(sp, e2)

        @block.gpsimd
        def _(pool):
            if picked:
                load_pair(pool, 0)

            low_weights(pool, 0, 0, first_low)
            low_weights(pool, 0, 1, 0)
            if pairs > 1:
                with pool.Fori(1, pairs) as e2:
                    for u in range(2):
                        low_weights(pool, e2, u, 0)

        @block.tensor
        def _(pe):
            def layer0(e2, v):
                u, b = v // NB, v % NB
                n = e2 * per_pair + v
                if b == 0:
                    pe.wait_ge(w_low[u], (e2 + 1) * NL)
                if u == 0:
                    pe.wait_ge(x_low, b + 1)
                for f in range(FT[0]):
                    pe.wait_ge(h_act[0], n * FT[0] + (f + 1))
                    for k in range(DK):
                        for j, (w, x) in enumerate(PARTS):
                            mm = pe.matmul(h_ps[0][:, f, 0:width(b)], w_parts[0][w][:, u, k, f * P:(f + 1) * P],
                                           x_parts[x][:, k, b * BLK:b * BLK + width(b)],
                                           start=(k == 0 and j == 0), stop=(k == DK - 1 and j == 2))
                    mm.then_inc(h_mm[0], 1)

            def layer1(e2, v):
                u, b = v // NB, v % NB
                n = e2 * per_pair + v
                pe.wait_ge(h_low[0], (n + 2) * FT[0])
                for f in range(FT[1]):
                    pe.wait_ge(h_act[1], n * FT[1] + (f + 1))
                    for k in range(FT[0]):
                        for j, (w, h) in enumerate(PARTS):
                            mm = pe.matmul(h_ps[1][:, f, 0:width(b)], w_parts[1][w][:, u, k, f * P:(f + 1) * P],
                                           h_parts[0][h][:, v % 2, k, 0:width(b)],
                                           start=(k == 0 and j == 0), stop=(k == FT[0] - 1 and j == 2))
                    mm.then_inc(h_mm[1], 1)

            def last(e2, v):
                u, b = v // NB, v % NB
                n = e2 * per_pair + v
                pe.wait_ge(h_low[-1], (n + 2) * FT[-1])
                for q in range(TB):
                    tokens = min(P, width(b) - q * P)
                    pe.wait_ge(y_add, n * TB + (q + 1))
                    for k in range(FT[-1]):
                        for j, (h, w) in enumerate(PARTS):
                            mm = pe.matmul(y_ps[0:tokens, q, 0:D], h_parts[-1][h][:, v % 2, k, q * P:q * P + tokens],
                                           w_parts[-1][w][:, u, k, :],
                                           start=(k == 0 and j == 0), stop=(k == FT[-1] - 1 and j == 2))
                    mm.then_inc(y_mm, 1)

            def pair(e2, more):
                for v in range(per_pair):
                    if NH == 2:
                        layer1(e2, v)
                    if v + 1 < per_pair:
                        layer0(e2, v + 1)
                    elif more:
                        layer0(e2 + 1, 0)
                    last(e2, v)

            if bn is not None:
                pe.wait_ge(bn_in, 16 * 5 * NH)
                for i in range(NH):
                    R = EX * FT[i]
                    for j in range(5):
                        pe.transpose(y_ps[:, i, j * R:(j + 1) * R], v_rows[i][:, j, :], m.ident[0:R, 0:R]).then_inc(bn_root, 1)
                pe.wait_ge(bn_dve, 1)
            pe.sem_inc(y_mm, YC)
            if NH == 2:
                pe.sem_inc(h_mm[1], HC)
            layer0(0, 0)
            if pairs > 1:
                with pe.Fori(0, pairs - 1) as e2:
                    pair(e2, True)
            pair(pairs - 1, False)

        @block.scalar
        def _(act):
            for i in range(NH):
                act.sem_inc(h_act[i], FT[i])
            if bn is not None:
                act.wait_ge(bn_dve, 2)
                for i in range(NH):
                    act.activation(v_sb[i][:, 4, :], v_sb[i][:, 4, :], ACT.Sqrt).then_inc(bn_root, 1)

            def hidden(i, e2, v):
                u, b = v // NB, v % NB
                n = e2 * per_pair + v
                if i == NH - 1:
                    act.wait_ge(y_mm, n * TB + (YC - TB))
                else:
                    act.wait_ge(h_mm[i + 1], n * FT[i + 1] + (HC - FT[i + 1]))
                if b == 0:
                    act.wait_ge(w_in[u], (e2 + 1) * (16 * nload))
                for f in range(FT[i]):
                    act.wait_ge(h_mm[i], n * FT[i] + (f + 1 + (HC if i else 0)))
                    bias = b_sb[i][:, u, 0, f:f + 1]
                    scale = 1.0 if bn is None else b_sb[i][:, u, 1, f:f + 1]
                    act.wait_ge(h_low[i], n * FT[i] + (f + 1))
                    w = width(b)
                    act.activation(h_sb[i][:, f, 0:w], h_ps[i][:, f, 0:w], func, bias=bias, scale=scale)
                    act.activation(h_parts[i][0][:, v % 2, f, 0:w], h_ps[i][:, f, 0:w], func, bias=bias,
                                   scale=scale).then_inc(h_act[i], 1)

            def high_weights(e2, u):
                act.wait_ge(w_in[u], (e2 + 1) * (16 * nload))
                for i in range(NL):
                    act.activation(w_parts[i][0][:, u, :, :], w_sb[i][:, u, :, :], ACT.Copy).then_inc(w_high[u], 1)

            def high_x(b):
                cut = slice(b * BLK, (b + 1) * BLK)
                act.activation(x_parts[0][:, :, cut], m.xT[:, :, cut], ACT.Copy).then_inc(x_high, 1)

            def pair(e2, more):
                for v in range(per_pair):
                    if NH == 2:
                        hidden(1, e2, v)
                    if v + 1 < per_pair:
                        hidden(0, e2, v + 1)
                    elif more:
                        hidden(0, e2 + 1, 0)
                    if v == 1:
                        high_weights(e2, 1)
                    elif v == NB + 1 and more:
                        high_weights(e2 + 1, 0)

            high_weights(0, 0)
            high_x(0)
            for b in range(1, NB):
                high_x(b)
            act.wait_ge(x_low, NB)
            hidden(0, 0, 0)
            if pairs > 1:
                with act.Fori(0, pairs - 1) as e2:
                    pair(e2, True)
            pair(pairs - 1, False)

        @block.vector
        def _(dve):
            dve.sem_inc(y_add, TB)
            for i in range(NH):
                dve.sem_inc(h_low[i], FT[i])
            own = Steps(dve, sem(f"{name}_dve"))
            if bn is not None:
                dve.wait_ge(bn_root, 5 * NH)
                for i in range(NH):
                    R = EX * FT[i]
                    own.join(dve.tensor_copy(v_sb[i][:, :, :].rearrange("p j r -> p (j r)"), y_ps[:, i, 0:5 * R]))
                dve.sem_inc(bn_dve, 1)
                for i in range(NH):
                    own.join(dve.tensor_scalar(v_sb[i][:, 4, :], v_sb[i][:, 4, :], 1e-3, None, ALU.add))
                dve.sem_inc(bn_dve, 1)
                dve.wait_ge(bn_root, 6 * NH)
                for i in range(NH):
                    b_, g_, be_, mu_, sd = (v_sb[i][:, j, :] for j in range(5))
                    own.join(dve.reciprocal(sd, sd))
                    own.join(dve.tensor_tensor(g_, g_, sd, ALU.mult))
                    own.join(dve.tensor_tensor(b_, b_, mu_, ALU.subtract))
                    own.join(dve.tensor_tensor(b_, b_, g_, ALU.mult))
                    own.join(dve.tensor_tensor(b_, b_, be_, ALU.add))
                dve.sem_inc(bn_dve, 1)

            low_weights(dve, 0, 0, 0, first_low)
            for b in range(NB):
                cut = slice(b * BLK, (b + 1) * BLK)
                dve.wait_ge(x_high, b + 1)
                dve.tensor_tensor(x_parts[1][:, :, cut], m.xT[:, :, cut], x_parts[0][:, :, cut].bitcast(F32),
                                  ALU.subtract).then_inc(x_low, 1)

            def low(i, e2, v):
                n = e2 * per_pair + v
                for f in range(FT[i]):
                    dve.wait_ge(h_act[i], (n + 1) * FT[i] + (f + 1))
                    w = width(v % NB)
                    dve.tensor_tensor(h_parts[i][1][:, v % 2, f, 0:w], h_sb[i][:, f, 0:w],
                                      h_parts[i][0][:, v % 2, f, 0:w].bitcast(F32), ALU.subtract).then_inc(h_low[i], 1)

            def pair(e2, more):
                for v in range(per_pair):
                    u, b = v // NB, v % NB
                    n = e2 * per_pair + v
                    if NH == 2:
                        low(1, e2, v)
                    if v + 1 < per_pair:
                        low(0, e2, v + 1)
                    elif more:
                        low(0, e2 + 1, 0)
                    for q in range(TB):
                        t = b * TB + q
                        dve.wait_ge(y_mm, n * TB + (q + 1 + YC))
                        tokens = min(P, width(b) - q * P)
                        if picked:
                            w = m.pair_w[0:tokens, u:u + 1]
                        elif weight is None:
                            w = m.ones[0:tokens, 0:1]
                        else:
                            w = weight[0:tokens, t, ds(e2 * 2 + u, 1)]
                        dve.scalar_tensor_tensor(dest[0:tokens, t, :], y_ps[0:tokens, q, 0:D], w, dest[0:tokens, t, :], ALU.mult,
                                                 ALU.add).then_inc(y_add, 1)

            low(0, 0, 0)
            if pairs > 1:
                with dve.Fori(0, pairs - 1) as e2:
                    pair(e2, True)
            pair(pairs - 1, False)


def phase_add_row(nc, m, name, row):
    sem = nc.alloc_semaphore
    row_in = sem(f"{name}_in")
    with nc.sbuf_tensor(f"{name}_row", [P, D], F32) as r, nc.Block() as block:
        @block.sync
        def _(sp):
            sp.dma_start(r[:, :], row.partition_broadcast(P)).then_inc(row_in, 16)

        @block.vector
        def _(dve):
            dve.wait_ge(row_in, 16)
            dve.tensor_tensor(m.x[:, :, :], m.x[:, :, :], r[:, :].unsqueeze(1).to_broadcast([P, NT, D]), ALU.add)



def phase_attention(nc, m, W, Wl, Wr, b):
    H, DO = 4, 64
    DA = DO + 1
    QN = NT // 4
    sem = nc.alloc_semaphore
    w_in, xl_mm, xl_out, xl_done, wide_done, own_sem, el_mm, el_out, ask, told = (
        sem(f"att_{n}") for n in ("w_in", "xl_mm", "xl_out", "xl_done", "wide_done", "dve", "el_mm", "el_out", "ask", "told"))
    gained, scored_d, scored_p, o_mm, o_out, o_turn, fin_done, min_done, exp_done, tail = (
        sem(f"att_{n}") for n in ("gained", "scored_d", "scored_p", "o_mm", "o_out", "o_turn", "fin", "min", "exp", "tail"))
    a_in = [sem(f"att_a_in{i}") for i in range(2)]
    with ExitStack() as ctx:
        def sb(n, shape, dt=F32):
            return ctx.enter_context(nc.sbuf_tensor(f"att_{n}", shape, dt))

        w_sb = sb("w", [P, DK, DO])
        wlr = sb("wlr", [DO, 2, H])
        wl_wide = sb("wl_wide", [DO, H, P])
        xlT = sb("xlT", [DO, NP])
        xl1 = sb("xl1", [P, NT, DA])
        xF = sb("xF", [P, NT, H, DA])
        e_tok = sb("e_tok", [P, NT, 2, H])
        F_src, F_dst, G_dst = sb("F_src", [P, NT, H]), sb("F_dst", [P, NT, H]), sb("G_dst", [P, NT, H])
        top = sb("top", [P, H])
        G_src = sb("G_src", [P, H, NP])
        a_sb = m.xT[:, :, :].rearrange("p a (t n) -> p a t n", t=QN)
        gain = m.o[:, 0:4 * H, :].rearrange("p (a h c) d -> p a h (c d)", a=2, h=H)
        S = m.xn[:, 0:4 * H, :].rearrange("p (a h c) d -> p a h (c d)", a=2, h=H)
        oT = sb("oT", [DA, H, BLK])
        bias = sb("bias", [P, DO])
        fin = sb("fin", [P, H, DO])
        neg = sb("neg", [P, H, DO])
        rs = sb("rs", [P, 2, H])
        ps = ctx.enter_context(nc.psum_tensor("att_ps", [P, 8, BLK], F32))

        with nc.Block() as block:
            @block.sync
            def _(sp):
                sp.dma_start(w_sb[:, :, :], rows(W)).then_inc(w_in, 16)
                for i, w in enumerate((Wl, Wr)):
                    sp.dma_start(wlr[:, i, :], w.rearrange("h d -> d h"), allow_slow_non_contiguous=True).then_inc(w_in, 16)
                sp.dma_start(bias[:, :], b.partition_broadcast(P)).then_inc(w_in, 16)

            @block.tensor
            def _(pe):
                pe.wait_ge(w_in, 64)
                for c in range(NB):
                    if c >= 2:
                        pe.wait_ge(xl_out, c - 1)
                    for k in range(DK):
                        mm = pe.matmul(ps[0:DO, c % 2, :], w_sb[:, k, :], m.xT[:, k, c * BLK:(c + 1) * BLK],
                                       start=(k == 0), stop=(k == DK - 1))
                    mm.then_inc(xl_mm, 1)
                pe.wait_ge(wide_done, 1)
                for h in range(H):
                    for c in range(NB):
                        n = h * NB + c
                        pe.wait_ge(xl_out, c + 1)
                        if n >= 2:
                            pe.wait_ge(el_out, n - 1)
                        pe.matmul(ps[:, 6 + n % 2, :], wl_wide[:, h, :], xlT[:, c * BLK:(c + 1) * BLK],
                                  start=True, stop=True).then_inc(el_mm, 1)
                for t in range(NT):
                    pe.transpose(ps[:, 2 + t // 8, (t % 8) * DO:(t % 8 + 1) * DO], xlT[:, t * P:(t + 1) * P],
                                 m.ident[0:DO, 0:DO])
                    mm = pe.matmul(ps[:, 5, t * 2 * H:(t + 1) * 2 * H], xlT[:, t * P:(t + 1) * P],
                                   wlr[:, :, :].rearrange("p i h -> p (i h)"), start=True, stop=True)
                mm.then_inc(xl_done, 1)

            @block.scalar
            def _(act):
                for c in range(NB):
                    act.wait_ge(xl_mm, c + 1)
                    act.activation(xlT[:, c * BLK:(c + 1) * BLK], ps[0:DO, c % 2, :], ACT.Copy).then_inc(xl_out, 1)
                for h in range(H):
                    for c in range(NB):
                        act.wait_ge(el_mm, h * NB + c + 1)
                        act.activation(G_src[:, h, c * BLK:(c + 1) * BLK], ps[:, 6 + (h * NB + c) % 2, :],
                                       ACT.Copy).then_inc(el_out, 1)
                for i, v in enumerate((G_dst[:, :, :], F_dst[:, :, :], F_src[:, :, :])):
                    act.wait_ge(ask, i + 1)
                    act.activation(v, v, ACT.Exp).then_inc(told, 1)
                for h in range(H):
                    act.wait_ge(ask, 4 + h)
                    act.activation(G_src[:, h, :], G_src[:, h, :], ACT.Exp).then_inc(told, 1)

            @block.vector
            def _(dve):
                own = Steps(dve, own_sem)

                def wide(v):
                    return v.unsqueeze(1).to_broadcast([P, NT, H])
                dve.wait_ge(w_in, 64)
                dve.tensor_copy(wl_wide[:, :, :], wlr[:, 0, :].unsqueeze(2).to_broadcast([DO, H, P])).then_inc(wide_done, 1)
                own.step(dve.memset(xl1[:, :, DO:DA], 1.0))
                for h in range(H):
                    dve.wait_ge(el_out, (h + 1) * NB)
                    own.step(dve.tensor_reduce(top[:, h:h + 1], G_src[:, h, 0:N], AX.X, ALU.max))
                dve.wait_ge(xl_done, 1)
                own.step(dve.tensor_copy(xl1[:, 0:16, 0:DO], ps[:, 2:4, :].rearrange("p a (t d) -> p (a t) d", d=DO)))
                own.step(dve.tensor_copy(xl1[:, 16:NT, 0:DO], ps[:, 4, 0:(NT - 16) * DO].rearrange("p (t d) -> p t d", d=DO)))
                own.join(dve.tensor_copy(e_tok[:, :, :, :], ps[:, 5, 0:NT * 2 * H].rearrange("p (t i h) -> p t i h", i=2, h=H)))
                own.join(dve.tensor_tensor(e_tok[:, :, 1, :], e_tok[:, :, 1, :], wide(top[:, :]), ALU.add))
                own.join(dve.tensor_tensor(e_tok[:, :, 0, :], e_tok[:, :, 0, :], wide(top[:, :]), ALU.subtract))
                dve.tensor_scalar(G_dst[:, :, :], e_tok[:, :, 1, :], 0.8, EXP_TOP, ALU.mult, ALU.min).then_inc(ask, 1)
                dve.tensor_scalar(F_dst[:, :, :], e_tok[:, :, 1, :], 0.2, EXP_TOP, ALU.mult, ALU.min).then_inc(ask, 1)
                dve.tensor_scalar(F_src[:, :, :], e_tok[:, :, 0, :], 0.2, EXP_TOP, ALU.mult, ALU.min).then_inc(ask, 1)
                for h in range(H):
                    own.join(dve.tensor_scalar(G_src[:, h, :], G_src[:, h, :], top[:, h:h + 1], 0.8, ALU.subtract, ALU.mult))
                    dve.tensor_scalar(G_src[:, h, :], G_src[:, h, :], EXP_TOP, None, ALU.min).then_inc(ask, 1)
                dve.wait_ge(told, 2)
                for h in range(H):
                    dve.tensor_tensor(xF[:, :, h, :], xl1[:, :, :], F_dst[:, :, h:h + 1].to_broadcast([P, NT, DA]), ALU.mult)

        with nc.Block() as block:
            @block.sync
            def _(sp):
                with sp.Fori(0, NB) as c:
                    for i in range(4):
                        sp.wait_ge(scored_d, c * NT + (i * QN + 1))
                        sp.wait_ge(scored_p, c * NT + (i * QN + 1))
                        sp.dma_start(a_sb[:, i % 2, :, :],
                                     m.A[i * QN:(i + 1) * QN, :, ds(c * BLK, BLK)].rearrange("t p n -> p t n")
                                     ).then_inc(a_in[i % 2], 16)

            def score(eng, c, s, lo, hi, scored):
                if s % QN == 0:
                    eng.wait_ge(a_in[s // QN % 2], c * 32 + 16 * (s // QN // 2 + 1))
                eng.tensor_tensor(S[:, s % 2, lo:hi, :], gain[:, s % 2, lo:hi, :],
                                  a_sb[:, s // QN % 2, s % QN, :].unsqueeze(1).to_broadcast([P, hi - lo, BLK]),
                                  ALU.mult).then_inc(scored, 1)

            HD = 2

            @block.vector
            def _(dve):
                dve.sem_inc(scored_d, QN + 1)
                dve.sem_inc(fin_done, 1)

                def gains(c, s):
                    dve.wait_ge(scored_p, c * NT + (s + QN))
                    dve.wait_ge(scored_d, c * NT + (s + QN))
                    for h in reversed(range(H)):
                        dve.tensor_scalar(gain[:, s % 2, h, :], G_src[:, h, ds(c * BLK, BLK)], G_dst[:, s, h:h + 1], 1.0,
                                          ALU.mult, ALU.max).then_inc(gained, 1)

                def finish(c, q):
                    own = Steps(dve, tail, base=(c * TB + q) * 7)
                    j = c * TB + q
                    dve.wait_ge(o_turn, j + 1)
                    o = ps[:, 4 + q % 2, 0:H * DA].rearrange("p (h d) -> p h d", h=H)
                    Fs = F_src[:, ds(j, 1), :].rearrange("p a h -> p (a h)")
                    own.join(dve.tensor_tensor(rs[:, 0, :], o[:, :, DO], Fs, ALU.mult))
                    own.join(dve.tensor_scalar(rs[:, 0, :], rs[:, 0, :], 1e-12, None, ALU.max))
                    own.join(dve.reciprocal(rs[:, 1, :], rs[:, 0, :]))
                    own.join(dve.tensor_tensor(rs[:, 1, :], rs[:, 1, :], Fs, ALU.mult))
                    own.join(dve.tensor_tensor(fin[:, :, :], o[:, :, 0:DO], rs[:, 1, :].unsqueeze(2).to_broadcast([P, H, DO]), ALU.mult))
                    own.join(dve.tensor_tensor(fin[:, :, :], fin[:, :, :], bias[:, :].unsqueeze(1).to_broadcast([P, H, DO]), ALU.add))
                    dve.tensor_scalar(neg[:, :, :], fin[:, :, :], 0.0, None, ALU.min).then_inc(min_done, 1)
                    dve.wait_ge(exp_done, j + 1)
                    own.join(dve.scalar_tensor_tensor(fin[:, :, :], fin[:, :, :], 0.0, neg[:, :, :], ALU.max, ALU.add))
                    xt = m.x[:, ds(j, 1), :].rearrange("p a d -> p (a d)")
                    dve.scalar_tensor_tensor(xt, fin[:, :, :].rearrange("p h d -> p (h d)"), -1.0, xt, ALU.add,
                                             ALU.add).then_inc(fin_done, 1)

                def one_block(c, before):
                    gains(c, 0)
                    for s in range(NT):
                        if s + 1 < NT:
                            gains(c, s + 1)
                        dve.wait_ge(gained, c * (NT * H) + (s + 1) * H)
                        dve.wait_ge(o_mm, c * (NT * H) + (s * H + 1))
                        score(dve, c, s, 0, HD, scored_d)
                        if before and s % 4 == 3 and s // 4 < TB:
                            finish(c - 1, s // 4)

                one_block(0, False)
                with dve.Fori(1, NB) as c:
                    one_block(c, True)
                for q in range(TB):
                    finish(NB - 1, q)

            @block.gpsimd
            def _(pool):
                pool.sem_inc(scored_p, QN + 1)
                with pool.Fori(0, NB) as c:
                    for s in range(NT):
                        pool.wait_ge(gained, c * (NT * H) + (s * H + (H - HD)))
                        pool.wait_ge(o_mm, c * (NT * H) + (s * H + 1))
                        score(pool, c, s, HD, H, scored_p)

            @block.scalar
            def _(act):
                act.sem_inc(o_out, 1)

                def exps(c):
                    for q in range(TB):
                        act.wait_ge(min_done, c * TB + (q + 1))
                        act.activation(neg[:, :, :], neg[:, :, :], ACT.Exp).then_inc(exp_done, 1)

                def copy(c):
                    act.wait_ge(o_mm, c * (NT * H) + (NT * H + H + 1))
                    act.activation(oT[:, :, :], ps[0:DA, 0:H, :], ACT.Copy).then_inc(o_out, 1)

                copy(0)
                with act.Fori(1, NB) as c:
                    exps(c - 1)
                    copy(c)
                exps(NB - 1)

            @block.tensor
            def _(pe):
                pe.sem_inc(o_mm, H + 1)

                def turn(c, q):
                    pe.wait_ge(fin_done, c * TB + max(0, q - 1) + (1 if q else 0))
                    for h in range(H):
                        mm = pe.transpose(ps[:, 4 + q % 2, h * DA:(h + 1) * DA], oT[:, h, q * P:(q + 1) * P],
                                          m.ident[0:DA, 0:DA])
                    mm.then_inc(o_turn, 1)

                def one_block(c, before):
                    pe.wait_ge(o_out, c + 1)
                    for s in range(NT):
                        pe.wait_ge(scored_d, c * NT + (s + 2 + QN))
                        pe.wait_ge(scored_p, c * NT + (s + 2 + QN))
                        for h in range(H):
                            pe.matmul(ps[0:DA, h, :], xF[:, s, h, :], S[:, s % 2, h, :],
                                      start=(s == 0), stop=(s == NT - 1)).then_inc(o_mm, 1)
                        if before and s % 4 == 1 and s // 4 < TB:
                            turn(c - 1, s // 4)

                one_block(0, False)
                with pe.Fori(1, NB) as c:
                    one_block(c, True)
                pe.wait_ge(o_out, NB + 1)
                for q in range(TB):
                    turn(NB - 1, q)


def phase_store(nc, m, out):
    stored = nc.alloc_semaphore("stored")
    full = N // P
    with nc.Block() as block:
        @block.sync
        def _(sp):
            sp.dma_start(out[0:full * P, :].rearrange("(t p) d -> p t d", p=P), m.x[:, 0:full, :]).then_inc(stored, 16)
            sp.dma_start(out[full * P:N, :], m.x[0:N - full * P, full, :]).then_inc(stored, 16)
            sp.wait_ge(stored, 32)


def program(nc, i, out, upto=99):
    m = Mem()
    m.A = nc.dram_tensor("counts", (NT, P, NP), F32, kind="Internal").ap()
    m.AT_high, m.AT_low = (nc.dram_tensor(f"counts_t_{n}", (NT, P, NP), F16, kind="Internal").ap() for n in ("high", "low"))
    with ExitStack() as ctx:
        def sb(name, shape, dt=F32):
            return ctx.enter_context(nc.sbuf_tensor(name, shape, dt))

        m.x = sb("x_tok", [P, NT, D])
        m.xn = sb("xn_tok", [P, NT, D])
        m.xT = sb("x_feat", [P, DK, NP])
        m.o = sb("o_tok", [P, NT, D])
        m.ident, m.ones = sb("ident", [P, P]), sb("ones", [P, P])
        m.zeros16, m.half16 = sb("zeros16", [P, P], F16), sb("half16", [P, P], F16)
        m.src_no = m.o[:, :, :].rearrange("p t d -> p (t d)")[:, 0:NP // 2].bitcast(F16)
        m.expert_no = sb("expert_no", [P, NT, 8])
        m.part_no = sb("part_no", [P, 1])
        m.ranges = sb("ranges", [1, 2, NT], I32)
        m.has_low = sb("has_low", [1, 1], I32)
        m.deg, m.inv_count, m.dinv_loop, m.dinv = (sb(n, [P, NT]) for n in ("deg", "inv_count", "dinv_loop", "dinv"))
        m.dinv_row = sb("dinv_row", [P, NP])
        m.src_col, m.dst_col = m.dinv_row[:, 0:GC * NG], m.dinv_row[:, GC * NG:2 * GC * NG]
        m.wd = sb("route_w", [P, NT, 8])
        m.pair_w = sb("pair_w", [P, 2])
        m.w1_rows, m.w2_rows = sb("w1_rows", [P, 2, DK], I32), sb("w2_rows", [P, 2, FH // P], I32)
        m.wl, m.wr, m.wg = (sb(n, [P, DK, D]) for n in ("wl_t", "wr_t", "wg_t"))

        def expert_mats(*ws):
            return [lambda e, w=w: w[ds(e, 1), :, :].rearrange("a (k p) n -> p (a k) n", p=P) for w in ws]

        def expert_bias(*bs):
            return [lambda e, b=b: b[ds(e, 1), :].rearrange("a (k p) -> p (a k)", p=P) for b in bs]

        mats1 = expert_mats(i["L1_ffn_expert_w1"], i["L1_ffn_expert_w2"], i["L1_ffn_expert_w3"])
        mats2 = expert_mats(i["L2_ffn_W1"], i["L2_ffn_W2"])
        mats3 = expert_mats(i["L3_ffn_W1"], i["L3_ffn_W2"], i["L3_ffn_Wo"])
        phases = [
            lambda: phase_setup(nc, m, i["x"], i["src"], i["dst"]),
            lambda: phase_counts(nc, m),
            lambda: phase_degrees(nc, m),
            lambda: phase_transpose_weights(nc, m, [(i["L0_gnn_W_l"], m.wl), (i["L0_gnn_W_r"], m.wr), (i["L1_gnn_W"], m.wg)]),
            lambda: phase_norm(nc, m, "n0", m.x, m.xn, m.xT),
            lambda: phase_gather(nc, m, "g0", m.xn, "mean", m.wl, m.wr, i["L0_gnn_b_r"]),
            lambda: phase_norm(nc, m, "n1", m.x, m.xn, m.xT),
            lambda: phase_route(nc, m, "r0", "mean", 8, i["L0_ffn_Wr"], i["L0_ffn_br"], i["L0_ffn_b2"], m.o, m.xn),
            lambda: phase_experts(nc, m, "e0", 2, ACT.Gelu, [FH],
                                  [i["L0_ffn_W1"].rearrange("e d f -> (e d) f"), i["L0_ffn_W2"].rearrange("e f d -> (e f) d")],
                                  [i["L0_ffn_b1"].rearrange("e (f a) -> (e f) a", a=1)], m.o, picked=True),
            lambda: phase_norm(nc, m, "n2", m.o, m.o, gamma=i["L0_ffn_gamma"], beta=i["L0_ffn_beta"], finish="add"),
            lambda: phase_norm(nc, m, "n3", m.x, m.xn, m.xT, scale=m.dinv_loop),
            lambda: phase_gather(nc, m, "g1", m.xn, "loop", m.wg, bias=i["L1_gnn_b"]),
            lambda: phase_norm(nc, m, "n4", m.o, m.o, gamma=i["L1_gnn_gamma"], beta=i["L1_gnn_beta"], finish="relu_add"),
            lambda: phase_norm(nc, m, "n5", m.x, m.xn, m.xT),
            lambda: phase_route(nc, m, "r1", "mlp", 6, i["L1_ffn_router_w2"], i["L1_ffn_router_b2"], i["L1_ffn_expert_b3"],
                                m.x, m.x, i["L1_ffn_router_w1"], i["L1_ffn_router_b1"], ahead=([256, 256], mats1)),
            lambda: phase_experts(nc, m, "e1", 6, ACT.Relu, [256, 256],
                                  mats1, expert_bias(i["L1_ffn_expert_b1"], i["L1_ffn_expert_b2"]), m.x, weight=m.wd,
                                  loaded=True),
            lambda: phase_norm(nc, m, "n6", m.x, m.xn, m.xT, scale=m.dinv),
            lambda: phase_gather(nc, m, "g2", m.xn, "keep"),
            lambda: phase_experts(nc, m, "e2", 2, ACT.Gelu, [FH],
                                  [lambda e: rows(i["L2_gnn_W1"][:, e * FH:(e + 1) * FH]),
                                   lambda e: rows(i["L2_gnn_W2"][e * FH:(e + 1) * FH, :])],
                                  [lambda e: per_partition(i["L2_gnn_b1"][e * FH:(e + 1) * FH])], m.x),
            lambda: phase_add_row(nc, m, "b2", i["L2_gnn_b2"]),
            lambda: phase_norm(nc, m, "n7", m.x, m.xn),
            lambda: phase_norm(nc, m, "n8", m.xn, m.o, m.xT, gamma=i["L2_ffn_gamma"], beta=i["L2_ffn_beta"]),
            lambda: phase_route(nc, m, "r2", "top", 8, i["L2_ffn_Wr"], i["L2_ffn_br"], i["L2_ffn_b2"], m.x, m.x,
                                ahead=([FH], mats2)),
            lambda: phase_experts(nc, m, "e3", 8, ACT.Gelu, [FH], mats2, expert_bias(i["L2_ffn_b1"]), m.x, weight=m.wd,
                                  loaded=True),
            lambda: phase_norm(nc, m, "n9", m.x, m.xn, m.xT),
            lambda: phase_attention(nc, m, i["L3_gnn_W"], i["L3_gnn_Wl"], i["L3_gnn_Wr"], i["L3_gnn_b"]),
            lambda: phase_norm(nc, m, "n10", m.x, m.xn, m.xT),
            lambda: phase_route(nc, m, "r3", "dense", 8, i["L3_ffn_Wr"], i["L3_ffn_br"], i["L3_ffn_bo"], m.x, m.x,
                                ahead=([256, 256], mats3)),
            lambda: phase_experts(nc, m, "e4", 8, ACT.Relu, [256, 256],
                                  mats3,
                                  [i["L3_ffn_b1"], i["L3_ffn_b2"]], m.x, weight=m.wd, loaded=True,
                                  bn=[tuple(i[f"L3_ffn_{v}{n}"] for v in ("g", "be", "m", "v")) for n in (1, 2)]),
        ]
        for phase in phases[:upto]:
            with nc.cleanup_on_exit():
                phase()
        phase_store(nc, m, out)


def kernel(**inputs):
    import numpy as _np
    import concourse.bacc as _bacc
    from concourse import mybir as _mybir
    from concourse.bass_utils import run_bass_kernel_spmd as _run

    nc = _bacc.Bacc("TRN2", target_bir_lowering=False, num_devices=1)
    arrays, views = {}, {}
    for name, value in inputs.items():
        a = _np.ascontiguousarray(value)
        arrays[f"in_{name}"] = a
        views[name] = nc.dram_tensor(f"in_{name}", a.shape, _mybir.dt.from_np(a.dtype), kind="ExternalInput").ap()
    out = nc.dram_tensor("out_x", (N, D), F32, kind="ExternalOutput").ap()
    program(nc, views, out)
    r = _run(nc, [arrays], core_ids=[0])
    return r.results[0]["out_x"]
```
